# Optimizing a Trainium2 kernel written in Bass

```python
import numpy as np
import jax
import jax.numpy as jnp

def _softmax(x, axis=-1):
    return jax.nn.softmax(x, axis=axis)

def _gelu(x):
    return jax.nn.gelu(x, approximate=True)

def _silu(x):
    return jax.nn.silu(x)

def _sigmoid(x):
    return jax.nn.sigmoid(x)

def _layernorm(x, axis=-1, eps=1e-05):
    m = jnp.mean(x, axis=axis, keepdims=True)
    v = jnp.var(x, axis=axis, keepdims=True)
    return (x - m) / jnp.sqrt(v + eps)

def _scatter_add(tgt, idx, src, axis=0):
    return tgt.at[idx].add(src)

def _segment_sum(src, seg, n):
    return jax.ops.segment_sum(src, seg, n)
kernel_name = 'mk_cond_resid_d4_seqx_r8_717b29'

def setup_inputs(seed: int=0):
    np.random.seed(seed)
    _w = jnp.asarray

    def _rec_inputs():
        import jax
        import jax.numpy as jnp
        _rk = jax.random.key(seed)
        x = -7.109e-05 + 0.9999 * jax.random.normal(jax.random.fold_in(_rk, 1), (32, 32, 512), jnp.float32)
        _lenS = 32 - jax.random.randint(jax.random.fold_in(_rk, 7), (32,), 0, max(1, 32 // 4) + 1, jnp.int32)
        _lenS2 = 32 - jax.random.randint(jax.random.fold_in(_rk, 8), (32,), 0, max(1, 32 // 4) + 1, jnp.int32)
        itok_B_0_15 = jax.random.randint(jax.random.fold_in(_rk, 11), (32,), 0, 16, jnp.int32)
        itok_B_0_2 = jax.random.randint(jax.random.fold_in(_rk, 12), (32,), 0, 3, jnp.int32)
        itok_B_3_7 = jax.random.randint(jax.random.fold_in(_rk, 13), (32,), 3, 8, jnp.int32)
        itok_Bx16_0_63 = jax.random.randint(jax.random.fold_in(_rk, 14), (32, 16), 0, 64, jnp.int32)
        itok_B_207_1644 = jax.random.randint(jax.random.fold_in(_rk, 15), (32,), 207, 1645, jnp.int32)
        return (x, itok_B_0_15, itok_B_0_2, itok_B_3_7, itok_Bx16_0_63, itok_B_207_1644)
    x, itok_B_0_15, itok_B_0_2, itok_B_3_7, itok_Bx16_0_63, itok_B_207_1644 = _rec_inputs()

    def _L0_cond_setup():
        import jax, jax.numpy as jnp
        import numpy as np
        B, C, T = (64, 32, 512)
        S, D = (16, 32)
        key = jax.random.key(seed)
        k1, k2, k3 = jax.random.split(key, 3)
        x = jax.random.normal(k1, (B, C, T), dtype=jnp.float32)
        condition = jax.random.randint(k2, (B,), 0, S, dtype=jnp.int64)
        bound = float(np.sqrt(6.0 / C))
        weights = jax.random.uniform(k3, (S, C, D), dtype=jnp.float32, minval=-bound, maxval=bound)
        return {'x': x, 'condition': condition, 'weights': weights}
    _L0_cond_all = _L0_cond_setup()
    _L0_cond_in = {k: v for k, v in _L0_cond_all.items() if k in ('weights',)}
    del _L0_cond_all

    def _L1_cond_setup():
        import jax, jax.numpy as jnp
        import numpy as np
        B, S, D_IN, D_OUT = (4, 256, 512, 512)
        R, NUM_LABELERS = (32, 5)
        LORA_SCALING = 16 / 32
        key = jax.random.key(seed)
        k1, k2, k3, k4, k5 = jax.random.split(key, 5)
        x = jax.random.normal(k1, (B, S, D_IN), dtype=jnp.float32)
        labeler_index = jax.random.randint(k2, (B,), 0, NUM_LABELERS, dtype=jnp.int64)
        W = jax.random.normal(k3, (D_OUT, D_IN), dtype=jnp.float32) * 0.02
        lora_A = jax.random.normal(k4, (NUM_LABELERS, D_IN, R), dtype=jnp.float32) * 0.02
        lora_B_w = jax.random.normal(k5, (D_OUT, R), dtype=jnp.float32) * 0.02
        return {'x': x, 'labeler_index': labeler_index, 'W': W, 'lora_A': lora_A, 'lora_B_w': lora_B_w}
    _L1_cond_all = _L1_cond_setup()
    _L1_cond_in = {k: v for k, v in _L1_cond_all.items() if k in ('W', 'lora_A', 'lora_B_w')}
    del _L1_cond_all

    def _L2_cond_setup():
        import jax, jax.numpy as jnp
        import numpy as np
        MAX_LORAS, OUT, IN = (8, 512, 512)
        B, S = (4, 256)
        key = jax.random.key(seed)
        k1, k2, k3 = jax.random.split(key, 3)
        x = jax.random.normal(k1, (B, S, IN), dtype=jnp.float32)
        weight = jax.random.normal(k2, (MAX_LORAS, OUT, IN), dtype=jnp.float32) * 0.02
        adapter_ids = jax.random.randint(k3, (B,), 0, MAX_LORAS, dtype=jnp.int32)
        return {'x': x, 'weight': weight, 'adapter_ids': adapter_ids}
    _L2_cond_all = _L2_cond_setup()
    _L2_cond_in = {k: v for k, v in _L2_cond_all.items() if k in ('weight',)}
    del _L2_cond_all

    def _L3_cond_setup():
        import jax, jax.numpy as jnp
        import numpy as np
        B, S, HID = (4, 128, 512)
        D, HQ, HK = (128, 32, 8)
        PAGES, PSIZE, NPP = (64, 32, 16)
        THETA = 10000.0
        EPS = 1e-06
        SCALE = 1.0 / float(np.sqrt(D))

        def _rmsnorm(t, w):
            var = jnp.mean(t * t, axis=-1, keepdims=True)
            return t * jax.lax.rsqrt(var + EPS) * w

        def _rope(t, pos):
            inv_freq = 1.0 / THETA ** (jnp.arange(0, D, 2, dtype=jnp.float32) / D)
            freqs = pos[..., None].astype(jnp.float32) * inv_freq
            cos = jnp.cos(freqs)[:, :, None, :]
            sin = jnp.sin(freqs)[:, :, None, :]
            t1, t2 = (t[..., :D // 2], t[..., D // 2:])
            return jnp.concatenate([t1 * cos - t2 * sin, t2 * cos + t1 * sin], axis=-1)
        key = jax.random.key(seed)
        ks = jax.random.split(key, 10)
        x = jax.random.normal(ks[0], (B, S, HID), jnp.float32)
        Wq = jax.random.normal(ks[1], (HQ * D, HID), jnp.float32) * 0.02
        Wk = jax.random.normal(ks[2], (HK * D, HID), jnp.float32) * 0.02
        Wv = jax.random.normal(ks[3], (HK * D, HID), jnp.float32) * 0.02
        Wo = jax.random.normal(ks[4], (HID, HQ * D), jnp.float32) * 0.02
        q_norm_w = jax.random.uniform(ks[5], (D,), jnp.float32)
        k_norm_w = jax.random.uniform(ks[6], (D,), jnp.float32)
        k_cache = jax.random.normal(ks[7], (PAGES, PSIZE, HK, D), jnp.float32)
        v_cache = jax.random.normal(ks[8], (PAGES, PSIZE, HK, D), jnp.float32)
        block_table = jnp.arange(B * NPP, dtype=jnp.int32).reshape(B, NPP)
        cache_seqlens = jax.random.randint(ks[9], (B,), 0, 475).astype(jnp.int32)
        return dict(x=x, Wq=Wq, Wk=Wk, Wv=Wv, Wo=Wo, q_norm_w=q_norm_w, k_norm_w=k_norm_w, k_cache=k_cache, v_cache=v_cache, block_table=block_table, cache_seqlens=cache_seqlens)
    _L3_cond_all = _L3_cond_setup()
    _L3_cond_in = {k: v for k, v in _L3_cond_all.items() if k in ('Wq', 'Wk', 'Wv', 'Wo', 'q_norm_w', 'k_norm_w', 'k_cache', 'v_cache')}
    del _L3_cond_all
    return {'x': x, 'itok_B_0_15': itok_B_0_15, 'itok_B_0_2': itok_B_0_2, 'itok_B_3_7': itok_B_3_7, 'itok_Bx16_0_63': itok_Bx16_0_63, 'itok_B_207_1644': itok_B_207_1644, 'L0_cond_weights': _L0_cond_in['weights'], 'L1_cond_W': _L1_cond_in['W'], 'L1_cond_lora_A': _L1_cond_in['lora_A'], 'L1_cond_lora_B_w': _L1_cond_in['lora_B_w'], 'L2_cond_weight': _L2_cond_in['weight'], 'L3_cond_Wq': _L3_cond_in['Wq'], 'L3_cond_Wk': _L3_cond_in['Wk'], 'L3_cond_Wv': _L3_cond_in['Wv'], 'L3_cond_Wo': _L3_cond_in['Wo'], 'L3_cond_q_norm_w': _L3_cond_in['q_norm_w'], 'L3_cond_k_norm_w': _L3_cond_in['k_norm_w'], 'L3_cond_k_cache': _L3_cond_in['k_cache'], 'L3_cond_v_cache': _L3_cond_in['v_cache']}

def reference(x, itok_B_0_15, itok_B_0_2, itok_B_3_7, itok_Bx16_0_63, itok_B_207_1644, L0_cond_weights, L1_cond_W, L1_cond_lora_A, L1_cond_lora_B_w, L2_cond_weight, L3_cond_Wq, L3_cond_Wk, L3_cond_Wv, L3_cond_Wo, L3_cond_q_norm_w, L3_cond_k_norm_w, L3_cond_k_cache, L3_cond_v_cache):
    import jax
    import jax.numpy as jnp

    def _L0_cond_ref(x, condition, weights):
        import jax, jax.numpy as jnp
        import numpy as np
        B, C, T = (64, 32, 512)
        S, D = (16, 32)
        W = weights[condition]
        return jnp.einsum('bct,bcd->bdt', x, W)

    def _L1_cond_ref(x, labeler_index, W, lora_A, lora_B_w):
        import jax, jax.numpy as jnp
        import numpy as np
        B, S, D_IN, D_OUT = (4, 256, 512, 512)
        R, NUM_LABELERS = (32, 5)
        LORA_SCALING = 16 / 32
        base = jnp.einsum('bsi,oi->bso', x, W)
        labelers_A = lora_A[labeler_index]
        low = jnp.einsum('bsi,bir->bsr', x, labelers_A)
        delta = jnp.einsum('bsr,or->bso', low, lora_B_w) * LORA_SCALING
        return base + delta

    def _L2_cond_ref(x, weight, adapter_ids):
        import jax, jax.numpy as jnp
        import numpy as np
        MAX_LORAS, OUT, IN = (8, 512, 512)
        B, S = (4, 256)
        w = weight[adapter_ids]
        return jnp.einsum('bsi,boi->bso', x, w)

    def _L3_cond_ref(x, Wq, Wk, Wv, Wo, q_norm_w, k_norm_w, k_cache, v_cache, block_table, cache_seqlens):
        import jax, jax.numpy as jnp
        import numpy as np
        B, S, HID = (4, 128, 512)
        D, HQ, HK = (128, 32, 8)
        PAGES, PSIZE, NPP = (64, 32, 16)
        THETA = 10000.0
        EPS = 1e-06
        SCALE = 1.0 / float(np.sqrt(D))

        def _rmsnorm(t, w):
            var = jnp.mean(t * t, axis=-1, keepdims=True)
            return t * jax.lax.rsqrt(var + EPS) * w

        def _rope(t, pos):
            inv_freq = 1.0 / THETA ** (jnp.arange(0, D, 2, dtype=jnp.float32) / D)
            freqs = pos[..., None].astype(jnp.float32) * inv_freq
            cos = jnp.cos(freqs)[:, :, None, :]
            sin = jnp.sin(freqs)[:, :, None, :]
            t1, t2 = (t[..., :D // 2], t[..., D // 2:])
            return jnp.concatenate([t1 * cos - t2 * sin, t2 * cos + t1 * sin], axis=-1)
        bsz, seqlen, _ = x.shape
        q = jnp.einsum('bsd,ed->bse', x, Wq).reshape(bsz, seqlen, HQ, D)
        k = jnp.einsum('bsd,ed->bse', x, Wk).reshape(bsz, seqlen, HK, D)
        v = jnp.einsum('bsd,ed->bse', x, Wv).reshape(bsz, seqlen, HK, D)
        q = _rmsnorm(q, q_norm_w)
        k = _rmsnorm(k, k_norm_w)
        pos = cache_seqlens[:, None] + jnp.arange(seqlen)[None, :]
        q = _rope(q, pos)
        k = _rope(k, pos)
        L = NPP * PSIZE
        kc = k_cache[block_table].reshape(bsz, L, HK, D)
        vc = v_cache[block_table].reshape(bsz, L, HK, D)
        k_all = jnp.concatenate([kc, k], axis=1)
        v_all = jnp.concatenate([vc, v], axis=1)
        valid_c = jnp.arange(L)[None, :] < cache_seqlens[:, None]
        valid = jnp.concatenate([valid_c, jnp.ones((bsz, seqlen), dtype=bool)], axis=1)
        rep = HQ // HK
        k_all = jnp.repeat(k_all, rep, axis=2)
        v_all = jnp.repeat(v_all, rep, axis=2)
        scores = jnp.einsum('bqhd,bkhd->bhqk', q, k_all) * SCALE
        scores = jnp.where(valid[:, None, None, :], scores, -1e+30)
        probs = jax.nn.softmax(scores, axis=-1)
        o = jnp.einsum('bhqk,bkhd->bqhd', probs, v_all)
        o = o.reshape(bsz, seqlen, HQ * D)
        return jnp.einsum('bse,de->bsd', o, Wo)
    x = x + _L0_cond_ref(x, itok_B_0_15, L0_cond_weights)
    x = x + _L1_cond_ref(x, itok_B_0_2, L1_cond_W, L1_cond_lora_A, L1_cond_lora_B_w)
    x = x + _L2_cond_ref(x, L2_cond_weight, itok_B_3_7)
    x = x + _L3_cond_ref(x, L3_cond_Wq, L3_cond_Wk, L3_cond_Wv, L3_cond_Wo, L3_cond_q_norm_w, L3_cond_k_norm_w, L3_cond_k_cache, L3_cond_v_cache, itok_Bx16_0_63, itok_B_207_1644)
    return x

_drawn_inputs = setup_inputs


def setup_inputs(seed=0):
    import zlib

    import numpy as np

    out = dict(_drawn_inputs(seed))
    spreads = {}
    factors = {'L3_cond_Wq': 2.915,
     'L3_cond_Wk': 8.0,
     'L3_cond_Wv': 8.0,
     'L3_cond_q_norm_w': 5.061,
     'L3_cond_k_norm_w': 8.0,
     'L3_cond_k_cache': 2.939}
    for name, (base, spread) in spreads.items():
        noise = np.random.default_rng([zlib.crc32(name.encode()), seed]).standard_normal(out[name].shape)
        drawn = base * np.exp(spread * noise) if base else spread * noise
        out[name] = jnp.asarray(drawn.astype(out[name].dtype))
    for name, factor in factors.items():
        out[name] = (out[name] * factor).astype(out[name].dtype)
    return out
```

```python
from contextlib import ExitStack

import concourse.bass as bass
import numpy as np
from concourse import mybir

F32 = mybir.dt.float32
F32R = mybir.dt.float32r
I32 = mybir.dt.int32
ALU = mybir.AluOpType
ACT = mybir.ActivationFunctionType
AX_X = mybir.AxisListType.X

P = 128
BANK = 512
B, S, H = 32, 32, 512
TOK = B * S
TT = TOK // P
BT = P // S
KC = H // P
NS0 = 16
NL, R = 5, 32
LR = NL * R
NE = 8
D, HQ, HK = 128, 32, 8
REP = HQ // HK
QW = REP * D
WE = QW + 2 * D
QK = QW + D
PAGES, PS, NPP = 64, 32, 16
L = NPP * PS
KEYS = L + S
NCH = L // P
PPT = P // PS
QS = REP * S
ST = QS + S
THETA, EPS = 10000.0, 1e-6
SCALE = float(1.0 / np.sqrt(D))
HALF = D // 2
MASKED = 1e30
MAGIC = 1.5 * 2.0**23
TWO_PI_HI = 6.28125
TWO_PI_LO = float(2.0 * np.pi - TWO_PI_HI)
PI_IN = float(np.nextafter(np.float32(np.pi), np.float32(0.0)))


def f32(ap):
    return ap.bitcast(F32)


class Bench:

    def __init__(self, nc, ctx, prefix):
        self.nc, self.ctx, self.prefix = nc, ctx, prefix

    def sb(self, name, shape, dt=F32):
        return self.ctx.enter_context(self.nc.sbuf_tensor(f"{self.prefix}_{name}", shape, dt))

    def psum(self, name, shape):
        return self.ctx.enter_context(self.nc.psum_tensor(f"{self.prefix}_{name}", shape, F32))

    def sem(self, name):
        return self.ctx.enter_context(self.nc.semaphore(f"{self.prefix}_{name}"))


def three_pass(pe, out, w_hi, w_lo, x_hi, x_lo, first, last):
    pe.matmul(out, w_lo, x_hi, start=first, stop=False)
    pe.matmul(out, w_hi, x_lo, start=False, stop=False)
    return pe.matmul(out, w_hi, x_hi, start=False, stop=last)


def stage_rope(nc, inp, tabs):
    with ExitStack() as ctx:
        m = Bench(nc, ctx, "rope")
        inv = m.sb("inv", [P, HALF])
        w = m.sb("w", [P, 2, D])
        wn = m.sb("wn", [P, 2, D])
        pos_i = m.sb("pos_i", [P, 1], I32)
        len_i = m.sb("len_i", [P, B], I32)
        pos = m.sb("pos", [P, TT])
        base = m.sb("base", [P, 1])
        row_i = m.sb("row_i", [P, 1], I32)
        fr = m.sb("fr", [P, TT, HALF])
        turns = m.sb("turns", [P, TT, HALF])
        red = m.sb("red", [P, TT, HALF])
        sin = m.sb("sin", [P, TT, HALF])
        cos = m.sb("cos", [P, TT, HALF])
        landed = m.sem("landed")
        iota_done = m.sem("iota_done")
        step = m.sem("step")
        angle = m.sem("angle")
        trig = m.sem("trig")
        cq, sq, ck, sk = tabs
        with nc.Block() as block:

            @block.sync
            def _(sp):
                sp.dma_start(inv[:], inp["rope_inv_freq"].partition_broadcast(P)).then_inc(landed, 16)
                sp.dma_start(w[:, 0, :], inp["L3_cond_q_norm_w"].partition_broadcast(P)).then_inc(landed, 16)
                sp.dma_start(w[:, 1, :], inp["L3_cond_k_norm_w"].partition_broadcast(P)).then_inc(landed, 16)
                sp.dma_start(len_i[:], inp["itok_B_207_1644"].partition_broadcast(P)).then_inc(landed, 16)

            @block.gpsimd
            def _(pool):
                nc.gpsimd.iota(pos_i[:], pattern=[[0, 1]], base=0, channel_multiplier=1).then_inc(iota_done, 1)

            @block.vector
            def _(dve):
                v = nc.vector
                n = [0]

                def link(ins):
                    ins.then_inc(step, 1)
                    n[0] += 1
                    dve.wait_ge(step, n[0])

                dve.wait_ge(iota_done, 1)
                link(v.tensor_scalar(row_i[:], pos_i[:], S - 1, None, ALU.bitwise_and))
                link(v.tensor_copy(base[:], row_i[:]))
                dve.wait_ge(landed, 16 * 4)
                for b in range(BT):
                    r = slice(b * S, (b + 1) * S)
                    link(v.tensor_copy(pos[r, :], len_i[r, :].rearrange("p (t b) -> p t b", b=BT)[:, :, b]))
                link(v.tensor_scalar(pos[:], pos[:], base[:, 0:1], None, ALU.add))
                for t in range(TT):
                    link(v.tensor_scalar(fr[:, t, :], inv[:], pos[:, t:t + 1], None, ALU.mult))
                link(v.tensor_scalar(w[:, 0, :], w[:, 0, :], -SCALE * float(np.sqrt(D)), None, ALU.mult))
                link(v.tensor_scalar(w[:, 1, :], w[:, 1, :], float(np.sqrt(D)), None, ALU.mult))
                link(v.tensor_scalar(wn[:], w[:], -1.0, None, ALU.mult))
                for k, (quarter, phase) in enumerate(((0.0, 0.0), (0.25, 0.5 * np.pi))):
                    if k:
                        dve.wait_ge(trig, k)
                    link(v.tensor_scalar(turns[:], fr[:], float(1.0 / (2.0 * np.pi)), quarter, ALU.mult, ALU.add))
                    link(v.tensor_scalar(turns[:], turns[:], MAGIC, None, ALU.add))
                    link(v.tensor_scalar(turns[:], turns[:], MAGIC, None, ALU.subtract))
                    link(v.scalar_tensor_tensor(red[:], turns[:], -TWO_PI_HI, fr[:], ALU.mult, ALU.add))
                    link(v.scalar_tensor_tensor(red[:], turns[:], -TWO_PI_LO, red[:], ALU.mult, ALU.add))
                    link(v.tensor_scalar(red[:], red[:], float(phase), PI_IN, ALU.add, ALU.min))
                    v.tensor_scalar(red[:], red[:], -PI_IN, None, ALU.max).then_inc(angle, 1)
                dve.wait_ge(trig, 2)
                for c, s, i in ((cq, sq, 0), (ck, sk, 1)):
                    for t in range(TT):
                        lo, hi = slice(0, HALF), slice(HALF, D)
                        v.tensor_tensor(c[:, t, lo], cos[:, t, :], w[:, i, lo], ALU.mult)
                        v.tensor_tensor(c[:, t, hi], cos[:, t, :], w[:, i, hi], ALU.mult)
                        v.tensor_tensor(s[:, t, lo], sin[:, t, :], wn[:, i, hi], ALU.mult)
                        v.tensor_tensor(s[:, t, hi], sin[:, t, :], w[:, i, lo], ALU.mult)

            @block.scalar
            def _(act):
                act.wait_ge(angle, 1)
                nc.scalar.activation(sin[:], red[:], ACT.Sin).then_inc(trig, 1)
                act.wait_ge(angle, 2)
                nc.scalar.activation(cos[:], red[:], ACT.Sin).then_inc(trig, 1)


def stage_layers(nc, inp, ident, xT_hi, xT_lo, x3_d):
    with ExitStack() as ctx:
        m = Bench(nc, ctx, "lay")
        x = m.sb("x", [P, TT, H])
        w0 = m.sb("w0", [P, TT, P])
        idx = m.sb("idx", [1, 2, B], I32)
        w1n = m.sb("w1n", [P, KC, H])
        w1_hi = m.sb("w1_hi", [P, KC, H], F32R)
        w1_lo = m.sb("w1_lo", [P, KC, H], F32R)
        a_n = m.sb("a_n", [P, KC, LR])
        a_hi = m.sb("a_hi", [P, KC, LR], F32R)
        a_lo = m.sb("a_lo", [P, KC, LR], F32R)
        bw_n = m.sb("bw_n", [P, KC, R])
        bw_r = m.sb("bw_r", [P, KC, LR])
        bw_t = m.sb("bw_t", [P, 2, H])
        lab_i = m.sb("lab_i", [P, B], I32)
        lab = m.sb("lab", [P, TT])
        lab_of = m.sb("lab_of", [P, LR])
        low = m.sb("low", [P, TT, LR])
        low_t = m.sb("low_t", [P, TT, 2 * P])
        w2n = m.sb("w2n", [P, 2, KC, H])
        w2t = m.sb("w2t", [P, NE, KC, H])
        XM = BT * (P + S)
        x2m = m.sb("x2m", [P, 2, KC, XM])
        ps = [m.psum(f"ps{i}", [P, BANK]) for i in range(8)]
        written = m.sem("written")
        x_in = m.sem("x_in")
        w0_zero = m.sem("w0_zero")
        ident_made = m.sem("ident_made")
        idx_in = m.sem("idx_in")
        w0_in = m.sem("w0_in")
        w1_in = m.sem("w1_in")
        small_in = m.sem("small_in")
        w2_in = [m.sem("w2_in0"), m.sem("w2_in1")]
        x_new = m.sem("x_new")
        split_hi = m.sem("split_hi")
        split_lo = m.sem("split_lo")
        a_split = m.sem("a_split")
        bw_rep = m.sem("bw_rep")
        bw_ready = m.sem("bw_ready")
        lab_ready = m.sem("lab_ready")
        low_ready = m.sem("low_ready")
        lowt_ready = m.sem("lowt_ready")
        w2_act = m.sem("w2_act")
        w2_dve = m.sem("w2_dve")
        x2m_zero = m.sem("x2m_zero")
        x2m_ready = m.sem("x2m_ready")
        x3_out = m.sem("x3_out")

        uses = [("L0", t) for t in range(TT)] + [("W1T", k) for k in range(KC)] + [("BwT", 0), ("BwT", 1)]
        uses += [("x1T", t) for t in range(TT)] + [("low", t) for t in range(TT)]
        ex = [("W2T", e * KC + k) for e in range(NE) for k in range(KC)]
        uses += ex[:8] + [("lowT", t) for t in range(TT)] + ex[8:16]
        uses += [("L1", t) for t in range(TT)] + ex[16:]
        for t in range(TT):
            uses += [("x2T", t)]
            if t:
                uses += [("L2", t - 1)]
        uses += [("L2", TT - 1)] + [("x3T", t) for t in range(TT)]
        pos_of = {u: i for i, u in enumerate(uses)}
        splits = [u for u in uses if u[0] in ("W1T", "x1T", "x3T")]
        split_no = {u: i + 1 for i, u in enumerate(splits)}

        def drained(u):
            kind, i = u
            if kind in ("L0", "L1", "L2"):
                return x_new, TT * int(kind[1]) + i + 1
            if u in split_no:
                return split_lo, split_no[u]
            if kind == "W2T":
                return (w2_dve if i % 2 else w2_act), i // 2 + 1
            return {"BwT": bw_ready, "low": low_ready, "lowT": lowt_ready, "x2T": x2m_ready}[kind], i + 1

        with nc.Block() as block:

            @block.sync
            def _(sp):
                sp.dma_start(idx[:, 0, :], inp["itok_B_0_15"].rearrange("(a b) -> a b", a=1)).then_inc(idx_in, 16)
                sp.dma_start(idx[:, 1, :], inp["itok_B_3_7"].rearrange("(a b) -> a b", a=1)).then_inc(idx_in, 16)
                sp.dma_start(x[:], inp["x"].rearrange("(t b) c h -> (b c) t h", b=BT)).then_inc(x_in, 16)
                sp.dma_start(w1n[:], inp["L1_cond_W"].rearrange("(o p) i -> p o i", p=P)).then_inc(w1_in, 16)
                for l in range(NL):
                    sp.dma_start(a_n[:, :, l * R:(l + 1) * R],
                                 inp["L1_cond_lora_A"][l].rearrange("(k p) r -> p k r", p=P)).then_inc(small_in, 16)
                sp.dma_start(bw_n[:], inp["L1_cond_lora_B_w"].rearrange("(o p) r -> p o r", p=P)).then_inc(small_in, 16)
                sp.dma_start(lab_i[:], inp["itok_B_0_2"].partition_broadcast(P)).then_inc(small_in, 16)
                for e in range(NE):
                    if e >= 2:
                        sp.wait_ge(written, pos_of[("W2T", (e - 2) * KC + KC - 1)] + 1)
                    sp.dma_start(w2n[:, e % 2], inp["L2_cond_weight"][e].rearrange("(o p) i -> p o i", p=P)).then_inc(w2_in[e % 2], 16)
                for t in range(TT):
                    sp.wait_ge(x_new, 2 * TT + t + 1)
                    sp.dma_start(x3_d[t], x[:, t, :]).then_inc(x3_out, 16)
                sp.wait_ge(x3_out, 16 * TT)

            @block.gpsimd
            def _(pool):
                nc.gpsimd.memset(w0[:], 0.0).then_inc(w0_zero, 1)
                nc.gpsimd.memset(ident[:], 0.0).then_inc(ident_made, 1)
                pool.wait_ge(ident_made, 1)
                nc.gpsimd.affine_select(out=ident[:], in_=ident[:], compare_op=ALU.not_equal, fill=1.0, base=0,
                                        pattern=[[-1, P]], channel_multiplier=1).then_inc(ident_made, 1)
                nc.gpsimd.memset(x2m[:], 0.0).then_inc(x2m_zero, 1)
                nc.gpsimd.iota(lab_of[:], pattern=[[1, NL], [0, R]], base=0, channel_multiplier=0,
                               allow_small_or_imprecise_dtypes=True).then_inc(x2m_zero, 1)

            @block.tensor
            def _(pe):
                def end(u, ins):
                    ins.then_inc(written, 1)

                pe.wait_ge(ident_made, 2)
                for n, u in enumerate(uses):
                    kind, i = u
                    bank = ps[n % 8]
                    if n >= 8:
                        pe.wait_ge(*drained(uses[n - 8]))
                    if kind == "L0":
                        if i == 0:
                            pe.wait_ge(x_in, 16)
                            pe.wait_ge(w0_in, 16 * B)
                        end(u, pe.matmul(bank[:], w0[:, i, :], x[:, i, :], start=True, stop=True))
                    elif kind == "W1T":
                        pe.wait_ge(w1_in, 16)
                        for o in range(KC):
                            t = pe.transpose(bank[:, o * P:(o + 1) * P], w1n[:, o, i * P:(i + 1) * P], ident[:])
                        end(u, t)
                    elif kind == "BwT":
                        pe.wait_ge(bw_rep, 1)
                        for o in range(KC):
                            src = bw_r[:, o, 0:P] if i == 0 else bw_r[:, o, P:LR]
                            t = pe.transpose(bank[0:src.shape[1], o * P:(o + 1) * P], src, ident[:])
                        end(u, t)
                    elif kind in ("x1T", "x2T", "x3T"):
                        pe.wait_ge(x_new, TT * (int(kind[1]) - 1) + i + 1)
                        for k in range(KC):
                            t = pe.transpose(bank[:, k * P:(k + 1) * P], x[:, i, k * P:(k + 1) * P], ident[:])
                        end(u, t)
                    elif kind == "low":
                        if i == 0:
                            pe.wait_ge(a_split, 2)
                        pe.wait_ge(split_lo, split_no[("x1T", i)])
                        tok = slice(i * P, (i + 1) * P)
                        for k in range(KC):
                            t = three_pass(pe, bank[:, 0:LR], xT_hi[:, k, tok], xT_lo[:, k, tok], a_hi[:, k, :], a_lo[:, k, :],
                                           k == 0, k == KC - 1)
                        end(u, t)
                    elif kind == "lowT":
                        pe.wait_ge(low_ready, i + 1)
                        pe.transpose(bank[:, 0:P], low[:, i, 0:P], ident[:])
                        end(u, pe.transpose(bank[0:R, P:2 * P], low[:, i, P:LR], ident[:]))
                    elif kind == "W2T":
                        e, k = divmod(i, KC)
                        pe.wait_ge(w2_in[e % 2], 16 * (e // 2 + 1))
                        for o in range(KC):
                            t = pe.transpose(bank[:, o * P:(o + 1) * P], w2n[:, e % 2, o, k * P:(k + 1) * P], ident[:])
                        end(u, t)
                    elif kind == "L1":
                        pe.wait_ge(split_lo, max(split_no[("x1T", i)], split_no[("W1T", KC - 1)]))
                        pe.wait_ge(lowt_ready, i + 1)
                        pe.wait_ge(bw_ready, 2)
                        tok = slice(i * P, (i + 1) * P)
                        for k in range(KC):
                            three_pass(pe, bank[:], xT_hi[:, k, tok], xT_lo[:, k, tok], w1_hi[:, k, :], w1_lo[:, k, :],
                                       k == 0, False)
                        pe.matmul(bank[:], low_t[:, i, 0:P], bw_t[:, 0, :], start=False, stop=False)
                        end(u, pe.matmul(bank[:], low_t[0:R, i, P:2 * P], bw_t[0:R, 1, :], start=False, stop=True))
                    elif kind == "L2":
                        if i == 0:
                            pe.wait_ge(idx_in, 32)
                            pe.wait_ge(w2_act, NE * KC // 2)
                            pe.wait_ge(w2_dve, NE * KC // 2)
                        pe.wait_ge(x2m_ready, i + 1)
                        for b in range(BT):
                            e = pe.value_load(idx[0:1, 1, i * BT + b:i * BT + b + 1], min_val=0, max_val=NE - 1)
                            for k in range(KC):
                                t = pe.matmul(bank[:], x2m[:, i % 2, k, b * P:(b + 1) * P],
                                              w2t[:, bass.ds(e, 1), k, :].rearrange("p a o -> p (a o)"),
                                              start=(b == 0 and k == 0), stop=(b == BT - 1 and k == KC - 1))
                        end(u, t)

            @block.scalar
            def _(act):
                act.wait_ge(idx_in, 32)
                act.wait_ge(w0_zero, 1)
                for b in range(B):
                    s = act.value_load(idx[0:1, 0, b:b + 1], min_val=0, max_val=NS0 - 1)
                    t, r = b // BT, slice((b % BT) * S, (b % BT + 1) * S)
                    act.dma_start(w0[r, t, r], inp["L0_cond_weights"][bass.ds(s, 1)].rearrange("a c d -> (a c) d")).then_inc(w0_in, 16)
                for i, u in enumerate(uses):
                    bank, kind, j = ps[i % 8], *u
                    if u in split_no:
                        act.wait_ge(written, i + 1)
                        if kind == "W1T":
                            dst = w1_hi[:, j, :]
                            src = bank[:]
                        else:
                            if kind == "x3T" and j == 0:
                                act.wait_ge(x_new, 2 * TT)
                            dst = xT_hi[:, :, j * P:(j + 1) * P]
                            src = bank[:].rearrange("p (k t) -> p k t", k=KC)
                        act.activation(dst, src, ACT.Copy).then_inc(split_hi, 1)
                    elif kind == "BwT":
                        act.wait_ge(written, i + 1)
                        rows = P if j == 0 else R
                        act.activation(bw_t[0:rows, j, :], bank[0:rows, :], ACT.Copy).then_inc(bw_ready, 1)
                    elif kind == "W2T" and j % 2 == 0:
                        act.wait_ge(written, i + 1)
                        act.activation(w2t[:, j // KC, j % KC, :], bank[:], ACT.Copy).then_inc(w2_act, 1)

            @block.vector
            def _(dve):
                v = nc.vector
                dve.wait_ge(small_in, 16 * (NL + 2))
                v.tensor_copy(a_hi[:], a_n[:]).then_inc(a_split, 1)
                for l in range(NL):
                    t = v.tensor_scalar(bw_r[:, :, l * R:(l + 1) * R], bw_n[:], 0.5, None, ALU.mult)
                t.then_inc(bw_rep, 1)
                for b in range(BT):
                    r = slice(b * S, (b + 1) * S)
                    t = v.tensor_copy(lab[r, :], lab_i[r, :].rearrange("p (t b) -> p t b", b=BT)[:, :, b])
                t.then_inc(lab_ready, 1)
                dve.wait_ge(a_split, 1)
                v.tensor_tensor(a_lo[:], a_n[:], f32(a_hi[:]), ALU.subtract).then_inc(a_split, 1)
                dve.wait_ge(x_in, 16)
                for i, u in enumerate(uses):
                    bank, kind, j = ps[i % 8], *u
                    if kind in ("L0", "L1", "L2"):
                        dve.wait_ge(written, i + 1)
                        if int(kind[1]):
                            dve.wait_ge(x_new, TT * int(kind[1]))
                        v.tensor_tensor(x[:, j, :], x[:, j, :], bank[:], ALU.add).then_inc(x_new, 1)
                    elif u in split_no:
                        dve.wait_ge(split_hi, split_no[u])
                        if kind == "W1T":
                            lo, hi, src = w1_lo[:, j, :], w1_hi[:, j, :], bank[:]
                        else:
                            t = slice(j * P, (j + 1) * P)
                            lo, hi, src = xT_lo[:, :, t], xT_hi[:, :, t], bank[:].rearrange("p (k t) -> p k t", k=KC)
                        v.tensor_tensor(lo, src, f32(hi), ALU.subtract).then_inc(split_lo, 1)
                    elif kind == "low":
                        dve.wait_ge(written, i + 1)
                        dve.wait_ge(lab_ready, 1)
                        dve.wait_ge(x2m_zero, 2)
                        v.scalar_tensor_tensor(low[:, j, :], lab_of[:], lab[:, j:j + 1], bank[:, 0:LR],
                                               ALU.is_equal, ALU.mult).then_inc(low_ready, 1)
                    elif kind == "lowT":
                        dve.wait_ge(written, i + 1)
                        v.tensor_copy(low_t[:, j, 0:P], bank[:, 0:P])
                        v.tensor_copy(low_t[0:R, j, P:2 * P], bank[0:R, P:2 * P]).then_inc(lowt_ready, 1)
                    elif kind == "W2T" and j % 2 == 1:
                        dve.wait_ge(written, i + 1)
                        v.tensor_copy(w2t[:, j // KC, j % KC, :], bank[:]).then_inc(w2_dve, 1)
                    elif kind == "x2T":
                        dve.wait_ge(written, i + 1)
                        if j >= 2:
                            dve.wait_ge(written, pos_of[("L2", j - 2)] + 1)
                        dve.wait_ge(x2m_zero, 1)
                        for k in range(KC):
                            dst = x2m[:, j % 2, k, :].rearrange("p (b c) -> p b c", c=P + S)[:, :, 0:S]
                            t = v.tensor_copy(dst, bank[:, k * P:(k + 1) * P].rearrange("p (b c) -> p b c", c=S))
                        t.then_inc(x2m_ready, 1)


def stage_project(nc, inp, ident, xT_hi, xT_lo, tabs, q_d, k_d, v_d, kt_d):
    N = HK * TT
    with ExitStack() as ctx:
        m = Bench(nc, ctx, "prj")
        wn = [m.sb(f"wn{i}", [P, WE // P, H]) for i in range(2)]
        wt_hi = [m.sb(f"wt_hi{i}", [P, KC, WE], F32R) for i in range(2)]
        wt_lo = [m.sb(f"wt_lo{i}", [P, KC, WE], F32R) for i in range(2)]
        kn = [m.sb(f"kn{i}", [P, HK * D]) for i in range(2)]
        kst = [m.sb(f"kst{i}", [P, PPT, HK, PS]) for i in range(2)]
        sq = [m.sb(f"sq{i}", [P, QK]) for i in range(2)]
        ta = [m.sb(f"ta{i}", [P, QK]) for i in range(2)]
        tb = [m.sb(f"tb{i}", [P, QK]) for i in range(2)]
        qn = [m.sb(f"qn{i}", [P, QK]) for i in range(2)]
        ss = [m.sb(f"ss{i}", [P, REP + 1]) for i in range(2)]
        rs = [m.sb(f"rs{i}", [P, REP + 1]) for i in range(2)]
        rstd = [m.sb(f"rstd{i}", [P, REP + 1]) for i in range(2)]
        power = m.sb("power", [P, REP + 1])
        floor = m.sb("floor", [P, REP + 1])
        qst = [m.sb(f"qst{i}", [P, BT, ST]) for i in range(2)]
        vst = [m.sb(f"vst{i}", [P, D]) for i in range(4)]
        ps = [m.psum(f"ps{i}", [P, 2 * BANK]) for i in range(2)]
        pt = m.psum("pt", [P, 2 * BANK])
        pw = m.psum("pw", [P, 2, BANK])

        w_in = [m.sem(f"w_in{i}") for i in range(2)]
        kn_in = [m.sem(f"kn_in{i}") for i in range(2)]
        job_t = m.sem("job_t")
        job_act = m.sem("job_act")
        job_dve = m.sem("job_dve")
        mm_done = m.sem("mm_done")
        q_squared = m.sem("q_squared")
        squared = m.sem("squared")
        k_roped = m.sem("k_roped")
        v_staged = m.sem("v_staged")
        roped = m.sem("roped")
        reduced = m.sem("reduced")
        normed = m.sem("normed")
        pool_step = m.sem("pool_step")
        turned = m.sem("turned")
        q_staged = m.sem("q_staged")
        stage_free = m.sem("stage_free")
        kst_free = m.sem("kst_free")
        stored = m.sem("stored")
        k_stored = m.sem("k_stored")

        cq, sn_q, ck, sn_k = tabs
        w_dram = (inp["L3_cond_Wq"], inp["L3_cond_Wk"], inp["L3_cond_Wv"])
        k_rows = inp["L3_cond_k_cache"].rearrange("a s h d -> (a s) (h d)")

        WJ = KC + 2
        UNROLL = 2 * TT

        def job_of(c, g, last_head):
            return WJ + c * (WJ + 2) + g - (WJ if last_head else 0)

        def loop(eng, body):
            last = HK // 2 - 1
            with eng.Fori(0, last) as it:
                for j in range(UNROLL):
                    body(it, j, False)
            for j in range(UNROLL):
                body(last, j, True)

        with nc.Block() as block:

            @block.sync
            def _(sp):
                def load_w(c, slot):
                    for w, rows, o in zip(w_dram, (QW, D, D), (0, REP, REP + 1)):
                        src = w.rearrange("(c o p) i -> c p o i", p=P, o=rows // P)[bass.ds(c, 1)]
                        sp.dma_start(wn[slot][:, o:o + rows // P, :],
                                     src.rearrange("a p o i -> (a p) o i")).then_inc(w_in[slot], 16)

                def load_k(t, slot):
                    src = k_rows.rearrange("(t p) c -> t p c", p=P)[bass.ds(t, 1)]
                    sp.dma_start(kn[slot][:], src.rearrange("a p c -> (a p) c")).then_inc(kn_in[slot], 16)

                sp.sem_inc(stage_free, 2)
                sp.sem_inc(kst_free, 2)
                load_w(0, 0)
                load_w(1, 1)
                load_k(0, 0)
                load_k(1, 1)

                def body(it, j, tail):
                    n, c, t, slot = it * UNROLL + j, it * 2 + j // TT, j % TT, j // TT
                    if t == 0 and not tail:
                        sp.wait_ge(job_t, job_of(c, 0, False))
                        load_w(c + 2, slot)
                    sp.wait_ge(q_staged, n + 3)
                    tile = slice(t * BT, (t + 1) * BT)
                    sp.dma_start(q_d[tile, bass.ds(c, 1)].rearrange("b a d x -> d (b a) x"),
                                 qst[j % 2][:, :, 0:QS]).then_inc(stored, 16)
                    sp.dma_start(k_d[tile, :, bass.ds(c * S, S)].rearrange("b d x -> d b x"),
                                 qst[j % 2][:, :, QS:ST]).then_inc(stored, 16)
                    sp.wait_ge(v_staged, n + 1)
                    sp.dma_start(v_d[t, :, bass.ds(c * D, D)], vst[j % 4][:]).then_inc(stored, 16)
                    sp.wait_ge(stored, (n + 1) * 48)
                    sp.sem_inc(stage_free, 1)
                    if t >= TT - 2:
                        u = t % 2
                        k = c * 2 + u
                        last_head = tail and slot == 1
                        sp.wait_ge(job_act, job_of(c, WJ + u, last_head) + 1)
                        sp.wait_ge(job_dve, job_of(c, WJ + u, last_head) + 1)
                        dst = kt_d[bass.ds(k * PPT, PPT)].rearrange("g d x -> d g x")
                        sp.dma_start(dst, kst[u][:].rearrange("p g h t -> p g (h t)")).then_inc(k_stored, 16)
                        if not last_head:
                            load_k(k + 2, u)
                        sp.wait_ge(k_stored, (k + 1) * 16)
                        sp.sem_inc(kst_free, 1)

                loop(sp, body)

            @block.tensor
            def _(pe):
                def weight_job(g, slot):
                    for i in range(4):
                        k, o = (g, i) if g < KC else ((g - KC) * 2 + i // 2, REP + i % 2)
                        t = pe.transpose(pw[:, g % 2, i * P:(i + 1) * P], wn[slot][:, o, k * P:(k + 1) * P], ident[:])
                    t.then_inc(job_t, 1)

                def cache_job(slot):
                    for h in range(HK):
                        o = pw[:, h // 4, (h % 4) * P:(h % 4 + 1) * P]
                        t = pe.transpose(o, kn[slot][:, h * D:(h + 1) * D], ident[:])
                    t.then_inc(job_t, 1)

                def multiply(j):
                    t, slot = j % TT, j // TT % 2
                    tok = slice(t * P, (t + 1) * P)
                    for out, cols in ((ps[j % 2][:, 0:QW], slice(0, QW)), (ps[j % 2][:, QW:WE], slice(QW, WE))):
                        for k in range(KC):
                            last = three_pass(pe, out, xT_hi[:, k, tok], xT_lo[:, k, tok], wt_hi[slot][:, k, cols],
                                              wt_lo[slot][:, k, cols], k == 0, k == KC - 1)
                    last.then_inc(mm_done, 1)

                pe.wait_ge(w_in[0], 48)
                for g in range(WJ):
                    if g >= 2:
                        pe.wait_ge(job_dve, g - 1)
                    weight_job(g, 0)
                pe.wait_ge(job_dve, WJ)
                multiply(0)
                multiply(1)

                def body(it, j, tail):
                    n, c, t, slot = it * UNROLL + j, it * 2 + j // TT, j % TT, j // TT
                    last_head = tail and slot == 1
                    if t >= WJ or not last_head:
                        pe.wait_ge(job_dve, job_of(c, t, last_head))
                        pe.wait_ge(job_act, job_of(c, t, last_head))
                        if t == 0:
                            pe.wait_ge(w_in[1 - slot], (it + 1 + slot) * 48)
                        if t < WJ:
                            weight_job(t, 1 - slot)
                        else:
                            pe.wait_ge(kn_in[t % 2], (c + 1) * 16)
                            cache_job(t % 2)
                    if not (tail and j >= UNROLL - 2):
                        pe.wait_ge(roped, n + 1)
                        pe.wait_ge(v_staged, n + 1)
                        multiply(j + 2)
                    pe.wait_ge(normed, n + 1)
                    pe.wait_ge(q_staged, n + 2)
                    for h in range(REP + 1):
                        o = pt[:, h * P:(h + 1) * P]
                        last = pe.transpose(o, qn[j % 2][:, h * P:(h + 1) * P], ident[:])
                    last.then_inc(turned, 1)

                loop(pe, body)

            def split_of(g, slot):
                if g < KC:
                    return wt_hi[slot][:, g, 0:QW], wt_lo[slot][:, g, 0:QW], pw[:, g, :] if g < 2 else pw[:, g % 2, :]
                k = slice((g - KC) * 2, (g - KC) * 2 + 2)
                return (wt_hi[slot][:, k, QW:WE], wt_lo[slot][:, k, QW:WE],
                        pw[:, g % 2, :].rearrange("p (k c) -> p k c", k=2))

            def keys_of(half, slot):
                return (kst[slot][:, :, half * 4:half * 4 + 4, :].rearrange("p g h t -> p h g t"),
                        pw[:, half, :].rearrange("p (h g t) -> p h g t", h=4, g=PPT))

            @block.scalar
            def _(act):
                act.sem_inc(q_staged, 2)
                for g in range(WJ):
                    hi, _, bank = split_of(g, 0)
                    act.wait_ge(job_t, g + 1)
                    act.activation(hi, bank, ACT.Copy).then_inc(job_act, 1)

                def squares(j, n):
                    act.wait_ge(mm_done, n + 1)
                    if not isinstance(n, int) or n >= 2:
                        act.wait_ge(reduced, n - 1)
                    act.activation(sq[j % 2][:, 0:QW], ps[j % 2][:, 0:QW], ACT.Square).then_inc(q_squared, 1)
                    act.wait_ge(k_roped, n + 1)
                    act.activation(sq[j % 2][:, QW:QK], ps[j % 2][:, QW:QK], ACT.Square).then_inc(squared, 1)
                    if not isinstance(n, int) or n >= 4:
                        act.wait_ge(stage_free, n - 1)
                    act.activation(vst[j % 4][:], ps[j % 2][:, QK:WE], ACT.Copy).then_inc(v_staged, 1)

                squares(0, 0)
                squares(1, 1)

                def body(it, j, tail):
                    n, c, t, slot = it * UNROLL + j, it * 2 + j // TT, j % TT, j // TT
                    last_head = tail and slot == 1
                    if t >= WJ or not last_head:
                        act.wait_ge(job_t, job_of(c, t, last_head) + 1)
                        if t < WJ:
                            hi, _, bank = split_of(t, 1 - slot)
                            act.activation(hi, bank, ACT.Copy).then_inc(job_act, 1)
                        else:
                            act.wait_ge(kst_free, c * 2 + t % 2 + 1)
                            dst, bank = keys_of(0, t % 2)
                            act.activation(dst, bank, ACT.Copy).then_inc(job_act, 1)
                    if not (tail and j >= UNROLL - 2):
                        squares(j + 2, n + 2)
                    act.wait_ge(turned, n + 1)
                    act.wait_ge(stage_free, n + 1)
                    q_src = pt[:, 0:QW].rearrange("p (h b t) -> p b h t", h=REP, b=BT)
                    k_src = pt[:, QW:QK].rearrange("p (b t) -> p b t", b=BT)
                    act.activation(qst[j % 2][:, :, 0:QS].rearrange("p b (h t) -> p b h t", h=REP), q_src, ACT.Copy)
                    act.activation(qst[j % 2][:, :, QS:ST], k_src, ACT.Copy).then_inc(q_staged, 1)

                loop(act, body)

            @block.vector
            def _(dve):
                v = nc.vector
                for g in range(WJ):
                    hi, lo, bank = split_of(g, 0)
                    dve.wait_ge(job_act, g + 1)
                    v.tensor_tensor(lo, bank, f32(hi), ALU.subtract).then_inc(job_dve, 1)

                def rope(j, n):
                    t, s = j % TT, j % 2
                    dve.wait_ge(mm_done, n + 1)
                    if not isinstance(n, int) or n >= 2:
                        dve.wait_ge(normed, n - 1)
                    q = ps[s][:, 0:QW].rearrange("p (h d) -> p h d", h=REP)
                    a = ta[s][:, 0:QW].rearrange("p (h d) -> p h d", h=REP)
                    b = tb[s][:, 0:QW].rearrange("p (h d) -> p h d", h=REP)
                    lo, hi = slice(0, HALF), slice(HALF, D)
                    k = ps[s][:, QW:QK]
                    v.tensor_tensor(ta[s][:, QW:QK], k, ck[:, t, :], ALU.mult)
                    v.tensor_tensor(tb[s][:, QW:QW + HALF], k[:, hi], sn_k[:, t, lo], ALU.mult)
                    v.tensor_tensor(tb[s][:, QW + HALF:QK], k[:, lo], sn_k[:, t, hi], ALU.mult).then_inc(k_roped, 1)
                    dve.wait_ge(q_squared, n + 1)
                    v.tensor_tensor(a, q, cq[:, t:t + 1, :].broadcast_to([P, REP, D]), ALU.mult)
                    v.tensor_tensor(b[:, :, lo], q[:, :, hi], sn_q[:, t:t + 1, lo].broadcast_to([P, REP, HALF]), ALU.mult)
                    v.tensor_tensor(b[:, :, hi], q[:, :, lo], sn_q[:, t:t + 1, hi].broadcast_to([P, REP, HALF]), ALU.mult).then_inc(roped, 1)
                    dve.wait_ge(squared, n + 1)
                    v.tensor_reduce(ss[s][:], sq[s][:].rearrange("p (h d) -> p h d", h=REP + 1), AX_X, ALU.add).then_inc(reduced, 1)

                rope(0, 0)
                rope(1, 1)

                def body(it, j, tail):
                    n, c, t, slot = it * UNROLL + j, it * 2 + j // TT, j % TT, j // TT
                    last_head = tail and slot == 1
                    if t >= WJ or not last_head:
                        if t < WJ:
                            hi, lo, bank = split_of(t, 1 - slot)
                            dve.wait_ge(job_act, job_of(c, t, last_head) + 1)
                            v.tensor_tensor(lo, bank, f32(hi), ALU.subtract).then_inc(job_dve, 1)
                        else:
                            dve.wait_ge(job_t, job_of(c, t, last_head) + 1)
                            dve.wait_ge(kst_free, c * 2 + t % 2 + 1)
                            dst, bank = keys_of(1, t % 2)
                            v.tensor_copy(dst, bank).then_inc(job_dve, 1)
                    if not (tail and j >= UNROLL - 2):
                        rope(j + 2, n + 2)

                loop(dve, body)

            @block.gpsimd
            def _(pool):
                g = nc.gpsimd
                g.memset(power[:], -0.5)
                g.memset(floor[:], D * EPS).then_inc(pool_step, 1)
                pool.wait_ge(pool_step, 1)

                def body(it, j, tail):
                    n, s = it * UNROLL + j, j % 2
                    pool.wait_ge(roped, n + 1)
                    g.tensor_tensor(ta[s][:], ta[s][:], tb[s][:], ALU.add).then_inc(pool_step, 1)
                    pool.wait_ge(reduced, n + 1)
                    pool.wait_ge(q_staged, n + 1)
                    g.tensor_tensor(rs[s][:], ss[s][:], floor[:], ALU.add).then_inc(pool_step, 1)
                    pool.wait_ge(pool_step, n * 3 + 3)
                    g.tensor_tensor(rstd[s][:], rs[s][:], power[:], ALU.pow).then_inc(pool_step, 1)
                    pool.wait_ge(pool_step, n * 3 + 4)
                    r = rstd[s][:].rearrange("p (h a) -> p h a", a=1).broadcast_to([P, REP + 1, D])
                    rows = lambda x: x[s][:].rearrange("p (h d) -> p h d", h=REP + 1)
                    g.tensor_tensor(rows(qn), rows(ta), r, ALU.mult).then_inc(normed, 1)

                loop(pool, body)


def stage_attend(nc, inp, ident, q_d, k_d, v_d, kt_d, o_d):
    GROUP = 4
    UNROLL = 2 * HK
    N = B * HK
    AHEAD = 3
    with ExitStack() as ctx:
        m = Bench(nc, ctx, "att")
        PG = NPP + 1
        PA = (PG + 1) // 2
        KA, KB = PA * PS, (PG - PA) * PS
        PAD = 2 * KA
        kT = [m.sb(f"kT{i}", [P, PG, HK, PS]) for i in range(2)]
        vc = [m.sb(f"vc{i}", [P, NCH, HK * D]) for i in range(2)]
        q = [m.sb(f"q{i}", [P, HK, QS]) for i in range(2)]
        vn = [m.sb(f"vn{i}", [S, HK * D]) for i in range(2)]
        table = m.sb("table", [1, B * NPP], I32)
        len_i = m.sb("len_i", [P, B], I32)
        lens = m.sb("lens", [P, B])
        key_no = m.sb("key_no", [P, PAD])
        mask = [m.sb(f"mask{i}", [P, PAD]) for i in range(2)]
        neg = [m.sb(f"neg{i}", [P, PAD]) for i in range(2)]
        nmax = [m.sb(f"nmax{i}", [P, 1]) for i in range(2)]
        prob = [m.sb(f"prob{i}", [P, KEYS]) for i in range(2)]
        total = [m.sb(f"total{i}", [P, 1]) for i in range(2)]
        inv = [m.sb(f"inv{i}", [P, 1]) for i in range(2)]
        pT = m.sb("pT", [P, NCH + 1, P])
        ost = [m.sb(f"ost{i}", [P, HK, P]) for i in range(2)]
        ps = [m.psum(f"ps{i}", [P, 2, BANK]) for i in range(2)]
        pa = m.psum("pa", [P, BANK])
        pb = m.psum("pb", [P, BANK])
        po = [m.psum(f"po{i}", [P, BANK]) for i in range(2)]

        NA = 2
        table_in = m.sem("table_in")
        lens_in = m.sem("lens_in")
        lens_ready = m.sem("lens_ready")
        kq_in = [m.sem(f"kq_in{i}") for i in range(2)]
        v_in = [m.sem(f"v_in{i}") for i in range(2)]
        numbered = m.sem("numbered")
        padded = m.sem("padded")
        masked = m.sem("masked")
        may_reduce = m.sem("may_reduce")
        scored = m.sem("scored")
        maxed = m.sem("maxed")
        exped = m.sem("exped")
        inverted = m.sem("inverted")
        normed = m.sem("normed")
        turned = m.sem("turned")
        out_a = m.sem("out_a")
        out_b = m.sem("out_b")
        valued = m.sem("valued")
        o_staged = m.sem("o_staged")
        o_stored = m.sem("o_stored")
        ost_free = m.sem("ost_free")

        def pages_of(b, engine):
            return nc.values_load_multi_w_load_instructions(table[0:1, bass.ds(b * NPP, NPP)], engines=[engine],
                                                            min_val=0, max_val=PAGES - 1)[1]

        v_pages = inp["L3_cond_v_cache"].rearrange("g s h d -> g s (h d)")

        with nc.Block() as block:

            @block.sync
            def _(sp):
                sp.dma_start(table[:], inp["itok_Bx16_0_63"].rearrange("(a b) j -> a (b j)", a=1)).then_inc(table_in, 16)
                sp.dma_start(len_i[:], inp["itok_B_207_1644"].partition_broadcast(P)).then_inc(lens_in, 16)
                sp.wait_ge(table_in, 16)
                sp.sem_inc(ost_free, 2)

                def load(b, slot):
                    sp.dma_start(q[slot][:], q_d[bass.ds(b, 1)].rearrange("a h d x -> d (a h) x")).then_inc(kq_in[slot], 16)
                    sp.dma_start(kT[slot][:, NPP].rearrange("p h t -> p (h t)"),
                                 k_d[bass.ds(b, 1)].rearrange("a d x -> (a d) x")).then_inc(kq_in[slot], 16)
                    for j, g in enumerate(pages_of(b, mybir.EngineType.SP)):
                        sp.dma_start(kT[slot][:, j].rearrange("p h t -> p (h t)"),
                                     kt_d[bass.ds(g, 1)].rearrange("a d x -> (a d) x")).then_inc(kq_in[slot], 16)

                load(0, 0)
                load(1, 1)

                def body(it, tail):
                    for slot in range(2):
                        b = it * 2 + slot
                        if not tail:
                            sp.wait_ge(scored, b * HK + HK)
                            load(b + 2, slot)
                        sp.wait_ge(o_staged, (b + 1) * (HK // GROUP) + 2)
                        sp.dma_start(o_d[bass.ds(b, 1)].rearrange("a d x -> (a d) x"),
                                     ost[slot][:].rearrange("p h x -> p (h x)")).then_inc(o_stored, 16)
                        sp.wait_ge(o_stored, (b + 1) * 16)
                        sp.sem_inc(ost_free, 1)

                with sp.Fori(0, B // 2 - 1) as it:
                    body(it, False)
                body(B // 2 - 1, True)

            @block.gpsimd
            def _(pool):
                g = nc.gpsimd
                g.iota(key_no[:, 0:L], pattern=[[1, L]], base=0, channel_multiplier=0,
                       allow_small_or_imprecise_dtypes=True).then_inc(numbered, 1)
                g.memset(key_no[:, L:KEYS], -1.0).then_inc(numbered, 1)
                g.memset(key_no[:, KEYS:PAD], MASKED).then_inc(numbered, 1)
                pool.wait_ge(table_in, 16)

                def load(b, slot):
                    pool.dma_start(vn[slot][:], v_d[bass.ds(b, 1)].rearrange("a s c -> (a s) c")).then_inc(v_in[slot], 16)
                    for j, page in enumerate(pages_of(b, mybir.EngineType.Pool)):
                        r = slice(j % PPT * PS, (j % PPT + 1) * PS)
                        pool.dma_start(vc[slot][r, j // PPT, :], v_pages[bass.ds(page, 1)].rearrange("a s c -> (a s) c")).then_inc(v_in[slot], 16)

                load(0, 0)
                load(1, 1)
                with pool.Fori(0, B // 2 - 1) as it:
                    for slot in range(2):
                        b = it * 2 + slot
                        pool.wait_ge(valued, b * HK + HK)
                        load(b + 2, slot)

            @block.tensor
            def _(pe):
                def scores(j, it=None):
                    s, h = j // HK % 2, j % HK
                    pe.matmul(ps[j % 2][:, 0, 0:KA], q[s][:, h, :], kT[s][:, 0:PA, h, :], start=True, stop=True)
                    pe.matmul(ps[j % 2][:, 1, 0:KB], q[s][:, h, :], kT[s][:, PA:PG, h, :], start=True, stop=True).then_inc(scored, 1)

                def turn(j):
                    p = prob[j % 2]
                    for c in range(NCH):
                        o = pa[:, c * P:(c + 1) * P] if c < NA else pb[:, (c - NA) * P:(c - NA + 1) * P]
                        pe.transpose(o, p[:, c * P:(c + 1) * P], ident[:])
                    pe.transpose(pb[0:S, (NCH - NA) * P:(NCH - NA + 1) * P], p[:, L:KEYS], ident[:]).then_inc(turned, 1)

                def values(j):
                    s, h = j // HK % 2, j % HK
                    cols = slice(h * D, (h + 1) * D)
                    o = po[j // GROUP % 2][:, j % GROUP * P:(j % GROUP + 1) * P]
                    for c in range(NCH):
                        pe.matmul(o, vc[s][:, c, cols], pT[:, c, :], start=(c == 0), stop=False)
                    pe.matmul(o, vn[s][:, cols], pT[0:S, NCH, :], start=False, stop=True).then_inc(valued, 1)

                pe.wait_ge(padded, 2)
                pe.wait_ge(kq_in[0], 16 * (PG + 1))
                scores(0)
                scores(1)
                pe.wait_ge(normed, 1)
                turn(0)
                pe.wait_ge(maxed, 1)
                scores(2)

                def body(it, j, tail):
                    n = it * UNROLL + j
                    b = it * 2 + j // HK
                    pe.wait_ge(out_a, n + 1)
                    pe.wait_ge(out_b, n + 1)
                    if j % GROUP == 0:
                        pe.wait_ge(o_staged, it * (UNROLL // GROUP) + j // GROUP + 1)
                    if j % HK == 0:
                        pe.wait_ge(v_in[j // HK], (it + 1) * 16 * PG)
                    values(j)
                    if not (tail and j + 1 >= UNROLL):
                        pe.wait_ge(normed, n + 2)
                        turn(j + 1)
                    if not (tail and j + AHEAD >= UNROLL):
                        pe.wait_ge(maxed, n + 2)
                        if (j + AHEAD) % HK == 0:
                            pe.wait_ge(kq_in[(j + AHEAD) // HK % 2], (it + (j + AHEAD) // UNROLL + 1) * 16 * (PG + 1))
                        scores(j + AHEAD)

                with pe.Fori(0, B // 2 - 1) as it:
                    for j in range(UNROLL):
                        body(it, j, False)
                for j in range(UNROLL):
                    body(B // 2 - 1, j, True)

            @block.vector
            def _(dve):
                v = nc.vector
                for i in range(2):
                    v.memset(ps[i][:, 1, KB:KA], 0.0).then_inc(padded, 1)
                dve.wait_ge(lens_in, 16)
                v.tensor_copy(lens[:], len_i[:]).then_inc(lens_ready, 1)

                def smallest(j):
                    halves = [a.rearrange("p (a k) -> p a k", a=2) for a in (neg[j % 2][:], mask[j // HK % 2][:])]
                    v.tensor_tensor_reduce(halves[0], halves[1], ps[j % 2][:, :, 0:KA], 1.0, 3.0e38,
                                           ALU.add, ALU.min, nmax[j % 2][:]).then_inc(maxed, 1)

                def make_mask(b, slot):
                    v.tensor_scalar(mask[slot][:], key_no[:], lens[:, bass.ds(b, 1)], MASKED, ALU.is_ge, ALU.mult).then_inc(masked, 1)

                def minimum(j, n, b):
                    dve.wait_ge(scored, n + 1)
                    if j % HK == 0:
                        dve.wait_ge(masked, b + 1)
                    dve.sem_inc(may_reduce, 1)
                    smallest(j)

                def normalize(j, n):
                    dve.wait_ge(exped, n + 1)
                    v.reciprocal(inv[j % 2][:], total[j % 2][:]).then_inc(inverted, 1)
                    dve.wait_ge(inverted, n + 1)
                    v.tensor_scalar(prob[j % 2][:], prob[j % 2][:], inv[j % 2][:, 0:1], None, ALU.mult).then_inc(normed, 1)

                dve.wait_ge(padded, 2)
                dve.wait_ge(numbered, 3)
                dve.wait_ge(lens_ready, 1)
                make_mask(0, 0)
                make_mask(1, 1)
                minimum(0, 0, 0)
                minimum(1, 1, 0)
                normalize(0, 0)

                def body(it, j, tail):
                    n = it * UNROLL + j
                    dve.wait_ge(turned, n + 1)
                    v.tensor_copy(pT[:, 0:NA, :], pa[:, 0:NA * P].rearrange("p (c q) -> p c q", c=NA)).then_inc(out_a, 1)
                    if not (tail and j + 1 >= UNROLL):
                        normalize(j + 1, n + 1)
                    if not (tail and j + 2 >= UNROLL):
                        minimum(j + 2, n + 2, it * 2 + (j + 2) // HK)
                    if not tail and j % HK == HK - 2:
                        dve.wait_ge(maxed, n + 2)
                        make_mask(it * 2 + 2 + j // HK, j // HK)

                with dve.Fori(0, B // 2 - 1) as it:
                    for j in range(UNROLL):
                        body(it, j, False)
                for j in range(UNROLL):
                    body(B // 2 - 1, j, True)

            @block.scalar
            def _(act):
                act.sem_inc(o_staged, 2)

                def exps(j, n):
                    act.wait_ge(maxed, n + 1)
                    act.activation(prob[j % 2][:], neg[j % 2][:, 0:KEYS], ACT.Exp, bias=nmax[j % 2][:, 0:1], scale=-1.0,
                                   accum_out=total[j % 2][:]).then_inc(exped, 1)

                def keep(n):
                    act.wait_ge(turned, n + 1)
                    act.activation(pT[:, NA:NCH, :], pb[:, 0:(NCH - NA) * P].rearrange("p (c q) -> p c q", q=P), ACT.Copy)
                    act.activation(pT[0:S, NCH, :], pb[0:S, (NCH - NA) * P:(NCH - NA + 1) * P], ACT.Copy).then_inc(out_b, 1)

                exps(0, 0)
                exps(1, 1)
                keep(0)

                def body(it, j, tail):
                    n = it * UNROLL + j
                    if not (tail and j + 2 >= UNROLL):
                        exps(j + 2, n + 2)
                    if not (tail and j + 1 >= UNROLL):
                        keep(n + 1)
                    if j % GROUP == GROUP - 1:
                        g = j // GROUP
                        act.wait_ge(valued, n + 1)
                        if g % 2 == 0:
                            act.wait_ge(ost_free, it * 2 + j // HK + 1)
                        act.activation(ost[j // HK][:, g % 2 * GROUP:(g % 2 + 1) * GROUP, :],
                                       po[g % 2][:].rearrange("p (h q) -> p h q", h=GROUP), ACT.Copy).then_inc(o_staged, 1)

                with act.Fori(0, B // 2 - 1) as it:
                    for j in range(UNROLL):
                        body(it, j, False)
                for j in range(UNROLL):
                    body(B // 2 - 1, j, True)


def stage_output(nc, inp, ident, o_d, x3_d, out_d):
    CH = HQ * D // P
    Q = 4
    CQ = CH // Q
    UNROLL = 2 * Q
    SL = 8
    CS = CH // SL
    with ExitStack() as ctx:
        m = Bench(nc, ctx, "out")
        wn = [m.sb(f"wn{i}", [P, KC, CS * P]) for i in range(2)]
        wt_hi = m.sb("wt_hi", [P, CH, H], F32R)
        wt_lo = m.sb("wt_lo", [P, CH, H], F32R)
        o_n = [m.sb(f"o_n{i}", [P, BT, CQ * S]) for i in range(2)]
        o_hi = [m.sb(f"o_hi{i}", [P, CQ, P], F32R) for i in range(2)]
        o_lo = [m.sb(f"o_lo{i}", [P, CQ, P], F32R) for i in range(2)]
        x3 = [m.sb(f"x3{i}", [P, H]) for i in range(2)]
        y = [m.sb(f"y{i}", [P, H]) for i in range(2)]
        pw = [m.psum(f"pw{i}", [P, BANK]) for i in range(4)]
        py = [m.psum(f"py{i}", [P, BANK]) for i in range(2)]

        w_in = [m.sem(f"w_in{i}") for i in range(2)]
        w_turned = m.sem("w_turned")
        w_hi = m.sem("w_hi")
        w_lo = m.sem("w_lo")
        o_in = [m.sem(f"o_in{i}") for i in range(2)]
        x3_in = [m.sem(f"x3_in{i}") for i in range(2)]
        o_hi_done = m.sem("o_hi_done")
        o_lo_done = m.sem("o_lo_done")
        unit_done = m.sem("unit_done")
        summed = m.sem("summed")
        stored = [m.sem(f"stored{i}") for i in range(2)]

        with nc.Block() as block:

            @block.sync
            def _(sp):
                def load_w(s):
                    src = inp["L3_cond_Wo"][:, s * CS * P:(s + 1) * CS * P].rearrange("(o p) e -> p o e", p=P)
                    sp.dma_start(wn[s % 2][:], src).then_inc(w_in[s % 2], 16)

                def load_o(it, i):
                    t, q, s = it * 2 + i // Q, i % Q, i % 2
                    src = o_d[bass.ds(t * BT, BT), :, q * CQ * S:(q + 1) * CQ * S].rearrange("b d x -> d b x")
                    sp.dma_start(o_n[s][:], src).then_inc(o_in[s], 16)
                    if q == 0:
                        x = x3_d[bass.ds(t, 1)].rearrange("a p h -> (a p) h")
                        sp.dma_start(x3[i // Q % 2][:], x).then_inc(x3_in[i // Q % 2], 16)

                for s in range(SL):
                    if s >= 2:
                        sp.wait_ge(w_turned, (s - 1) * CS)
                    load_w(s)
                load_o(0, 0)
                load_o(0, 1)

                def store(t, s):
                    sp.wait_ge(summed, t + 1)
                    sp.dma_start(out_d[bass.ds(t, 1)].rearrange("a p h -> (a p) h"), y[s][:]).then_inc(stored[s], 16)

                def body(it, i, first, tail):
                    u = it * UNROLL + i
                    if not (tail and i + 2 >= UNROLL):
                        sp.wait_ge(o_lo_done, u + 1)
                        if (i + 2) % Q == 0 and not (first and i + 2 == Q):
                            sp.wait_ge(summed, it * 2 + (i + 2) // Q - 1)
                        load_o(it, i + 2)
                    if i % Q == 1 and not (first and i == 1):
                        store(it * 2 + i // Q - 1, (i // Q + 1) % 2)

                for i in range(UNROLL):
                    body(0, i, True, False)
                with sp.Fori(1, TT // 2 - 1) as it:
                    for i in range(UNROLL):
                        body(it, i, False, False)
                for i in range(UNROLL):
                    body(TT // 2 - 1, i, False, True)
                store(TT - 1, (TT - 1) % 2)
                for s in range(2):
                    sp.wait_ge(stored[s], 16 * (TT // 2))

            @block.tensor
            def _(pe):
                for c in range(CH):
                    s = c // CS
                    if c % CS == 0:
                        pe.wait_ge(w_in[s % 2], 16 * (s // 2 + 1))
                    if c >= 4:
                        pe.wait_ge(w_lo, c - 3)
                    for o in range(KC):
                        t = pe.transpose(pw[c % 4][:, o * P:(o + 1) * P], wn[s % 2][:, o, c % CS * P:(c % CS + 1) * P], ident[:])
                    t.then_inc(w_turned, 1)
                pe.wait_ge(w_lo, CH)

                def body(it, i, tail):
                    u, q = it * UNROLL + i, i % Q
                    pe.wait_ge(o_lo_done, u + 1)
                    if q == 0 and not (isinstance(it, int) and it == 0):
                        pe.wait_ge(summed, it * 2 + i // Q - 1)
                    for c in range(CQ):
                        w = q * CQ + c
                        last = three_pass(pe, py[i // Q][:], o_hi[i % 2][:, c, :], o_lo[i % 2][:, c, :], wt_hi[:, w, :],
                                          wt_lo[:, w, :], w == 0, w == CH - 1)
                    last.then_inc(unit_done, 1)

                for i in range(UNROLL):
                    body(0, i, False)
                with pe.Fori(1, TT // 2) as it:
                    for i in range(UNROLL):
                        body(it, i, False)

            @block.scalar
            def _(act):
                for c in range(CH):
                    act.wait_ge(w_turned, c + 1)
                    act.activation(wt_hi[:, c, :], pw[c % 4][:], ACT.Copy).then_inc(w_hi, 1)

                def body(it, i):
                    u = it * UNROLL + i
                    act.wait_ge(o_in[i % 2], (it * (UNROLL // 2) + i // 2 + 1) * 16)
                    if not isinstance(u, int) or u >= 2:
                        act.wait_ge(unit_done, u - 1)
                    src = o_n[i % 2][:].rearrange("p b (c t) -> p c b t", c=CQ)
                    dst = o_hi[i % 2][:].rearrange("p c (b t) -> p c b t", b=BT)
                    act.activation(dst, src, ACT.Copy).then_inc(o_hi_done, 1)

                for i in range(UNROLL):
                    body(0, i)
                with act.Fori(1, TT // 2) as it:
                    for i in range(UNROLL):
                        body(it, i)

            @block.vector
            def _(dve):
                v = nc.vector
                for c in range(CH):
                    dve.wait_ge(w_hi, c + 1)
                    v.tensor_tensor(wt_lo[:, c, :], pw[c % 4][:], f32(wt_hi[:, c, :]), ALU.subtract).then_inc(w_lo, 1)

                def add(t, s, round_of, first):
                    dve.wait_ge(unit_done, t * Q + Q)
                    dve.wait_ge(x3_in[s], (round_of + 1) * 16)
                    if not first:
                        dve.wait_ge(stored[s], round_of * 16)
                    v.tensor_tensor(y[s][:], x3[s][:], py[s][:], ALU.add).then_inc(summed, 1)

                def body(it, i, peeled):
                    u = it * UNROLL + i
                    dve.wait_ge(o_hi_done, u + 1)
                    src = o_n[i % 2][:].rearrange("p b (c t) -> p c b t", c=CQ)
                    dst = o_lo[i % 2][:].rearrange("p c (b t) -> p c b t", b=BT)
                    hi = f32(o_hi[i % 2][:]).rearrange("p c (b t) -> p c b t", b=BT)
                    v.tensor_tensor(dst, src, hi, ALU.subtract).then_inc(o_lo_done, 1)
                    if i == 1 and not peeled:
                        add(it * 2 - 1, 1, it - 1, isinstance(it, int))
                    if i == Q + 1:
                        add(it * 2, 0, it, peeled)

                for i in range(UNROLL):
                    body(0, i, True)
                for i in range(UNROLL):
                    body(1, i, False)
                with dve.Fori(2, TT // 2) as it:
                    for i in range(UNROLL):
                        body(it, i, False)
                add(TT - 1, 1, TT // 2 - 1, False)


def program(nc, inp, out):
    x3_d = nc.dram_tensor("x3_scratch", [TT, P, H], F32).ap()
    q_d = nc.dram_tensor("q_scratch", [B, HK, D, QS], F32).ap()
    k_d = nc.dram_tensor("k_scratch", [B, D, HK * S], F32).ap()
    v_d = nc.dram_tensor("v_scratch", [TT, P, HK * D], F32).ap()
    kt_d = nc.dram_tensor("kt_scratch", [PAGES, D, HK * PS], F32).ap()
    o_d = nc.dram_tensor("o_scratch", [B, D, HK * P], F32).ap()
    with ExitStack() as ctx:
        ident = ctx.enter_context(nc.sbuf_tensor("ident", [P, P], F32))
        with ExitStack() as early:
            xT_hi = early.enter_context(nc.sbuf_tensor("xT_hi", [P, KC, TOK], F32R))
            xT_lo = early.enter_context(nc.sbuf_tensor("xT_lo", [P, KC, TOK], F32R))
            stage_layers(nc, inp, ident, xT_hi, xT_lo, x3_d)
            tabs = [early.enter_context(nc.sbuf_tensor(f"tab{i}", [P, TT, D], F32)) for i in range(4)]
            stage_rope(nc, inp, tabs)
            stage_project(nc, inp, ident, xT_hi, xT_lo, tabs, q_d, k_d, v_d, kt_d)
        v_rows = v_d.rearrange("t (b s) c -> (t b) s c", s=S)
        stage_attend(nc, inp, ident, q_d, k_d, v_rows, kt_d, o_d)
        stage_output(nc, inp, ident, o_d, x3_d, out.rearrange("(t b) s h -> t (b s) h", b=BT))


INPUTS = ["x", "itok_B_0_15", "itok_B_0_2", "itok_B_3_7", "itok_Bx16_0_63", "itok_B_207_1644", "L0_cond_weights",
          "L1_cond_W", "L1_cond_lora_A", "L1_cond_lora_B_w", "L2_cond_weight", "L3_cond_Wq", "L3_cond_Wk", "L3_cond_Wv",
          "L3_cond_Wo", "L3_cond_q_norm_w", "L3_cond_k_norm_w", "L3_cond_k_cache", "L3_cond_v_cache"]


def inverse_frequencies():
    return (np.float32(1.0) / np.power(np.float32(THETA), np.arange(0, D, 2, dtype=np.float32) / np.float32(D))).astype(np.float32)


def kernel(**inputs):
    import concourse.bacc as bacc
    from concourse.bass_utils import run_bass_kernel_spmd as run

    nc = bacc.Bacc("TRN2", target_bir_lowering=False, num_devices=1)
    arrays, args = {}, {}
    for name in INPUTS + ["rope_inv_freq"]:
        a = inverse_frequencies() if name == "rope_inv_freq" else np.ascontiguousarray(inputs[name])
        arrays[f"in_{name}"] = a
        args[name] = nc.dram_tensor(f"in_{name}", a.shape, mybir.dt.from_np(a.dtype), kind="ExternalInput").ap()
    out = nc.dram_tensor("out", [B, S, H], F32, kind="ExternalOutput").ap()
    program(nc, args, out)
    return run(nc, [arrays], core_ids=[0]).results[0]["out"]
```

```python
from contextlib import ExitStack

import concourse.bass as bass
import numpy as np
from concourse import mybir

F32 = mybir.dt.float32
F32R = mybir.dt.float32r
I32 = mybir.dt.int32
ALU = mybir.AluOpType
ACT = mybir.ActivationFunctionType
AX_X = mybir.AxisListType.X

P = 128
BANK = 512
B, S, H = 32, 32, 512
TOK = B * S
TT = TOK // P
BT = P // S
KC = H // P
NS0 = 16
NL, R = 5, 32
LR = NL * R
NE = 8
D, HQ, HK = 128, 32, 8
REP = HQ // HK
QW = REP * D
WE = QW + 2 * D
QK = QW + D
PAGES, PS, NPP = 64, 32, 16
L = NPP * PS
KEYS = L + S
NCH = L // P
PPT = P // PS
QS = REP * S
ST = QS + S
THETA, EPS = 10000.0, 1e-6
SCALE = float(1.0 / np.sqrt(D))
HALF = D // 2
MASKED = 1e30
MAGIC = 1.5 * 2.0**23
TWO_PI_HI = 6.28125
TWO_PI_LO = float(2.0 * np.pi - TWO_PI_HI)
IN_RANGE = "the block table holds numbers of pages"
PI_IN = float(np.nextafter(np.float32(np.pi), np.float32(0.0)))


def f32(ap):
    return ap.bitcast(F32)


class Bench:

    def __init__(self, nc, ctx, prefix):
        self.nc, self.ctx, self.prefix = nc, ctx, prefix

    def sb(self, name, shape, dt=F32):
        return self.ctx.enter_context(self.nc.sbuf_tensor(f"{self.prefix}_{name}", shape, dt))

    def psum(self, name, shape):
        return self.ctx.enter_context(self.nc.psum_tensor(f"{self.prefix}_{name}", shape, F32))

    def sem(self, name):
        return self.ctx.enter_context(self.nc.semaphore(f"{self.prefix}_{name}"))


def three_pass(pe, out, w_hi, w_lo, x_hi, x_lo, first, last):
    pe.matmul(out, w_lo, x_hi, start=first, stop=False)
    pe.matmul(out, w_hi, x_lo, start=False, stop=False)
    return pe.matmul(out, w_hi, x_hi, start=False, stop=last)


def load_head(eng, inp, c, tile, sem):
    for name, rows, o in zip(("L3_cond_Wq", "L3_cond_Wk", "L3_cond_Wv"), (QW, D, D), (0, REP, REP + 1)):
        src = inp[name].rearrange("(c o p) i -> c p o i", p=P, o=rows // P)[bass.ds(c, 1)]
        eng.dma_start(tile[:, o:o + rows // P, :], src.rearrange("a p o i -> (a p) o i")).then_inc(sem, 16)


def stage_layers(nc, inp, ident, xT_hi, xT_lo, tabs, len_i, w2n, w_in, x3_d):
    with ExitStack() as ctx:
        m = Bench(nc, ctx, "lay")
        x = m.sb("x", [P, TT, H])
        room = tabs[:].rearrange("p a t d -> p (a t d)")
        w0 = room[:, 3 * TT * P:].rearrange("p (t c) -> p t c", t=TT)
        idx = m.sb("idx", [1, 2, B], I32)
        w1n = m.sb("w1n", [P, KC, H])
        w1_hi = m.sb("w1_hi", [P, KC, H], F32R)
        w1_lo = m.sb("w1_lo", [P, KC, H], F32R)
        a_n = m.sb("a_n", [P, KC, LR])
        a_hi = m.sb("a_hi", [P, KC, LR], F32R)
        a_lo = m.sb("a_lo", [P, KC, LR], F32R)
        bw_n = m.sb("bw_n", [P, KC, R])
        bw_r = m.sb("bw_r", [P, KC, LR])
        bw_t = room[:, 2 * TT * P:3 * TT * P].rearrange("p (a o) -> p a o", a=2)
        lab_i = m.sb("lab_i", [P, B], I32)
        lab = m.sb("lab", [P, TT])
        lab_of = m.sb("lab_of", [P, LR])
        low = m.sb("low", [P, TT, LR])
        low_t = room[:, 0:2 * TT * P].rearrange("p (t c) -> p t c", t=TT)
        w2t = m.sb("w2t", [P, NE, KC, H])
        XM = BT * (P + S)
        x2m = m.sb("x2m", [P, 2, KC, XM])
        inv = m.sb("inv", [P, HALF])
        pos_i = m.sb("pos_i", [P, 1], I32)
        row_i = m.sb("row_i", [P, 1], I32)
        base = m.sb("base", [P, 1])
        pos = m.sb("pos", [P, TT])
        angle = low[:].rearrange("p t r -> p (t r)")[:, 0:TT * HALF].rearrange("p (t d) -> p t d", t=TT)
        turns, *trig = (w1n[:, i].rearrange("p (t d) -> p t d", t=TT) for i in range(3))
        nw, nw_neg = (w1n[:, 3, i * 2 * D:(i + 1) * 2 * D].rearrange("p (a d) -> p a d", a=2) for i in range(2))
        ps = [m.psum(f"ps{i}", [P, BANK]) for i in range(8)]
        written = m.sem("written")
        x_in = [m.sem("x_in0"), m.sem("x_in1")]
        bw_in = m.sem("bw_in")
        w0_zero = m.sem("w0_zero")
        ident_made = m.sem("ident_made")
        idx_in = m.sem("idx_in")
        w0_in = [m.sem("w0_in0"), m.sem("w0_in1")]
        w1_in = m.sem("w1_in")
        small_in = m.sem("small_in")
        w2_in = [m.sem("w2_in0"), m.sem("w2_in1")]
        x_new = m.sem("x_new")
        split_hi = m.sem("split_hi")
        split_lo = m.sem("split_lo")
        a_split = m.sem("a_split")
        bw_rep = m.sem("bw_rep")
        bw_ready = m.sem("bw_ready")
        lab_ready = m.sem("lab_ready")
        low_ready = m.sem("low_ready")
        lowt_ready = m.sem("lowt_ready")
        w2_act = m.sem("w2_act")
        w2_dve = m.sem("w2_dve")
        lab_numbered = m.sem("lab_numbered")
        x2m_zero = m.sem("x2m_zero")
        x2m_ready = m.sem("x2m_ready")
        rope_in = m.sem("rope_in")
        rope_no = m.sem("rope_no")
        prep = m.sem("prep")
        reduced = m.sem("reduced")
        trig_done = m.sem("trig_done")
        x3_out = m.sem("x3_out")

        ex = [("W2T", e * KC + k) for e in range(NE) for k in range(KC)]
        uses = [("W1T", k) for k in range(KC)] + ex[:4] + [("BwT", 0), ("BwT", 1)]
        uses += [("L0", t) for t in range(TT)] + [("x1T", t) for t in range(TT)]
        uses += ex[4:8] + [("low", t) for t in range(TT)]
        uses += ex[8:12] + [("lowT", t) for t in range(TT)] + ex[12:16]
        for t in range(TT):
            uses += [("L1", t)] + ex[16 + 2 * t:18 + 2 * t]
        uses += [("x2T", 0)]
        for t in range(TT):
            uses += [("x2T", t + 1)] if t + 1 < TT else []
            uses += [("L2", t)]
            uses += [("x3T", t - 1)] if t else []
        uses += [("x3T", TT - 1)]
        pos_of = {u: i for i, u in enumerate(uses)}
        splits = [u for u in uses if u[0] in ("W1T", "x1T", "x3T")]
        split_no = {u: i + 1 for i, u in enumerate(splits)}

        def drained(u):
            kind, i = u
            if kind in ("L0", "L1", "L2"):
                return x_new, TT * int(kind[1]) + i + 1
            if u in split_no:
                return split_lo, split_no[u]
            if kind == "W2T":
                return (w2_dve if i % 2 else w2_act), i // 2 + 1
            return {"BwT": bw_ready, "low": low_ready, "lowT": lowt_ready, "x2T": x2m_ready}[kind], i + 1

        def states(engine, first):
            return nc.values_load_multi_w_load_instructions(idx[0:1, 0, first:first + B // 2], engines=[engine], min_val=0,
                                                            max_val=NS0 - 1,
                                                            skip_runtime_bounds_check_because="conditions are states")[1]

        def load_w0(eng, half, states):
            for i, s in enumerate(states):
                b = half * (B // 2) + i
                t, r = b // BT, slice((b % BT) * S, (b % BT + 1) * S)
                eng.dma_start(w0[r, t, r], inp["L0_cond_weights"][bass.ds(s, 1)].rearrange("a c d -> (a c) d")).then_inc(w0_in[half], 16)

        with nc.Block() as block:

            @block.sync
            def _(sp):
                def load_w2(e):
                    sp.dma_start(w2n[:, e % 2], inp["L2_cond_weight"][e].rearrange("(o p) i -> p o i", p=P)).then_inc(w2_in[e % 2], 16)

                sp.dma_start(idx[:, 0, :], inp["itok_B_0_15"].rearrange("(a b) -> a b", a=1)).then_inc(idx_in, 16)
                sp.dma_start(idx[:, 1, :], inp["itok_B_3_7"].rearrange("(a b) -> a b", a=1)).then_inc(idx_in, 16)
                sp.dma_start(w1n[:], inp["L1_cond_W"].rearrange("(o p) i -> p o i", p=P)).then_inc(w1_in, 16)
                x_rows = inp["x"].rearrange("(t b) c h -> (b c) t h", b=BT)
                for i in range(2):
                    half = slice(i * TT // 2, (i + 1) * TT // 2)
                    sp.dma_start(x[:, half], x_rows[:, half]).then_inc(x_in[i], 16)
                load_w2(0)
                sp.dma_start(bw_n[:], inp["L1_cond_lora_B_w"].rearrange("(o p) r -> p o r", p=P)).then_inc(bw_in, 16)
                sp.wait_ge(idx_in, 32)
                sp.wait_ge(w0_zero, 1)
                load_w0(sp, 1, states(mybir.EngineType.SP, B // 2))
                for l in range(NL):
                    sp.dma_start(a_n[:, :, l * R:(l + 1) * R],
                                 inp["L1_cond_lora_A"][l].rearrange("(k p) r -> p k r", p=P)).then_inc(small_in, 16)
                sp.dma_start(lab_i[:], inp["itok_B_0_2"].partition_broadcast(P)).then_inc(small_in, 16)
                load_w2(1)
                sp.wait_ge(written, pos_of[("W1T", KC - 1)] + 1)
                sp.dma_start(inv[:], inp["rope_inv_freq"].partition_broadcast(P)).then_inc(rope_in, 16)
                sp.dma_start(nw[:, 0, :], inp["L3_cond_q_norm_w"].partition_broadcast(P)).then_inc(rope_in, 16)
                sp.dma_start(nw[:, 1, :], inp["L3_cond_k_norm_w"].partition_broadcast(P)).then_inc(rope_in, 16)
                sp.dma_start(len_i[:], inp["itok_B_207_1644"].partition_broadcast(P)).then_inc(rope_in, 16)
                for e in range(2, NE):
                    sp.wait_ge(written, pos_of[("W2T", (e - 2) * KC + KC - 1)] + 1)
                    load_w2(e)
                sp.wait_ge(written, pos_of[ex[-1]] + 1)
                load_head(sp, inp, 0, w2n[:].rearrange("p e k h -> p (e k) h")[:, 0:WE // P, :], w_in)
                for t in range(TT):
                    sp.wait_ge(x_new, 2 * TT + t + 1)
                    sp.dma_start(x3_d[t], x[:, t, :]).then_inc(x3_out, 16)
                sp.wait_ge(x3_out, 16 * TT)
                sp.wait_ge(w_in, 48)

            @block.gpsimd
            def _(pool):
                nc.gpsimd.memset(w0, 0.0).then_inc(w0_zero, 1)
                nc.gpsimd.memset(ident[:], 0.0).then_inc(ident_made, 1)
                pool.wait_ge(ident_made, 1)
                nc.gpsimd.affine_select(out=ident[:], in_=ident[:], compare_op=ALU.not_equal, fill=1.0, base=0,
                                        pattern=[[-1, P]], channel_multiplier=1).then_inc(ident_made, 1)
                nc.gpsimd.memset(x2m[:], 0.0).then_inc(x2m_zero, 1)
                nc.gpsimd.iota(pos_i[:], pattern=[[0, 1]], base=0, channel_multiplier=1).then_inc(rope_no, 1)
                nc.gpsimd.iota(lab_of[:], pattern=[[1, NL], [0, R]], base=0, channel_multiplier=0,
                               allow_small_or_imprecise_dtypes=True).then_inc(lab_numbered, 1)

                g = nc.gpsimd
                pool.wait_ge(trig_done, 2)
                pool.wait_ge(x_new, 2 * TT)
                sin, cos = trig
                lo, hi = slice(0, HALF), slice(HALF, D)

                def table(i, half, values, weights):
                    w = weights.rearrange("p (a d) -> p a d", a=1).broadcast_to([P, TT, HALF])
                    g.tensor_tensor(tabs[:, i, :, half], values, w, ALU.mult)

                for i in range(2):
                    table(2 * i, lo, cos, nw[:, i, lo])
                    table(2 * i, hi, cos, nw[:, i, hi])
                    table(2 * i + 1, lo, sin, nw_neg[:, i, hi])
                    table(2 * i + 1, hi, sin, nw[:, i, lo])

            @block.tensor
            def _(pe):
                def end(u, ins):
                    ins.then_inc(written, 1)

                pe.wait_ge(ident_made, 2)
                for n, u in enumerate(uses):
                    kind, i = u
                    bank = ps[n % 8]
                    if n >= 8:
                        pe.wait_ge(*drained(uses[n - 8]))
                    if kind == "L0":
                        if i % (TT // 2) == 0:
                            pe.wait_ge(x_in[i // (TT // 2)], 16)
                            pe.wait_ge(w0_in[i // (TT // 2)], 16 * B // 2)
                        end(u, pe.matmul(bank[:], w0[:, i, :], x[:, i, :], start=True, stop=True))
                    elif kind == "W1T":
                        pe.wait_ge(w1_in, 16)
                        for o in range(KC):
                            t = pe.transpose(bank[:, o * P:(o + 1) * P], w1n[:, o, i * P:(i + 1) * P], ident[:])
                        end(u, t)
                    elif kind == "BwT":
                        pe.wait_ge(bw_rep, 1)
                        for o in range(KC):
                            src = bw_r[:, o, 0:P] if i == 0 else bw_r[:, o, P:LR]
                            t = pe.transpose(bank[0:src.shape[1], o * P:(o + 1) * P], src, ident[:])
                        end(u, t)
                    elif kind in ("x1T", "x2T", "x3T"):
                        pe.wait_ge(x_new, TT * (int(kind[1]) - 1) + i + 1)
                        for k in range(KC):
                            t = pe.transpose(bank[:, k * P:(k + 1) * P], x[:, i, k * P:(k + 1) * P], ident[:])
                        end(u, t)
                    elif kind == "low":
                        if i == 0:
                            pe.wait_ge(a_split, 2)
                        pe.wait_ge(split_lo, split_no[("x1T", i)])
                        tok = slice(i * P, (i + 1) * P)
                        for k in range(KC):
                            t = three_pass(pe, bank[:, 0:LR], xT_hi[:, k, tok], xT_lo[:, k, tok], a_hi[:, k, :], a_lo[:, k, :],
                                           k == 0, k == KC - 1)
                        end(u, t)
                    elif kind == "lowT":
                        pe.wait_ge(low_ready, i + 1)
                        pe.transpose(bank[:, 0:P], low[:, i, 0:P], ident[:])
                        end(u, pe.transpose(bank[0:R, P:2 * P], low[:, i, P:LR], ident[:]))
                    elif kind == "W2T":
                        e, k = divmod(i, KC)
                        pe.wait_ge(w2_in[e % 2], 16 * (e // 2 + 1))
                        for o in range(KC):
                            t = pe.transpose(bank[:, o * P:(o + 1) * P], w2n[:, e % 2, o, k * P:(k + 1) * P], ident[:])
                        end(u, t)
                    elif kind == "L1":
                        pe.wait_ge(split_lo, max(split_no[("x1T", i)], split_no[("W1T", KC - 1)]))
                        pe.wait_ge(lowt_ready, i + 1)
                        pe.wait_ge(bw_ready, 2)
                        tok = slice(i * P, (i + 1) * P)
                        for k in range(KC):
                            three_pass(pe, bank[:], xT_hi[:, k, tok], xT_lo[:, k, tok], w1_hi[:, k, :], w1_lo[:, k, :],
                                       k == 0, False)
                        pe.matmul(bank[:], low_t[:, i, 0:P], bw_t[:, 0, :], start=False, stop=False)
                        end(u, pe.matmul(bank[:], low_t[0:R, i, P:2 * P], bw_t[0:R, 1, :], start=False, stop=True))
                    elif kind == "L2":
                        if i == 0:
                            pe.wait_ge(idx_in, 32)
                            pe.wait_ge(w2_act, NE * KC // 2)
                            pe.wait_ge(w2_dve, NE * KC // 2)
                        pe.wait_ge(x2m_ready, i + 1)
                        for b in range(BT):
                            e = pe.value_load(idx[0:1, 1, i * BT + b:i * BT + b + 1], min_val=0, max_val=NE - 1)
                            for k in range(KC):
                                t = pe.matmul(bank[:], x2m[:, i % 2, k, b * P:(b + 1) * P],
                                              w2t[:, bass.ds(e, 1), k, :].rearrange("p a o -> p (a o)"),
                                              start=(b == 0 and k == 0), stop=(b == BT - 1 and k == KC - 1))
                        end(u, t)

            @block.scalar
            def _(act):
                act.wait_ge(idx_in, 32)
                act.wait_ge(w0_zero, 1)
                load_w0(act, 0, states(mybir.EngineType.Activation, 0))

                for i, u in enumerate(uses):
                    bank, kind, j = ps[i % 8], *u
                    if u == ("L2", 0):
                        act.wait_ge(reduced, 2)
                        for angles in trig:
                            act.activation(angles, angles, ACT.Sin).then_inc(trig_done, 1)
                    if u in split_no:
                        act.wait_ge(written, i + 1)
                        if kind == "W1T":
                            dst = w1_hi[:, j, :]
                            src = bank[:]
                        else:
                            if kind == "x3T" and j == 0:
                                act.wait_ge(x_new, 2 * TT)
                            dst = xT_hi[:, :, j * P:(j + 1) * P]
                            src = bank[:].rearrange("p (k t) -> p k t", k=KC)
                        act.activation(dst, src, ACT.Copy).then_inc(split_hi, 1)
                    elif kind == "BwT":
                        act.wait_ge(written, i + 1)
                        rows = P if j == 0 else R
                        act.activation(bw_t[0:rows, j, :], bank[0:rows, :], ACT.Copy).then_inc(bw_ready, 1)
                    elif kind == "W2T" and j % 2 == 0:
                        act.wait_ge(written, i + 1)
                        act.activation(w2t[:, j // KC, j % KC, :], bank[:], ACT.Copy).then_inc(w2_act, 1)

            @block.vector
            def _(dve):
                v = nc.vector
                n = [0]

                def link(ins):
                    ins.then_inc(prep, 1)
                    n[0] += 1
                    dve.wait_ge(prep, n[0])

                dve.wait_ge(bw_in, 16)
                for l in range(NL):
                    t = v.tensor_scalar(bw_r[:, :, l * R:(l + 1) * R], bw_n[:], 0.5, None, ALU.mult)
                t.then_inc(bw_rep, 1)

                def labels():
                    dve.wait_ge(small_in, 16 * (NL + 1))
                    v.tensor_copy(a_hi[:], a_n[:]).then_inc(a_split, 1)
                    for b in range(BT):
                        r = slice(b * S, (b + 1) * S)
                        t = v.tensor_copy(lab[r, :], lab_i[r, :].rearrange("p (t b) -> p t b", b=BT)[:, :, b])
                    t.then_inc(lab_ready, 1)
                    dve.wait_ge(a_split, 1)
                    v.tensor_tensor(a_lo[:], a_n[:], f32(a_hi[:]), ALU.subtract).then_inc(a_split, 1)

                def angles():
                    dve.wait_ge(written, pos_of[("lowT", TT - 1)] + 1)
                    dve.wait_ge(rope_no, 1)
                    link(v.tensor_scalar(row_i[:], pos_i[:], S - 1, None, ALU.bitwise_and))
                    link(v.tensor_copy(base[:], row_i[:]))
                    dve.wait_ge(rope_in, 16 * 4)
                    for b in range(BT):
                        r = slice(b * S, (b + 1) * S)
                        link(v.tensor_copy(pos[r, :], len_i[r, :].rearrange("p (t b) -> p t b", b=BT)[:, :, b]))
                    link(v.tensor_scalar(pos[:], pos[:], base[:, 0:1], None, ALU.add))
                    for t in range(TT):
                        v.tensor_scalar(angle[:, t, :], inv[:], pos[:, t:t + 1], None, ALU.mult)
                    v.tensor_scalar(nw[:, 0, :], nw[:, 0, :], -SCALE * float(np.sqrt(D)), None, ALU.mult)
                    link(v.tensor_scalar(nw[:, 1, :], nw[:, 1, :], float(np.sqrt(D)), None, ALU.mult))
                    link(v.tensor_scalar(nw_neg, nw, -1.0, None, ALU.mult))

                def reduce(k, quarter, phase):
                    red = trig[k]
                    link(v.tensor_scalar(turns, angle, float(1.0 / (2.0 * np.pi)), quarter, ALU.mult, ALU.add))
                    link(v.tensor_scalar(turns, turns, MAGIC, None, ALU.add))
                    link(v.tensor_scalar(turns, turns, MAGIC, None, ALU.subtract))
                    link(v.scalar_tensor_tensor(red, turns, -TWO_PI_HI, angle, ALU.mult, ALU.add))
                    link(v.scalar_tensor_tensor(red, turns, -TWO_PI_LO, red, ALU.mult, ALU.add))
                    link(v.tensor_scalar(red, red, float(phase), PI_IN, ALU.add, ALU.min))
                    v.tensor_scalar(red, red, -PI_IN, None, ALU.max).then_inc(reduced, 1)

                dve.wait_ge(x_in[0], 16)
                dve.wait_ge(x_in[1], 16)
                for i, u in enumerate(uses):
                    bank, kind, j = ps[i % 8], *u
                    if u == ("x1T", 0):
                        labels()
                    if u == ("L1", 1):
                        angles()
                    if u == ("L1", 3):
                        reduce(0, 0.0, 0.0)
                    if u == ("L1", 5):
                        reduce(1, 0.25, 0.5 * np.pi)
                    if kind in ("L0", "L1", "L2"):
                        dve.wait_ge(written, i + 1)
                        if int(kind[1]):
                            dve.wait_ge(x_new, TT * int(kind[1]))
                        v.tensor_tensor(x[:, j, :], x[:, j, :], bank[:], ALU.add).then_inc(x_new, 1)
                    elif u in split_no:
                        dve.wait_ge(split_hi, split_no[u])
                        if kind == "W1T":
                            lo, hi, src = w1_lo[:, j, :], w1_hi[:, j, :], bank[:]
                        else:
                            t = slice(j * P, (j + 1) * P)
                            lo, hi, src = xT_lo[:, :, t], xT_hi[:, :, t], bank[:].rearrange("p (k t) -> p k t", k=KC)
                        v.tensor_tensor(lo, src, f32(hi), ALU.subtract).then_inc(split_lo, 1)
                    elif kind == "low":
                        dve.wait_ge(written, i + 1)
                        dve.wait_ge(lab_ready, 1)
                        dve.wait_ge(lab_numbered, 1)
                        v.scalar_tensor_tensor(low[:, j, :], lab_of[:], lab[:, j:j + 1], bank[:, 0:LR],
                                               ALU.is_equal, ALU.mult).then_inc(low_ready, 1)
                    elif kind == "lowT":
                        dve.wait_ge(written, i + 1)
                        v.tensor_copy(low_t[:, j, 0:P], bank[:, 0:P])
                        v.tensor_copy(low_t[0:R, j, P:2 * P], bank[0:R, P:2 * P]).then_inc(lowt_ready, 1)
                    elif kind == "W2T" and j % 2 == 1:
                        dve.wait_ge(written, i + 1)
                        v.tensor_copy(w2t[:, j // KC, j % KC, :], bank[:]).then_inc(w2_dve, 1)
                    elif kind == "x2T":
                        dve.wait_ge(written, i + 1)
                        if j >= 2:
                            dve.wait_ge(written, pos_of[("L2", j - 2)] + 1)
                        dve.wait_ge(x2m_zero, 1)
                        for k in range(KC):
                            dst = x2m[:, j % 2, k, :].rearrange("p (b c) -> p b c", c=P + S)[:, :, 0:S]
                            t = v.tensor_copy(dst, bank[:, k * P:(k + 1) * P].rearrange("p (b c) -> p b c", c=S))
                        t.then_inc(x2m_ready, 1)


def stage_project(nc, inp, ident, xT_hi, xT_lo, tabs, wn0, w_in0, table, q_d, k_d, v_d, kt_d):
    N = HK * TT
    with ExitStack() as ctx:
        m = Bench(nc, ctx, "prj")
        wn = [wn0[:].rearrange("p e k h -> p (e k) h"), m.sb("wn1", [P, WE // P, H])]
        wt_hi = [m.sb(f"wt_hi{i}", [P, KC, WE], F32R) for i in range(2)]
        wt_lo = [m.sb(f"wt_lo{i}", [P, KC, WE], F32R) for i in range(2)]
        kn = [m.sb(f"kn{i}", [P, HK * D]) for i in range(2)]
        kst = [m.sb(f"kst{i}", [P, PPT, HK, PS]) for i in range(2)]
        sq = [m.sb(f"sq{i}", [P, QK]) for i in range(2)]
        ta = [m.sb(f"ta{i}", [P, QK]) for i in range(2)]
        tb = [m.sb(f"tb{i}", [P, QK]) for i in range(2)]
        qn = [m.sb(f"qn{i}", [P, QK]) for i in range(2)]
        ss = [m.sb(f"ss{i}", [P, REP + 1]) for i in range(2)]
        rs = [m.sb(f"rs{i}", [P, REP + 1]) for i in range(2)]
        rstd = [m.sb(f"rstd{i}", [P, REP + 1]) for i in range(2)]
        power = m.sb("power", [P, REP + 1])
        floor = m.sb("floor", [P, REP + 1])
        qst = [m.sb(f"qst{i}", [P, BT, ST]) for i in range(2)]
        vst = [m.sb(f"vst{i}", [P, D]) for i in range(4)]
        ps = [m.psum(f"ps{i}", [P, 2 * BANK]) for i in range(2)]
        pt = m.psum("pt", [P, 2 * BANK])
        pw = m.psum("pw", [P, 2, BANK])

        w_in = [w_in0, m.sem("w_in1")]
        kn_in = [m.sem(f"kn_in{i}") for i in range(2)]
        job_t = m.sem("job_t")
        job_act = m.sem("job_act")
        job_dve = m.sem("job_dve")
        mm_done = m.sem("mm_done")
        q_squared = m.sem("q_squared")
        squared = m.sem("squared")
        k_roped = m.sem("k_roped")
        v_staged = m.sem("v_staged")
        roped = m.sem("roped")
        reduced = m.sem("reduced")
        normed = m.sem("normed")
        pool_step = m.sem("pool_step")
        turned = m.sem("turned")
        q_staged = m.sem("q_staged")
        stage_free = m.sem("stage_free")
        kst_free = m.sem("kst_free")
        ids_in = m.sem("ids_in")
        stored = m.sem("stored")
        k_stored = m.sem("k_stored")

        cq, sn_q, ck, sn_k = (tabs[:, i] for i in range(4))
        k_rows = inp["L3_cond_k_cache"].rearrange("a s h d -> (a s) (h d)")

        WJ = KC + 2
        UNROLL = 2 * TT

        def job_of(c, g, last_head):
            return WJ + c * (WJ + 2) + g - (WJ if last_head else 0)

        def loop(eng, body):
            last = HK // 2 - 1
            with eng.Fori(0, last) as it:
                for j in range(UNROLL):
                    body(it, j, False)
            for j in range(UNROLL):
                body(last, j, True)

        with nc.Block() as block:

            @block.sync
            def _(sp):
                def load_w(c, slot):
                    load_head(sp, inp, c, wn[slot], w_in[slot])

                def load_k(t, slot):
                    src = k_rows.rearrange("(t p) c -> t p c", p=P)[bass.ds(t, 1)]
                    sp.dma_start(kn[slot][:], src.rearrange("a p c -> (a p) c")).then_inc(kn_in[slot], 16)

                sp.sem_inc(stage_free, 2)
                sp.sem_inc(kst_free, 2)
                load_w(1, 1)
                load_k(0, 0)
                load_k(1, 1)
                sp.dma_start(table[:], inp["itok_Bx16_0_63"].rearrange("(a b) j -> a (b j)", a=1)).then_inc(ids_in, 16)
                sp.wait_ge(ids_in, 16)

                def body(it, j, tail):
                    n, c, t, slot = it * UNROLL + j, it * 2 + j // TT, j % TT, j // TT
                    if t == 0 and not tail:
                        sp.wait_ge(job_t, job_of(c, 0, False))
                        load_w(c + 2, slot)
                    sp.wait_ge(q_staged, n + 3)
                    tile = slice(t * BT, (t + 1) * BT)
                    sp.dma_start(q_d[tile, bass.ds(c, 1)].rearrange("b a d x -> d (b a) x"),
                                 qst[j % 2][:, :, 0:QS]).then_inc(stored, 16)
                    sp.dma_start(k_d[tile, :, bass.ds(c * S, S)].rearrange("b d x -> d b x"),
                                 qst[j % 2][:, :, QS:ST]).then_inc(stored, 16)
                    sp.wait_ge(v_staged, n + 1)
                    sp.dma_start(v_d[t, :, bass.ds(c * D, D)], vst[j % 4][:]).then_inc(stored, 16)
                    sp.wait_ge(stored, (n + 1) * 48)
                    sp.sem_inc(stage_free, 1)
                    if t >= TT - 2:
                        u = t % 2
                        k = c * 2 + u
                        last_head = tail and slot == 1
                        sp.wait_ge(job_act, job_of(c, WJ + u, last_head) + 1)
                        sp.wait_ge(job_dve, job_of(c, WJ + u, last_head) + 1)
                        dst = kt_d[bass.ds(k * PPT, PPT)].rearrange("g d x -> d g x")
                        sp.dma_start(dst, kst[u][:].rearrange("p g h t -> p g (h t)")).then_inc(k_stored, 16)
                        if not last_head:
                            load_k(k + 2, u)
                        sp.wait_ge(k_stored, (k + 1) * 16)
                        sp.sem_inc(kst_free, 1)

                loop(sp, body)

            @block.tensor
            def _(pe):
                def weight_job(g, slot):
                    for i in range(4):
                        k, o = (g, i) if g < KC else ((g - KC) * 2 + i // 2, REP + i % 2)
                        t = pe.transpose(pw[:, g % 2, i * P:(i + 1) * P], wn[slot][:, o, k * P:(k + 1) * P], ident[:])
                    t.then_inc(job_t, 1)

                def cache_job(slot):
                    for h in range(HK):
                        o = pw[:, h // 4, (h % 4) * P:(h % 4 + 1) * P]
                        t = pe.transpose(o, kn[slot][:, h * D:(h + 1) * D], ident[:])
                    t.then_inc(job_t, 1)

                def multiply(j):
                    t, slot = j % TT, j // TT % 2
                    tok = slice(t * P, (t + 1) * P)
                    for out, cols in ((ps[j % 2][:, 0:QW], slice(0, QW)), (ps[j % 2][:, QW:WE], slice(QW, WE))):
                        for k in range(KC):
                            last = three_pass(pe, out, xT_hi[:, k, tok], xT_lo[:, k, tok], wt_hi[slot][:, k, cols],
                                              wt_lo[slot][:, k, cols], k == 0, k == KC - 1)
                    last.then_inc(mm_done, 1)

                pe.wait_ge(w_in[0], 48)
                for g in range(WJ):
                    if g >= 2:
                        pe.wait_ge(job_dve, g - 1)
                    weight_job(g, 0)
                pe.wait_ge(job_dve, WJ)
                multiply(0)
                multiply(1)

                def body(it, j, tail):
                    n, c, t, slot = it * UNROLL + j, it * 2 + j // TT, j % TT, j // TT
                    last_head = tail and slot == 1
                    if t >= WJ or not last_head:
                        pe.wait_ge(job_dve, job_of(c, t, last_head))
                        pe.wait_ge(job_act, job_of(c, t, last_head))
                        if t == 0:
                            pe.wait_ge(w_in[1 - slot], (it + 1 + slot) * 48)
                        if t < WJ:
                            weight_job(t, 1 - slot)
                        else:
                            pe.wait_ge(kn_in[t % 2], (c + 1) * 16)
                            cache_job(t % 2)
                    if not (tail and j >= UNROLL - 2):
                        pe.wait_ge(roped, n + 1)
                        pe.wait_ge(v_staged, n + 1)
                        multiply(j + 2)
                    pe.wait_ge(normed, n + 1)
                    pe.wait_ge(q_staged, n + 2)
                    for h in range(REP + 1):
                        o = pt[:, h * P:(h + 1) * P]
                        last = pe.transpose(o, qn[j % 2][:, h * P:(h + 1) * P], ident[:])
                    last.then_inc(turned, 1)

                loop(pe, body)

            def split_of(g, slot):
                if g < KC:
                    return wt_hi[slot][:, g, 0:QW], wt_lo[slot][:, g, 0:QW], pw[:, g, :] if g < 2 else pw[:, g % 2, :]
                k = slice((g - KC) * 2, (g - KC) * 2 + 2)
                return (wt_hi[slot][:, k, QW:WE], wt_lo[slot][:, k, QW:WE],
                        pw[:, g % 2, :].rearrange("p (k c) -> p k c", k=2))

            def keys_of(half, slot):
                return (kst[slot][:, :, half * 4:half * 4 + 4, :].rearrange("p g h t -> p h g t"),
                        pw[:, half, :].rearrange("p (h g t) -> p h g t", h=4, g=PPT))

            @block.scalar
            def _(act):
                act.sem_inc(q_staged, 2)
                for g in range(WJ):
                    hi, _, bank = split_of(g, 0)
                    act.wait_ge(job_t, g + 1)
                    act.activation(hi, bank, ACT.Copy).then_inc(job_act, 1)

                def squares(j, n):
                    act.wait_ge(mm_done, n + 1)
                    if not isinstance(n, int) or n >= 2:
                        act.wait_ge(reduced, n - 1)
                    act.activation(sq[j % 2][:, 0:QW], ps[j % 2][:, 0:QW], ACT.Square).then_inc(q_squared, 1)
                    act.wait_ge(k_roped, n + 1)
                    act.activation(sq[j % 2][:, QW:QK], ps[j % 2][:, QW:QK], ACT.Square).then_inc(squared, 1)
                    if not isinstance(n, int) or n >= 4:
                        act.wait_ge(stage_free, n - 1)
                    act.activation(vst[j % 4][:], ps[j % 2][:, QK:WE], ACT.Copy).then_inc(v_staged, 1)

                squares(0, 0)
                squares(1, 1)

                def body(it, j, tail):
                    n, c, t, slot = it * UNROLL + j, it * 2 + j // TT, j % TT, j // TT
                    last_head = tail and slot == 1
                    if t >= WJ or not last_head:
                        act.wait_ge(job_t, job_of(c, t, last_head) + 1)
                        if t < WJ:
                            hi, _, bank = split_of(t, 1 - slot)
                            act.activation(hi, bank, ACT.Copy).then_inc(job_act, 1)
                        else:
                            act.wait_ge(kst_free, c * 2 + t % 2 + 1)
                            dst, bank = keys_of(0, t % 2)
                            act.activation(dst, bank, ACT.Copy).then_inc(job_act, 1)
                    if not (tail and j >= UNROLL - 2):
                        squares(j + 2, n + 2)
                    act.wait_ge(turned, n + 1)
                    act.wait_ge(stage_free, n + 1)
                    q_src = pt[:, 0:QW].rearrange("p (h b t) -> p b h t", h=REP, b=BT)
                    k_src = pt[:, QW:QK].rearrange("p (b t) -> p b t", b=BT)
                    act.activation(qst[j % 2][:, :, 0:QS].rearrange("p b (h t) -> p b h t", h=REP), q_src, ACT.Copy)
                    act.activation(qst[j % 2][:, :, QS:ST], k_src, ACT.Copy).then_inc(q_staged, 1)

                loop(act, body)

            @block.vector
            def _(dve):
                v = nc.vector
                for g in range(WJ):
                    hi, lo, bank = split_of(g, 0)
                    dve.wait_ge(job_act, g + 1)
                    v.tensor_tensor(lo, bank, f32(hi), ALU.subtract).then_inc(job_dve, 1)

                def rope(j, n):
                    t, s = j % TT, j % 2
                    dve.wait_ge(mm_done, n + 1)
                    if not isinstance(n, int) or n >= 2:
                        dve.wait_ge(normed, n - 1)
                    q = ps[s][:, 0:QW].rearrange("p (h d) -> p h d", h=REP)
                    a = ta[s][:, 0:QW].rearrange("p (h d) -> p h d", h=REP)
                    b = tb[s][:, 0:QW].rearrange("p (h d) -> p h d", h=REP)
                    lo, hi = slice(0, HALF), slice(HALF, D)
                    k = ps[s][:, QW:QK]
                    v.tensor_tensor(ta[s][:, QW:QK], k, ck[:, t, :], ALU.mult)
                    v.tensor_tensor(tb[s][:, QW:QW + HALF], k[:, hi], sn_k[:, t, lo], ALU.mult)
                    v.tensor_tensor(tb[s][:, QW + HALF:QK], k[:, lo], sn_k[:, t, hi], ALU.mult).then_inc(k_roped, 1)
                    dve.wait_ge(q_squared, n + 1)
                    v.tensor_tensor(a, q, cq[:, t:t + 1, :].broadcast_to([P, REP, D]), ALU.mult)
                    v.tensor_tensor(b[:, :, lo], q[:, :, hi], sn_q[:, t:t + 1, lo].broadcast_to([P, REP, HALF]), ALU.mult)
                    v.tensor_tensor(b[:, :, hi], q[:, :, lo], sn_q[:, t:t + 1, hi].broadcast_to([P, REP, HALF]), ALU.mult).then_inc(roped, 1)
                    dve.wait_ge(squared, n + 1)
                    v.tensor_reduce(ss[s][:], sq[s][:].rearrange("p (h d) -> p h d", h=REP + 1), AX_X, ALU.add).then_inc(reduced, 1)

                rope(0, 0)
                rope(1, 1)

                def body(it, j, tail):
                    n, c, t, slot = it * UNROLL + j, it * 2 + j // TT, j % TT, j // TT
                    last_head = tail and slot == 1
                    if t >= WJ or not last_head:
                        if t < WJ:
                            hi, lo, bank = split_of(t, 1 - slot)
                            dve.wait_ge(job_act, job_of(c, t, last_head) + 1)
                            v.tensor_tensor(lo, bank, f32(hi), ALU.subtract).then_inc(job_dve, 1)
                        else:
                            dve.wait_ge(job_t, job_of(c, t, last_head) + 1)
                            dve.wait_ge(kst_free, c * 2 + t % 2 + 1)
                            dst, bank = keys_of(1, t % 2)
                            v.tensor_copy(dst, bank).then_inc(job_dve, 1)
                    if not (tail and j >= UNROLL - 2):
                        rope(j + 2, n + 2)

                loop(dve, body)

            @block.gpsimd
            def _(pool):
                g = nc.gpsimd
                g.memset(power[:], -0.5)
                g.memset(floor[:], D * EPS).then_inc(pool_step, 1)
                pool.wait_ge(pool_step, 1)

                def body(it, j, tail):
                    n, s = it * UNROLL + j, j % 2
                    pool.wait_ge(roped, n + 1)
                    g.tensor_tensor(ta[s][:], ta[s][:], tb[s][:], ALU.add).then_inc(pool_step, 1)
                    pool.wait_ge(reduced, n + 1)
                    pool.wait_ge(q_staged, n + 1)
                    g.tensor_tensor(rs[s][:], ss[s][:], floor[:], ALU.add).then_inc(pool_step, 1)
                    pool.wait_ge(pool_step, n * 3 + 3)
                    g.tensor_tensor(rstd[s][:], rs[s][:], power[:], ALU.pow).then_inc(pool_step, 1)
                    pool.wait_ge(pool_step, n * 3 + 4)
                    r = rstd[s][:].rearrange("p (h a) -> p h a", a=1).broadcast_to([P, REP + 1, D])
                    rows = lambda x: x[s][:].rearrange("p (h d) -> p h d", h=REP + 1)
                    g.tensor_tensor(rows(qn), rows(ta), r, ALU.mult).then_inc(normed, 1)

                loop(pool, body)


SL = 8


def load_wo(eng, inp, s, tile, sem):
    w = HQ * D // SL
    eng.dma_start(tile[:], inp["L3_cond_Wo"][:, s * w:(s + 1) * w].rearrange("(o p) e -> p o e", p=P)).then_inc(sem, 16)


def stage_attend(nc, inp, ident, table, len_i, wo, wo_in, q_d, k_d, v_d, kt_d, o_d):
    GROUP = 4
    UNROLL = 2 * HK
    N = B * HK
    AHEAD = 4
    SPLITS = 4
    POOL_PAGES = 6
    EARLY = 7
    with ExitStack() as ctx:
        m = Bench(nc, ctx, "att")
        PG = NPP + 1
        PA = (PG + 1) // 2
        KA, KB = PA * PS, (PG - PA) * PS
        PAD = 2 * KA
        kT = [m.sb(f"kT{i}", [P, PG, HK, PS]) for i in range(2)]
        k_hi = [m.sb(f"k_hi{i}", [P, PG, PS], F32R) for i in range(SPLITS)]
        k_lo = [m.sb(f"k_lo{i}", [P, PG, PS], F32R) for i in range(SPLITS)]
        q_hi = [m.sb(f"q_hi{i}", [P, QS], F32R) for i in range(SPLITS)]
        q_lo = [m.sb(f"q_lo{i}", [P, QS], F32R) for i in range(SPLITS)]
        vc = [m.sb(f"vc{i}", [P, NCH, HK * D]) for i in range(2)]
        q = [m.sb(f"q{i}", [P, HK, QS]) for i in range(2)]
        vn = [m.sb(f"vn{i}", [S, HK * D]) for i in range(2)]
        lens = m.sb("lens", [P, B])
        key_no = m.sb("key_no", [P, PAD])
        mask = [m.sb(f"mask{i}", [P, PAD]) for i in range(2)]
        neg = [m.sb(f"neg{i}", [P, PAD]) for i in range(2)]
        nmax = [m.sb(f"nmax{i}", [P, 1]) for i in range(2)]
        prob = [m.sb(f"prob{i}", [P, KEYS]) for i in range(2)]
        total = [m.sb(f"total{i}", [P, 1]) for i in range(2)]
        inv = [m.sb(f"inv{i}", [P, 1]) for i in range(2)]
        pT = [m.sb(f"pT{i}", [P, NCH + 1, P]) for i in range(2)]
        ost = [m.sb(f"ost{i}", [P, HK, P]) for i in range(2)]
        ps = [m.psum(f"ps{i}", [P, 2, BANK]) for i in range(2)]
        pa = m.psum("pa", [P, BANK])
        pb = m.psum("pb", [P, BANK])
        po = [m.psum(f"po{i}", [P, BANK]) for i in range(2)]

        NA = 2
        lens_ready = m.sem("lens_ready")
        kq_in = [m.sem(f"kq_in{i}") for i in range(2)]
        v_in = [m.sem(f"v_in{i}") for i in range(2)]
        k_hi_done = m.sem("k_hi_done")
        q_hi_done = m.sem("q_hi_done")
        k_split = m.sem("k_split")
        q_split = m.sem("q_split")
        v_pool_in = [m.sem(f"v_pool_in{i}") for i in range(2)]
        numbered = m.sem("numbered")
        padded = m.sem("padded")
        masked = m.sem("masked")
        may_reduce = m.sem("may_reduce")
        scored = m.sem("scored")
        maxed = m.sem("maxed")
        exped = m.sem("exped")
        inverted = m.sem("inverted")
        normed = m.sem("normed")
        turned_a = m.sem("turned_a")
        turned_b = m.sem("turned_b")
        out_a = m.sem("out_a")
        out_b = m.sem("out_b")
        valued = m.sem("valued")
        o_staged = m.sem("o_staged")
        o_stored = [m.sem(f"o_stored{i}") for i in range(2)]

        def pages_of(b, first, count, engine):
            return nc.values_load_multi_w_load_instructions(table[0:1, bass.ds(b * NPP + first, count)], engines=[engine],
                                                            min_val=0, max_val=PAGES - 1,
                                                            skip_runtime_bounds_check_because=IN_RANGE)[1]

        v_pages = inp["L3_cond_v_cache"].rearrange("g s h d -> g s (h d)")

        def load_keys(eng, b, slot, pages):
            eng.dma_start(q[slot][:], q_d[bass.ds(b, 1)].rearrange("a h d x -> d (a h) x")).then_inc(kq_in[slot], 16)
            eng.dma_start(kT[slot][:, NPP].rearrange("p h t -> p (h t)"),
                          k_d[bass.ds(b, 1)].rearrange("a d x -> (a d) x")).then_inc(kq_in[slot], 16)
            for j, page in enumerate(pages):
                eng.dma_start(kT[slot][:, j].rearrange("p h t -> p (h t)"),
                              kt_d[bass.ds(page, 1)].rearrange("a d x -> (a d) x")).then_inc(kq_in[slot], 16)

        def load_page(eng, slot, j, page, sem):
            r = slice(j % PPT * PS, (j % PPT + 1) * PS)
            eng.dma_start(vc[slot][r, j // PPT, :], v_pages[bass.ds(page, 1)].rearrange("a s c -> (a s) c")).then_inc(sem, 16)

        def load_values(eng, b, slot, pages):
            eng.dma_start(vn[slot][:], v_d[bass.ds(b, 1)].rearrange("a s c -> (a s) c")).then_inc(v_in[slot], 16)
            for j in range(NPP - POOL_PAGES):
                load_page(eng, slot, j, pages[j], v_in[slot])

        with nc.Block() as block:

            @block.sync
            def _(sp):
                for slot in range(2):
                    sp.sem_inc(o_stored[slot], 16)

                for slot in range(2):
                    pages = pages_of(slot, 0, NPP, mybir.EngineType.SP)
                    load_keys(sp, slot, slot, pages)
                load_values(sp, 1, 1, pages)
                for i in range(2):
                    load_wo(sp, inp, i, wo[i], wo_in[i])

                def body(it, tail):
                    for slot in range(2):
                        b = it * 2 + slot
                        if not tail:
                            pages = pages_of(b + 2, 0, NPP, mybir.EngineType.SP)
                            sp.wait_ge(q_split, (b + 1) * HK)
                            sp.wait_ge(k_split, (b + 1) * HK)
                            load_keys(sp, b + 2, slot, pages)
                            sp.wait_ge(valued, (b + 1) * HK)
                            load_values(sp, b + 2, slot, pages)
                        sp.wait_ge(o_staged, (b + 1) * (HK // GROUP) + 2)
                        sp.dma_start(o_d[bass.ds(b, 1)].rearrange("a d x -> (a d) x"),
                                     ost[slot][:].rearrange("p h x -> p (h x)")).then_inc(o_stored[slot], 16)

                with sp.Fori(0, B // 2 - 1) as it:
                    body(it, False)
                body(B // 2 - 1, True)
                for slot in range(2):
                    sp.wait_ge(o_stored[slot], (B // 2 + 1) * 16)
                    sp.wait_ge(wo_in[slot], 16)

            @block.gpsimd
            def _(pool):
                g = nc.gpsimd
                g.iota(key_no[:, 0:L], pattern=[[1, L]], base=0, channel_multiplier=0,
                       allow_small_or_imprecise_dtypes=True).then_inc(numbered, 1)
                g.memset(key_no[:, L:KEYS], -1.0).then_inc(numbered, 1)
                g.memset(key_no[:, KEYS:PAD], MASKED).then_inc(numbered, 1)
                for i, page in enumerate(pages_of(0, NPP - POOL_PAGES, POOL_PAGES, mybir.EngineType.Pool)):
                    load_page(pool, 0, NPP - POOL_PAGES + i, page, v_pool_in[0])

                def split(j, n):
                    pool.wait_ge(k_hi_done, n + 1)
                    g.tensor_tensor(k_lo[j % SPLITS][:], kT[j // HK % 2][:, :, j % HK, :], f32(k_hi[j % SPLITS][:]),
                                    ALU.subtract).then_inc(k_split, 1)

                def body(it, j, first, tail):
                    split(j, it * UNROLL + j)
                    i = (j % HK + 1) % HK
                    b = j // HK + (i < 1)
                    if i < POOL_PAGES and not (first and b < 1) and not (tail and b >= 2):
                        page, = pages_of(it * 2 + b, NPP - POOL_PAGES + i, 1, mybir.EngineType.Pool)
                        if not (first and b < 2):
                            pool.wait_ge(valued, (it * 2 + b - 1) * HK)
                        load_page(pool, b % 2, NPP - POOL_PAGES + i, page, v_pool_in[b % 2])

                for j in range(UNROLL):
                    body(0, j, True, False)
                with pool.Fori(1, B // 2 - 1) as it:
                    for j in range(UNROLL):
                        body(it, j, False, False)
                for j in range(UNROLL):
                    body(B // 2 - 1, j, False, True)

            @block.tensor
            def _(pe):
                def scores(j, n):
                    i, x = j % 2, j % SPLITS
                    pe.wait_ge(q_split, n + 1)
                    pe.wait_ge(k_split, n + 1)
                    three_pass(pe, ps[i][:, 0, 0:KA], q_hi[x][:], q_lo[x][:], k_hi[x][:, 0:PA, :], k_lo[x][:, 0:PA, :], True, True)
                    three_pass(pe, ps[i][:, 1, 0:KB], q_hi[x][:], q_lo[x][:], k_hi[x][:, PA:PG, :], k_lo[x][:, PA:PG, :],
                               True, True).then_inc(scored, 1)

                def turn(j):
                    p = prob[j % 2]
                    for c in range(NA, NCH):
                        pe.transpose(pb[:, (c - NA) * P:(c - NA + 1) * P], p[:, c * P:(c + 1) * P], ident[:])
                    pe.transpose(pb[0:S, (NCH - NA) * P:(NCH - NA + 1) * P], p[:, L:KEYS], ident[:]).then_inc(turned_b, 1)
                    for c in range(NA):
                        t = pe.transpose(pa[:, c * P:(c + 1) * P], p[:, c * P:(c + 1) * P], ident[:])
                    t.then_inc(turned_a, 1)

                def values(j, n):
                    s, h = j // HK % 2, j % HK
                    cols = slice(h * D, (h + 1) * D)
                    o = po[j // GROUP % 2][:, j % GROUP * P:(j % GROUP + 1) * P]
                    pe.wait_ge(out_b, n + 1)
                    for c in range(NA, NCH):
                        pe.matmul(o, vc[s][:, c, cols], pT[j % 2][:, c, :], start=(c == NA), stop=False)
                    pe.matmul(o, vn[s][:, cols], pT[j % 2][0:S, NCH, :], start=False, stop=False)
                    pe.wait_ge(out_a, n + 1)
                    for c in range(NA):
                        t = pe.matmul(o, vc[s][:, c, cols], pT[j % 2][:, c, :], start=False, stop=(c == NA - 1))
                    t.then_inc(valued, 1)

                pe.wait_ge(padded, 2)
                scores(0, 0)
                scores(1, 1)
                for i in range(2):
                    pe.wait_ge(maxed, i + 1)
                    scores(i + 2, i + 2)
                    pe.wait_ge(normed, i + 1)
                    if i:
                        pe.wait_ge(out_a, i)
                        pe.wait_ge(out_b, i)
                    turn(i)

                def body(it, j, tail):
                    n = it * UNROLL + j
                    b = it * 2 + j // HK
                    if j % GROUP == 0:
                        pe.wait_ge(o_staged, it * (UNROLL // GROUP) + j // GROUP + 1)
                    if j % HK == 0:
                        pe.wait_ge(v_in[j // HK], (it + 1) * (PG - POOL_PAGES) * 16)
                        pe.wait_ge(v_pool_in[j // HK], (it + 1) * POOL_PAGES * 16)
                    values(j, n)
                    if not (tail and j + AHEAD >= UNROLL):
                        pe.wait_ge(maxed, n + 3)
                        scores(j + AHEAD, n + AHEAD)
                    if not (tail and j + 2 >= UNROLL):
                        pe.wait_ge(normed, n + 3)
                        pe.wait_ge(out_a, n + 2)
                        pe.wait_ge(out_b, n + 2)
                        turn(j + 2)

                with pe.Fori(0, B // 2 - 1) as it:
                    for j in range(UNROLL):
                        body(it, j, False)
                for j in range(UNROLL):
                    body(B // 2 - 1, j, True)

            @block.vector
            def _(dve):
                v = nc.vector
                for i in range(2):
                    v.memset(ps[i][:, 1, KB:KA], 0.0).then_inc(padded, 1)
                v.tensor_copy(lens[:], len_i[:]).then_inc(lens_ready, 1)

                def smallest(j):
                    halves = [a.rearrange("p (a k) -> p a k", a=2) for a in (neg[j % 2][:], mask[j // HK % 2][:])]
                    v.tensor_tensor_reduce(halves[0], halves[1], ps[j % 2][:, :, 0:KA], 1.0, 3.0e38,
                                           ALU.add, ALU.min, nmax[j % 2][:]).then_inc(maxed, 1)

                def make_mask(b, slot):
                    v.tensor_scalar(mask[slot][:], key_no[:], lens[:, bass.ds(b, 1)], MASKED, ALU.is_ge, ALU.mult).then_inc(masked, 1)

                def split_q(j, n, it):
                    if not isinstance(n, int) or n >= SPLITS:
                        dve.wait_ge(scored, n - SPLITS + 1)
                    if j % HK == 0:
                        dve.wait_ge(kq_in[j // HK % 2], (it + j // UNROLL + 1) * 16 * (PG + 1))
                    src = q[j // HK % 2][:, j % HK, :]
                    v.tensor_copy(q_hi[j % SPLITS][:], src).then_inc(q_hi_done, 1)
                    dve.wait_ge(q_hi_done, n + 1)
                    v.tensor_tensor(q_lo[j % SPLITS][:], src, f32(q_hi[j % SPLITS][:]), ALU.subtract).then_inc(q_split, 1)

                def minimum(j, n, b):
                    dve.wait_ge(scored, n + 1)
                    if j % HK == 0:
                        dve.wait_ge(masked, b + 1)
                    dve.sem_inc(may_reduce, 1)
                    smallest(j)

                def normalize(j, n):
                    dve.wait_ge(exped, n + 1)
                    v.reciprocal(inv[j % 2][:], total[j % 2][:]).then_inc(inverted, 1)
                    dve.wait_ge(inverted, n + 1)
                    v.tensor_scalar(prob[j % 2][:], prob[j % 2][:], inv[j % 2][:, 0:1], None, ALU.mult).then_inc(normed, 1)

                dve.wait_ge(padded, 2)
                dve.wait_ge(numbered, 3)
                dve.wait_ge(lens_ready, 1)
                make_mask(0, 0)
                make_mask(1, 1)
                def keep(j, n):
                    dve.wait_ge(turned_a, n + 1)
                    v.tensor_copy(pT[j % 2][:, 0:NA, :], pa[:, 0:NA * P].rearrange("p (c q) -> p c q", c=NA)).then_inc(out_a, 1)

                split_q(0, 0, 0)
                split_q(1, 1, 0)
                minimum(0, 0, 0)
                split_q(2, 2, 0)
                split_q(3, 3, 0)
                minimum(1, 1, 0)
                normalize(0, 0)
                keep(0, 0)
                minimum(2, 2, 0)
                normalize(1, 1)
                for i in range(SPLITS, EARLY):
                    split_q(i, i, 0)

                def body(it, j, tail):
                    n = it * UNROLL + j
                    if not (tail and j + 3 >= UNROLL):
                        minimum(j + 3, n + 3, it * 2 + (j + 3) // HK)
                    if not (tail and j + 1 >= UNROLL):
                        keep(j + 1, n + 1)
                    if not (tail and j + 2 >= UNROLL):
                        normalize(j + 2, n + 2)
                    if not (tail and j + EARLY >= UNROLL):
                        split_q(j + EARLY, n + EARLY, it)
                    if not tail and j % HK == HK - 4:
                        dve.wait_ge(maxed, n + 4)
                        make_mask(it * 2 + 2 + j // HK, j // HK)

                with dve.Fori(0, B // 2 - 1) as it:
                    for j in range(UNROLL):
                        body(it, j, False)
                for j in range(UNROLL):
                    body(B // 2 - 1, j, True)

            @block.scalar
            def _(act):
                act.sem_inc(o_staged, 2)
                load_values(act, 0, 0, pages_of(0, 0, NPP, mybir.EngineType.Activation))

                def exps(j, n):
                    if not isinstance(n, int) or n >= 2:
                        act.wait_ge(turned_a, n - 1)
                    act.wait_ge(maxed, n + 1)
                    act.activation(prob[j % 2][:], neg[j % 2][:, 0:KEYS], ACT.Exp, bias=nmax[j % 2][:, 0:1], scale=-1.0,
                                   accum_out=total[j % 2][:]).then_inc(exped, 1)

                def keep(j, n):
                    act.wait_ge(turned_b, n + 1)
                    act.activation(pT[j % 2][:, NA:NCH, :], pb[:, 0:(NCH - NA) * P].rearrange("p (c q) -> p c q", q=P), ACT.Copy)
                    act.activation(pT[j % 2][0:S, NCH, :], pb[0:S, (NCH - NA) * P:(NCH - NA + 1) * P], ACT.Copy).then_inc(out_b, 1)

                def split_k(j, n, it):
                    if not isinstance(n, int) or n >= SPLITS:
                        act.wait_ge(scored, n - SPLITS + 1)
                    if j % HK == 0:
                        act.wait_ge(kq_in[j // HK % 2], (it + j // UNROLL + 1) * 16 * (PG + 1))
                    act.activation(k_hi[j % SPLITS][:], kT[j // HK % 2][:, :, j % HK, :], ACT.Copy).then_inc(k_hi_done, 1)

                split_k(0, 0, 0)
                split_k(1, 1, 0)
                exps(0, 0)
                split_k(2, 2, 0)
                split_k(3, 3, 0)
                exps(1, 1)
                keep(0, 0)
                exps(2, 2)
                for i in range(SPLITS, EARLY):
                    split_k(i, i, 0)

                def body(it, j, tail):
                    n = it * UNROLL + j
                    if not (tail and j + 1 >= UNROLL):
                        keep(j + 1, n + 1)
                    if not (tail and j + 3 >= UNROLL):
                        exps(j + 3, n + 3)
                    if not (tail and j + EARLY >= UNROLL):
                        split_k(j + EARLY, n + EARLY, it)
                    if j % GROUP == GROUP - 1:
                        g = j // GROUP
                        act.wait_ge(valued, n + 1)
                        if g % 2 == 0:
                            act.wait_ge(o_stored[j // HK], (it + 1) * 16)
                        act.activation(ost[j // HK][:, g % 2 * GROUP:(g % 2 + 1) * GROUP, :],
                                       po[g % 2][:].rearrange("p (h q) -> p h q", h=GROUP), ACT.Copy).then_inc(o_staged, 1)

                with act.Fori(0, B // 2 - 1) as it:
                    for j in range(UNROLL):
                        body(it, j, False)
                for j in range(UNROLL):
                    body(B // 2 - 1, j, True)


def stage_output(nc, inp, ident, wn, w_in, o_d, x3_d, out_d):
    CH = HQ * D // P
    Q = 4
    CQ = CH // Q
    UNROLL = 2 * Q
    CS = CH // SL
    with ExitStack() as ctx:
        m = Bench(nc, ctx, "out")
        wt_hi = m.sb("wt_hi", [P, CH, H], F32R)
        wt_lo = m.sb("wt_lo", [P, CH, H], F32R)
        o_n = [m.sb(f"o_n{i}", [P, BT, CQ * S]) for i in range(2)]
        o_hi = [m.sb(f"o_hi{i}", [P, CQ, P], F32R) for i in range(2)]
        o_lo = [m.sb(f"o_lo{i}", [P, CQ, P], F32R) for i in range(2)]
        x3 = [m.sb(f"x3{i}", [P, H]) for i in range(2)]
        y = [m.sb(f"y{i}", [P, H]) for i in range(2)]
        pw = [m.psum(f"pw{i}", [P, BANK]) for i in range(4)]
        py = [m.psum(f"py{i}", [P, BANK]) for i in range(2)]

        w_turned = m.sem("w_turned")
        w_hi = m.sem("w_hi")
        w_lo = m.sem("w_lo")
        o_in = [m.sem(f"o_in{i}") for i in range(2)]
        x3_in = [m.sem(f"x3_in{i}") for i in range(2)]
        o_hi_done = m.sem("o_hi_done")
        o_lo_done = m.sem("o_lo_done")
        unit_done = m.sem("unit_done")
        summed = m.sem("summed")
        stored = [m.sem(f"stored{i}") for i in range(2)]

        with nc.Block() as block:

            @block.sync
            def _(sp):
                def load_o(it, i):
                    t, q, s = it * 2 + i // Q, i % Q, i % 2
                    src = o_d[bass.ds(t * BT, BT), :, q * CQ * S:(q + 1) * CQ * S].rearrange("b d x -> d b x")
                    sp.dma_start(o_n[s][:], src).then_inc(o_in[s], 16)
                    if q == 0:
                        x = x3_d[bass.ds(t, 1)].rearrange("a p h -> (a p) h")
                        sp.dma_start(x3[i // Q % 2][:], x).then_inc(x3_in[i // Q % 2], 16)

                for s in range(2, SL):
                    sp.wait_ge(w_turned, (s - 1) * CS)
                    load_wo(sp, inp, s, wn[s % 2], w_in[s % 2])
                    if s < 4:
                        load_o(0, s - 2)

                def store(t, s):
                    sp.wait_ge(summed, t + 1)
                    sp.dma_start(out_d[bass.ds(t, 1)].rearrange("a p h -> (a p) h"), y[s][:]).then_inc(stored[s], 16)

                def body(it, i, first, tail):
                    u = it * UNROLL + i
                    if not (tail and i + 2 >= UNROLL):
                        sp.wait_ge(o_lo_done, u + 1)
                        if (i + 2) % Q == 0 and not (first and i + 2 == Q):
                            sp.wait_ge(summed, it * 2 + (i + 2) // Q - 1)
                        load_o(it, i + 2)
                    if i % Q == 1 and not (first and i == 1):
                        store(it * 2 + i // Q - 1, (i // Q + 1) % 2)

                for i in range(UNROLL):
                    body(0, i, True, False)
                with sp.Fori(1, TT // 2 - 1) as it:
                    for i in range(UNROLL):
                        body(it, i, False, False)
                for i in range(UNROLL):
                    body(TT // 2 - 1, i, False, True)
                store(TT - 1, (TT - 1) % 2)
                for s in range(2):
                    sp.wait_ge(stored[s], 16 * (TT // 2))

            @block.tensor
            def _(pe):
                for c in range(CH):
                    s = c // CS
                    if c % CS == 0:
                        pe.wait_ge(w_in[s % 2], 16 * (s // 2 + 1))
                    if c >= 4:
                        pe.wait_ge(w_lo, c - 3)
                    for o in range(KC):
                        t = pe.transpose(pw[c % 4][:, o * P:(o + 1) * P], wn[s % 2][:, o, c % CS * P:(c % CS + 1) * P], ident[:])
                    t.then_inc(w_turned, 1)
                pe.wait_ge(w_lo, CH)

                def body(it, i, tail):
                    u, q = it * UNROLL + i, i % Q
                    pe.wait_ge(o_lo_done, u + 1)
                    if q == 0 and not (isinstance(it, int) and it == 0):
                        pe.wait_ge(summed, it * 2 + i // Q - 1)
                    for c in range(CQ):
                        w = q * CQ + c
                        last = three_pass(pe, py[i // Q][:], o_hi[i % 2][:, c, :], o_lo[i % 2][:, c, :], wt_hi[:, w, :],
                                          wt_lo[:, w, :], w == 0, w == CH - 1)
                    last.then_inc(unit_done, 1)

                for i in range(UNROLL):
                    body(0, i, False)
                with pe.Fori(1, TT // 2) as it:
                    for i in range(UNROLL):
                        body(it, i, False)

            @block.scalar
            def _(act):
                for c in range(CH):
                    act.wait_ge(w_turned, c + 1)
                    act.activation(wt_hi[:, c, :], pw[c % 4][:], ACT.Copy).then_inc(w_hi, 1)

                def body(it, i):
                    u = it * UNROLL + i
                    act.wait_ge(o_in[i % 2], (it * (UNROLL // 2) + i // 2 + 1) * 16)
                    if not isinstance(u, int) or u >= 2:
                        act.wait_ge(unit_done, u - 1)
                    src = o_n[i % 2][:].rearrange("p b (c t) -> p c b t", c=CQ)
                    dst = o_hi[i % 2][:].rearrange("p c (b t) -> p c b t", b=BT)
                    act.activation(dst, src, ACT.Copy).then_inc(o_hi_done, 1)

                for i in range(UNROLL):
                    body(0, i)
                with act.Fori(1, TT // 2) as it:
                    for i in range(UNROLL):
                        body(it, i)

            @block.vector
            def _(dve):
                v = nc.vector
                for c in range(CH):
                    dve.wait_ge(w_hi, c + 1)
                    v.tensor_tensor(wt_lo[:, c, :], pw[c % 4][:], f32(wt_hi[:, c, :]), ALU.subtract).then_inc(w_lo, 1)

                def add(t, s, round_of, first):
                    dve.wait_ge(unit_done, t * Q + Q)
                    dve.wait_ge(x3_in[s], (round_of + 1) * 16)
                    if not first:
                        dve.wait_ge(stored[s], round_of * 16)
                    v.tensor_tensor(y[s][:], x3[s][:], py[s][:], ALU.add).then_inc(summed, 1)

                def body(it, i, peeled):
                    u = it * UNROLL + i
                    dve.wait_ge(o_hi_done, u + 1)
                    src = o_n[i % 2][:].rearrange("p b (c t) -> p c b t", c=CQ)
                    dst = o_lo[i % 2][:].rearrange("p c (b t) -> p c b t", b=BT)
                    hi = f32(o_hi[i % 2][:]).rearrange("p c (b t) -> p c b t", b=BT)
                    v.tensor_tensor(dst, src, hi, ALU.subtract).then_inc(o_lo_done, 1)
                    if i == 1 and not peeled:
                        add(it * 2 - 1, 1, it - 1, isinstance(it, int))
                    if i == Q + 1:
                        add(it * 2, 0, it, peeled)

                for i in range(UNROLL):
                    body(0, i, True)
                for i in range(UNROLL):
                    body(1, i, False)
                with dve.Fori(2, TT // 2) as it:
                    for i in range(UNROLL):
                        body(it, i, False)
                add(TT - 1, 1, TT // 2 - 1, False)


def program(nc, inp, out):
    x3_d = nc.dram_tensor("x3_scratch", [TT, P, H], F32).ap()
    q_d = nc.dram_tensor("q_scratch", [B, HK, D, QS], F32).ap()
    k_d = nc.dram_tensor("k_scratch", [B, D, HK * S], F32).ap()
    v_d = nc.dram_tensor("v_scratch", [TT, P, HK * D], F32).ap()
    kt_d = nc.dram_tensor("kt_scratch", [PAGES, D, HK * PS], F32).ap()
    o_d = nc.dram_tensor("o_scratch", [B, D, HK * P], F32).ap()
    with ExitStack() as ctx:
        m = Bench(nc, ctx, "all")
        ident = m.sb("ident", [P, P])
        table = m.sb("table", [1, B * NPP], I32)
        len_i = m.sb("len_i", [P, B], I32)
        with ExitStack() as early:
            e = Bench(nc, early, "early")
            xT_hi, xT_lo = (e.sb(name, [P, KC, TOK], F32R) for name in ("xT_hi", "xT_lo"))
            tabs = e.sb("tabs", [P, 4, TT, D])
            w2n = e.sb("w2n", [P, 2, KC, H])
            w_in = e.sem("w_in")
            stage_layers(nc, inp, ident, xT_hi, xT_lo, tabs, len_i, w2n, w_in, x3_d)
            stage_project(nc, inp, ident, xT_hi, xT_lo, tabs, w2n, w_in, table, q_d, k_d, v_d, kt_d)
        wo = [m.sb(f"wo{i}", [P, KC, HQ * D // SL]) for i in range(2)]
        wo_in = [m.sem(f"wo_in{i}") for i in range(2)]
        v_rows = v_d.rearrange("t (b s) c -> (t b) s c", s=S)
        stage_attend(nc, inp, ident, table, len_i, wo, wo_in, q_d, k_d, v_rows, kt_d, o_d)
        stage_output(nc, inp, ident, wo, wo_in, o_d, x3_d, out.rearrange("(t b) s h -> t (b s) h", b=BT))


INPUTS = ["x", "itok_B_0_15", "itok_B_0_2", "itok_B_3_7", "itok_Bx16_0_63", "itok_B_207_1644", "L0_cond_weights",
          "L1_cond_W", "L1_cond_lora_A", "L1_cond_lora_B_w", "L2_cond_weight", "L3_cond_Wq", "L3_cond_Wk", "L3_cond_Wv",
          "L3_cond_Wo", "L3_cond_q_norm_w", "L3_cond_k_norm_w", "L3_cond_k_cache", "L3_cond_v_cache"]


def inverse_frequencies():
    return (np.float32(1.0) / np.power(np.float32(THETA), np.arange(0, D, 2, dtype=np.float32) / np.float32(D))).astype(np.float32)


def kernel(**inputs):
    import concourse.bacc as bacc
    from concourse.bass_utils import run_bass_kernel_spmd as run

    nc = bacc.Bacc("TRN2", target_bir_lowering=False, num_devices=1)
    arrays, args = {}, {}
    for name in INPUTS + ["rope_inv_freq"]:
        a = inverse_frequencies() if name == "rope_inv_freq" else np.ascontiguousarray(inputs[name])
        arrays[f"in_{name}"] = a
        args[name] = nc.dram_tensor(f"in_{name}", a.shape, mybir.dt.from_np(a.dtype), kind="ExternalInput").ap()
    out = nc.dram_tensor("out", [B, S, H], F32, kind="ExternalOutput").ap()
    program(nc, args, out)
    return run(nc, [arrays], core_ids=[0]).results[0]["out"]
```

```python
from contextlib import ExitStack

import concourse.bass as bass
import numpy as np
from concourse import mybir

F32 = mybir.dt.float32
F32R = mybir.dt.float32r
I32 = mybir.dt.int32
ALU = mybir.AluOpType
ACT = mybir.ActivationFunctionType
AX_X = mybir.AxisListType.X

P = 128
BANK = 512
B, S, H = 32, 32, 512
TOK = B * S
TT = TOK // P
BT = P // S
KC = H // P
NS0 = 16
NL, R = 5, 32
LR = NL * R
NE = 8
D, HQ, HK = 128, 32, 8
REP = HQ // HK
QW = REP * D
WE = QW + 2 * D
QK = QW + D
PAGES, PS, NPP = 64, 32, 16
L = NPP * PS
KEYS = L + S
NCH = L // P
PPT = P // PS
QS = REP * S
PG = NPP + 1
POOL_PAGES = 6
ST = QS + S
THETA, EPS = 10000.0, 1e-6
SCALE = float(1.0 / np.sqrt(D))
HALF = D // 2
MASKED = 1e30
MAGIC = 1.5 * 2.0**23
TWO_PI_HI = 6.28125
TWO_PI_LO = float(2.0 * np.pi - TWO_PI_HI)
IN_RANGE = "the block table holds numbers of pages"
PI_IN = float(np.nextafter(np.float32(np.pi), np.float32(0.0)))


def f32(ap):
    return ap.bitcast(F32)


class Bench:

    def __init__(self, nc, ctx, prefix):
        self.nc, self.ctx, self.prefix = nc, ctx, prefix

    def sb(self, name, shape, dt=F32):
        return self.ctx.enter_context(self.nc.sbuf_tensor(f"{self.prefix}_{name}", shape, dt))

    def psum(self, name, shape):
        return self.ctx.enter_context(self.nc.psum_tensor(f"{self.prefix}_{name}", shape, F32))

    def sem(self, name):
        return self.ctx.enter_context(self.nc.semaphore(f"{self.prefix}_{name}"))


def three_pass(pe, out, w_hi, w_lo, x_hi, x_lo, first, last):
    pe.matmul(out, w_lo, x_hi, start=first, stop=False)
    pe.matmul(out, w_hi, x_lo, start=False, stop=False)
    return pe.matmul(out, w_hi, x_hi, start=False, stop=last)


def load_head(eng, inp, c, tile, sem):
    for name, rows, o in zip(("L3_cond_Wq", "L3_cond_Wk", "L3_cond_Wv"), (QW, D, D), (0, REP, REP + 1)):
        src = inp[name].rearrange("(c o p) i -> c p o i", p=P, o=rows // P)[bass.ds(c, 1)]
        eng.dma_start(tile[:, o:o + rows // P, :], src.rearrange("a p o i -> (a p) o i")).then_inc(sem, 16)


def stage_layers(nc, inp, ident, xT_hi, xT_lo, flat_hi, tabs, len_i, x, w2n, w_in, x3_d):
    with ExitStack() as ctx:
        m = Bench(nc, ctx, "lay")
        room = tabs[:].rearrange("p a t d -> p (a t d)")
        w0 = room[:, 3 * TT * P:].rearrange("p (t c) -> p t c", t=TT)
        idx = m.sb("idx", [1, 2, B], I32)
        w1n = m.sb("w1n", [P, KC, H])
        w1 = m.sb("w1", [P, 2, KC, H], F32R)
        w1_hi, w1_lo = w1[:, 0], w1[:, 1]
        a_n = m.sb("a_n", [P, KC, LR])
        a_hi = m.sb("a_hi", [P, KC, LR], F32R)
        a_lo = m.sb("a_lo", [P, KC, LR], F32R)
        bw_n = m.sb("bw_n", [P, KC, R])
        bw_half = m.sb("bw_half", [P, KC, R])
        bw_t = room[0:R, TT * P:TT * P + H]
        lab_i = m.sb("lab_i", [P, B], I32)
        lab = m.sb("lab", [P, TT])
        lab_of = m.sb("lab_of", [P, LR])
        low_own = [m.sb(f"low_own{i}", [P, LR]) for i in range(2)]
        low = m.sb("low", [P, TT, R])
        low_t = room[0:R, 0:TT * P].rearrange("p (t c) -> p t c", t=TT)
        w2t = m.sb("w2t", [P, NE, KC, H])
        x2m_hi = m.sb("x2m_hi", [P, 2 * KC * BT * P + BT * S], F32R)
        x2m_lo = flat_hi
        KH = KC // 2
        SLOTS = 4
        w_hi = w1[:].rearrange("p a (b k) o -> p (a b) k o", k=KH)
        w_lo = xT_lo[:].rearrange("p k t -> p (k t)").rearrange("p (a k o) -> p a k o", a=SLOTS, k=KH)

        def masked(slot, k):
            return (slot * KC + k) * BT * P

        inv = m.sb("inv", [P, HALF])
        pos_i = m.sb("pos_i", [P, 1], I32)
        row_i = m.sb("row_i", [P, 1], I32)
        base = m.sb("base", [P, 1])
        pos = m.sb("pos", [P, TT])
        angle_t = m.sb("angle", [P, TT, HALF])
        angle = angle_t[:]
        turns, *trig = (w1n[:, i].rearrange("p (t d) -> p t d", t=TT) for i in range(3))
        nw, nw_neg = (w1n[:, 3, i * 2 * D:(i + 1) * 2 * D].rearrange("p (a d) -> p a d", a=2) for i in range(2))
        ps = [m.psum(f"ps{i}", [P, BANK]) for i in range(8)]
        written = m.sem("written")
        x_in = [m.sem("x_in0"), m.sem("x_in1")]
        bw_in = m.sem("bw_in")
        w0_zero = m.sem("w0_zero")
        ident_made = m.sem("ident_made")
        idx_in = m.sem("idx_in")
        w0_in = [m.sem(f"w0_in{i}") for i in range(3)]
        w1_in = [m.sem(f"w1_in{k}") for k in range(KC)]
        small_in = m.sem("small_in")
        w2_in = [m.sem("w2_in0"), m.sem("w2_in1")]
        x_new = m.sem("x_new")
        split_hi = m.sem("split_hi")
        split_lo = m.sem("split_lo")
        a_split = m.sem("a_split")
        bw_halved = m.sem("bw_halved")
        own_kept = m.sem("own_kept")
        bw_ready = m.sem("bw_ready")
        lab_ready = m.sem("lab_ready")
        low_ready = m.sem("low_ready")
        lowt_ready = m.sem("lowt_ready")
        w2_act = m.sem("w2_act")
        w2_dve = m.sem("w2_dve")
        lab_numbered = m.sem("lab_numbered")
        x2m_hi_zero = m.sem("x2m_hi_zero")
        x2m_lo_zero = m.sem("x2m_lo_zero")
        x2m_hi_done = m.sem("x2m_hi_done")
        x2m_ready = m.sem("x2m_ready")
        w_hi_done = m.sem("w_hi_done")
        w_lo_done = m.sem("w_lo_done")
        w_used = m.sem("w_used")
        rope_in = m.sem("rope_in")
        rope_no = m.sem("rope_no")
        prep = m.sem("prep")
        reduced = m.sem("reduced")
        trig_done = m.sem("trig_done")
        x3_out = m.sem("x3_out")

        ex = [("W2T", e * KC + k) for e in range(NE) for k in range(KC)]
        uses = [("W1T", k) for k in range(KC)] + ex[:4] + [("BwT", 0)]
        uses += [("L0", 0)]
        for t in range(TT):
            uses += ([("L0", t + 1)] if t + 1 < TT else []) + [("x1T", t)]
        for t in range(TT):
            uses += [("low", t), ex[4 + t]]
        uses += [("lowT", t) for t in range(TT)] + ex[12:16]
        for t in range(TT):
            uses += [("L1", t)] + (ex[16 + 2 * t:18 + 2 * t] if t < TT - 2 else [])
        uses += ex[28:] + [("x2T", 0)]
        for t in range(TT):
            uses += [("x2T", t + 1)] if t + 1 < TT else []
            uses += [("L2", t)]
        uses += [("x3T", t) for t in range(TT)]
        pos_of = {u: i for i, u in enumerate(uses)}
        splits = [u for u in uses if u[0] in ("W1T", "x1T", "x3T")]
        split_no = {u: i + 1 for i, u in enumerate(splits)}

        def drained(u):
            kind, i = u
            if kind in ("L0", "L1", "L2"):
                return x_new, TT * int(kind[1]) + i + 1
            if u in split_no:
                return split_lo, split_no[u]
            if kind == "W2T":
                return (w2_dve if i % 2 else w2_act), i // 2 + 1
            return {"BwT": bw_ready, "low": low_ready, "lowT": lowt_ready, "x2T": x2m_ready}[kind], i + 1

        HALVES = 2 * BT

        def weights_used(h):
            t, i = divmod(h, HALVES)
            return (w_used, t * (HALVES - 1) + i + 1) if i < HALVES - 1 else (written, pos_of[("L2", t)] + 1)

        def halves_in(t):
            return range(t * HALVES + SLOTS, min((t + 1) * HALVES + SLOTS, TT * HALVES))

        def half_of(h, adapter):
            k = slice(h % 2 * KH, (h % 2 + 1) * KH)
            return w2t[:, bass.ds(adapter[h // 2], 1), k, :].rearrange("p a k o -> p (a k) o")

        def adapters(engine):
            return nc.values_load_multi_w_load_instructions(idx[0:1, 1, :], engines=[engine], min_val=0, max_val=NE - 1,
                                                            skip_runtime_bounds_check_because="adapter_ids are adapters")[1]

        W0_TILES = (range(0, 3), range(3, 5), range(5, TT))

        def states(engine, tiles):
            b = slice(tiles[0] * BT, (tiles[-1] + 1) * BT)
            return nc.values_load_multi_w_load_instructions(idx[0:1, 0, b], engines=[engine], min_val=0,
                                                            max_val=NS0 - 1,
                                                            skip_runtime_bounds_check_because="conditions are states")[1]

        def load_w0(eng, engine, part):
            eng.wait_ge(idx_in, 32)
            eng.wait_ge(w0_zero, 1)
            tiles = W0_TILES[part]
            for b, s in enumerate(states(engine, tiles), tiles[0] * BT):
                t, r = b // BT, slice((b % BT) * S, (b % BT + 1) * S)
                eng.dma_start(w0[r, t, r], inp["L0_cond_weights"][bass.ds(s, 1)].rearrange("a c d -> (a c) d")).then_inc(w0_in[part], 16)

        with nc.Block() as block:

            @block.sync
            def _(sp):
                def load_w2(e):
                    sp.dma_start(w2n[:, e % 2], inp["L2_cond_weight"][e].rearrange("(o p) i -> p o i", p=P)).then_inc(w2_in[e % 2], 16)

                sp.dma_start(idx[:, 0, :], inp["itok_B_0_15"].rearrange("(a b) -> a b", a=1)).then_inc(idx_in, 16)
                sp.dma_start(idx[:, 1, :], inp["itok_B_3_7"].rearrange("(a b) -> a b", a=1)).then_inc(idx_in, 16)
                w1_rows = inp["L1_cond_W"].rearrange("(o p) i -> p o i", p=P)
                for k in range(KC):
                    cols = slice(k * P, (k + 1) * P)
                    sp.dma_start(w1n[:, :, cols], w1_rows[:, :, cols]).then_inc(w1_in[k], 16)
                x_rows = inp["x"].rearrange("(t b) c h -> (b c) t h", b=BT)
                for i in range(2):
                    half = slice(i * TT // 2, (i + 1) * TT // 2)
                    sp.dma_start(x[:, half], x_rows[:, half]).then_inc(x_in[i], 16)
                load_w2(0)
                sp.dma_start(bw_n[:], inp["L1_cond_lora_B_w"].rearrange("(o p) r -> p o r", p=P)).then_inc(bw_in, 16)
                load_w0(sp, mybir.EngineType.SP, 2)
                for l in range(NL):
                    sp.dma_start(a_n[:, :, l * R:(l + 1) * R],
                                 inp["L1_cond_lora_A"][l].rearrange("(k p) r -> p k r", p=P)).then_inc(small_in, 16)
                sp.dma_start(lab_i[:], inp["itok_B_0_2"].partition_broadcast(P)).then_inc(small_in, 16)
                load_w2(1)
                sp.wait_ge(written, pos_of[("W1T", KC - 1)] + 1)
                sp.dma_start(inv[:], inp["rope_inv_freq"].partition_broadcast(P)).then_inc(rope_in, 16)
                sp.dma_start(nw[:, 0, :], inp["L3_cond_q_norm_w"].partition_broadcast(P)).then_inc(rope_in, 16)
                sp.dma_start(nw[:, 1, :], inp["L3_cond_k_norm_w"].partition_broadcast(P)).then_inc(rope_in, 16)
                sp.dma_start(len_i[:], inp["itok_B_207_1644"].partition_broadcast(P)).then_inc(rope_in, 16)
                for e in range(2, NE):
                    sp.wait_ge(written, pos_of[("W2T", (e - 2) * KC + KC - 1)] + 1)
                    load_w2(e)
                sp.wait_ge(written, pos_of[ex[-1]] + 1)
                load_head(sp, inp, 0, w2n.rearrange("p e k h -> p (e k) h")[:, 0:WE // P, :], w_in)
                for t in range(TT):
                    sp.wait_ge(x_new, 2 * TT + t + 1)
                    sp.dma_start(x3_d[t], x[:, t, :]).then_inc(x3_out, 16)
                sp.wait_ge(x3_out, 16 * TT)
                sp.wait_ge(w_in, 48)

            @block.gpsimd
            def _(pool):
                nc.gpsimd.memset(w0, 0.0).then_inc(w0_zero, 1)
                nc.gpsimd.memset(ident[:], 0.0).then_inc(ident_made, 1)
                pool.wait_ge(ident_made, 1)
                nc.gpsimd.affine_select(out=ident[:], in_=ident[:], compare_op=ALU.not_equal, fill=1.0, base=0,
                                        pattern=[[-1, P]], channel_multiplier=1).then_inc(ident_made, 1)
                load_w0(pool, mybir.EngineType.Pool, 1)
                nc.gpsimd.memset(f32(x2m_hi[:]), 0.0).then_inc(x2m_hi_zero, 1)
                nc.gpsimd.iota(pos_i[:], pattern=[[0, 1]], base=0, channel_multiplier=1).then_inc(rope_no, 1)
                nc.gpsimd.iota(lab_of[:], pattern=[[1, NL], [0, R]], base=0, channel_multiplier=0,
                               allow_small_or_imprecise_dtypes=True).then_inc(lab_numbered, 1)

                g = nc.gpsimd
                pool.wait_ge(written, pos_of[("L1", TT - 1)] + 1)
                for slot in range(2):
                    g.memset(f32(x2m_lo[:, masked(slot, 0):masked(slot + 1, 0) + slot * BT * S]), 0.0).then_inc(x2m_lo_zero, 1)
                pool.wait_ge(trig_done, 2)
                pool.wait_ge(x_new, 2 * TT)
                sin, cos = trig
                lo, hi = slice(0, HALF), slice(HALF, D)

                def table(i, half, values, weights):
                    w = weights.rearrange("p (a d) -> p a d", a=1).broadcast_to([P, TT, HALF])
                    g.tensor_tensor(tabs[:, i, :, half], values, w, ALU.mult)

                for i in range(2):
                    table(2 * i, lo, cos, nw[:, i, lo])
                    table(2 * i, hi, cos, nw[:, i, hi])
                    table(2 * i + 1, lo, sin, nw_neg[:, i, hi])
                    table(2 * i + 1, hi, sin, nw[:, i, lo])

            @block.tensor
            def _(pe):
                def end(u, ins):
                    ins.then_inc(written, 1)

                pe.wait_ge(ident_made, 2)
                for n, u in enumerate(uses):
                    kind, i = u
                    bank = ps[n % 8]
                    if n >= 8:
                        pe.wait_ge(*drained(uses[n - 8]))
                    if kind == "L0":
                        if i % (TT // 2) == 0:
                            pe.wait_ge(x_in[i // (TT // 2)], 16)
                        for part, tiles in enumerate(W0_TILES):
                            if i == tiles[0]:
                                pe.wait_ge(w0_in[part], 16 * BT * len(tiles))
                        end(u, pe.matmul(bank[:], w0[:, i, :], x[:, i, :], start=True, stop=True))
                    elif kind == "W1T":
                        pe.wait_ge(w1_in[i], 16)
                        for o in range(KC):
                            t = pe.transpose(bank[:, o * P:(o + 1) * P], w1n[:, o, i * P:(i + 1) * P], ident[:])
                        end(u, t)
                    elif kind == "BwT":
                        pe.wait_ge(bw_halved, 1)
                        for o in range(KC):
                            t = pe.transpose(bank[0:R, o * P:(o + 1) * P], bw_half[:, o, :], ident[:])
                        end(u, t)
                    elif kind in ("x1T", "x2T", "x3T"):
                        pe.wait_ge(x_new, TT * (int(kind[1]) - 1) + i + 1)
                        for k in range(KC):
                            t = pe.transpose(bank[:, k * P:(k + 1) * P], x[:, i, k * P:(k + 1) * P], ident[:])
                        end(u, t)
                    elif kind == "low":
                        if i == 0:
                            pe.wait_ge(a_split, 2)
                        pe.wait_ge(split_lo, split_no[("x1T", i)])
                        tok = slice(i * P, (i + 1) * P)
                        for k in range(KC):
                            t = three_pass(pe, bank[:, 0:LR], xT_hi[:, k, tok], xT_lo[:, k, tok], a_hi[:, k, :], a_lo[:, k, :],
                                           k == 0, k == KC - 1)
                        end(u, t)
                    elif kind == "lowT":
                        pe.wait_ge(low_ready, i + 1)
                        end(u, pe.transpose(bank[0:R, 0:P], low[:, i, :], ident[:]))
                    elif kind == "W2T":
                        e, k = divmod(i, KC)
                        pe.wait_ge(w2_in[e % 2], 16 * (e // 2 + 1))
                        for o in range(KC):
                            t = pe.transpose(bank[:, o * P:(o + 1) * P], w2n[:, e % 2, o, k * P:(k + 1) * P], ident[:])
                        end(u, t)
                    elif kind == "L1":
                        pe.wait_ge(split_lo, max(split_no[("x1T", i)], split_no[("W1T", KC - 1)]))
                        pe.wait_ge(lowt_ready, i + 1)
                        pe.wait_ge(bw_ready, 1)
                        tok = slice(i * P, (i + 1) * P)
                        for k in range(KC):
                            three_pass(pe, bank[:], xT_hi[:, k, tok], xT_lo[:, k, tok], w1_hi[:, k, :], w1_lo[:, k, :],
                                       k == 0, False)
                        end(u, pe.matmul(bank[:], low_t[:, i, :], bw_t, start=False, stop=True))
                    elif kind == "L2":
                        pe.wait_ge(x2m_ready, i + 1)
                        for b in range(HALVES):
                            h = i * HALVES + b
                            pe.wait_ge(w_lo_done, h + 1)
                            for k in range(KH):
                                c = masked(i % 2, b % 2 * KH + k) + b // 2 * P
                                t = three_pass(pe, bank[:], x2m_hi[:, c:c + P], x2m_lo[:, c:c + P], w_hi[:, h % SLOTS, k, :],
                                               w_lo[:, h % SLOTS, k, :], b == 0 and k == 0, b == HALVES - 1 and k == KH - 1)
                            if b < HALVES - 1:
                                t.then_inc(w_used, 1)
                        end(u, t)

            @block.scalar
            def _(act):
                load_w0(act, mybir.EngineType.Activation, 0)

                def split_w(h):
                    if h >= SLOTS:
                        act.wait_ge(*weights_used(h - SLOTS))
                    act.activation(w_hi[:, h % SLOTS], half_of(h, adapter), ACT.Copy).then_inc(w_hi_done, 1)

                for i, u in enumerate(uses):
                    bank, kind, j = ps[i % 8], *u
                    if u == ("L2", 1):
                        act.wait_ge(reduced, 2)
                        for angles in trig:
                            act.activation(angles, angles, ACT.Sin).then_inc(trig_done, 1)
                    if u in split_no:
                        act.wait_ge(written, i + 1)
                        if kind == "W1T":
                            dst = w1_hi[:, j, :]
                            src = bank[:]
                        else:
                            dst = xT_hi[:, :, j * P:(j + 1) * P]
                            src = bank[:].rearrange("p (k t) -> p k t", k=KC)
                        act.activation(dst, src, ACT.Copy).then_inc(split_hi, 1)
                    elif kind == "BwT":
                        act.wait_ge(written, i + 1)
                        act.activation(bw_t, bank[0:R, :], ACT.Copy).then_inc(bw_ready, 1)
                    elif kind == "W2T" and j % 2 == 0:
                        act.wait_ge(written, i + 1)
                        act.activation(w2t[:, j // KC, j % KC, :], bank[:], ACT.Copy).then_inc(w2_act, 1)
                    elif kind == "x2T":
                        if j == 0:
                            adapter = adapters(mybir.EngineType.Activation)
                            act.wait_ge(w2_dve, NE * KC // 2)
                            act.wait_ge(w2_act, NE * KC // 2)
                            act.wait_ge(written, pos_of[("L1", TT - 1)] + 1)
                            act.wait_ge(x2m_hi_zero, 1)
                        act.wait_ge(written, i + 1)
                        if j >= 2:
                            act.wait_ge(written, pos_of[("L2", j - 2)] + 1)
                        for k in range(KC):
                            c = masked(j % 2, k)
                            dst = x2m_hi[:, c:c + BT * (P + S)].rearrange("p (b c) -> p b c", c=P + S)[:, :, 0:S]
                            t = act.activation(dst, bank[:, k * P:(k + 1) * P].rearrange("p (b c) -> p b c", c=S), ACT.Copy)
                        t.then_inc(x2m_hi_done, 1)
                        if j == 0:
                            for h in range(SLOTS):
                                split_w(h)
                    elif kind == "L2":
                        for h in halves_in(j):
                            split_w(h)

            @block.vector
            def _(dve):
                v = nc.vector
                n = [0]

                def link(ins):
                    ins.then_inc(prep, 1)
                    n[0] += 1
                    dve.wait_ge(prep, n[0])

                dve.wait_ge(bw_in, 16)
                v.tensor_scalar(bw_half[:], bw_n[:], 0.5, None, ALU.mult).then_inc(bw_halved, 1)

                def labels():
                    dve.wait_ge(small_in, 16 * (NL + 1))
                    v.tensor_copy(a_hi[:], a_n[:]).then_inc(a_split, 1)
                    for b in range(BT):
                        r = slice(b * S, (b + 1) * S)
                        t = v.tensor_copy(lab[r, :], lab_i[r, :].rearrange("p (t b) -> p t b", b=BT)[:, :, b])
                    t.then_inc(lab_ready, 1)
                    dve.wait_ge(a_split, 1)
                    v.tensor_tensor(a_lo[:], a_n[:], f32(a_hi[:]), ALU.subtract).then_inc(a_split, 1)

                def angles():
                    dve.wait_ge(rope_no, 1)
                    link(v.tensor_scalar(row_i[:], pos_i[:], S - 1, None, ALU.bitwise_and))
                    link(v.tensor_copy(base[:], row_i[:]))
                    dve.wait_ge(rope_in, 16 * 4)
                    for b in range(BT):
                        r = slice(b * S, (b + 1) * S)
                        link(v.tensor_copy(pos[r, :], len_i[r, :].rearrange("p (t b) -> p t b", b=BT)[:, :, b]))
                    link(v.tensor_scalar(pos[:], pos[:], base[:, 0:1], None, ALU.add))
                    for t in range(TT):
                        v.tensor_scalar(angle[:, t, :], inv[:], pos[:, t:t + 1], None, ALU.mult)
                    v.tensor_scalar(nw[:, 0, :], nw[:, 0, :], -SCALE * float(np.sqrt(D)), None, ALU.mult)
                    link(v.tensor_scalar(nw[:, 1, :], nw[:, 1, :], float(np.sqrt(D)), None, ALU.mult))
                    link(v.tensor_scalar(nw_neg, nw, -1.0, None, ALU.mult))

                def reduce(k, quarter, phase):
                    red = trig[k]
                    link(v.tensor_scalar(turns, angle, float(1.0 / (2.0 * np.pi)), quarter, ALU.mult, ALU.add))
                    link(v.tensor_scalar(turns, turns, MAGIC, None, ALU.add))
                    link(v.tensor_scalar(turns, turns, MAGIC, None, ALU.subtract))
                    link(v.scalar_tensor_tensor(red, turns, -TWO_PI_HI, angle, ALU.mult, ALU.add))
                    link(v.scalar_tensor_tensor(red, turns, -TWO_PI_LO, red, ALU.mult, ALU.add))
                    link(v.tensor_scalar(red, red, float(phase), PI_IN, ALU.add, ALU.min))
                    v.tensor_scalar(red, red, -PI_IN, None, ALU.max).then_inc(reduced, 1)

                def split_w(h):
                    dve.wait_ge(w_hi_done, h + 1)
                    v.tensor_tensor(w_lo[:, h % SLOTS], half_of(h, adapter), f32(w_hi[:, h % SLOTS]),
                                    ALU.subtract).then_inc(w_lo_done, 1)

                dve.wait_ge(x_in[0], 16)
                dve.wait_ge(x_in[1], 16)
                for i, u in enumerate(uses):
                    bank, kind, j = ps[i % 8], *u
                    if u == ("x1T", 0):
                        labels()
                    if u == ("L1", 1):
                        angles()
                    if u == ("L1", 3):
                        reduce(0, 0.0, 0.0)
                    if u == ("L1", 5):
                        reduce(1, 0.25, 0.5 * np.pi)
                    if kind == "L2":
                        for h in halves_in(j):
                            split_w(h)
                    if kind in ("L0", "L1", "L2"):
                        dve.wait_ge(written, i + 1)
                        if int(kind[1]):
                            dve.wait_ge(x_new, TT * int(kind[1]))
                        v.tensor_tensor(x[:, j, :], x[:, j, :], bank[:], ALU.add).then_inc(x_new, 1)
                    elif u in split_no:
                        dve.wait_ge(split_hi, split_no[u])
                        if kind == "W1T":
                            lo, hi, src = w1_lo[:, j, :], w1_hi[:, j, :], bank[:]
                        else:
                            t = slice(j * P, (j + 1) * P)
                            lo, hi, src = xT_lo[:, :, t], xT_hi[:, :, t], bank[:].rearrange("p (k t) -> p k t", k=KC)
                        v.tensor_tensor(lo, src, f32(hi), ALU.subtract).then_inc(split_lo, 1)
                    elif kind == "low":
                        dve.wait_ge(written, i + 1)
                        dve.wait_ge(lab_ready, 1)
                        dve.wait_ge(lab_numbered, 1)
                        own = low_own[j % 2]
                        if j >= 2:
                            dve.wait_ge(low_ready, j - 1)
                        v.scalar_tensor_tensor(own[:], lab_of[:], lab[:, j:j + 1], bank[:, 0:LR],
                                               ALU.is_equal, ALU.mult).then_inc(own_kept, 1)
                        dve.wait_ge(own_kept, j + 1)
                        v.tensor_reduce(low[:, j, :], own[:].rearrange("p (l r) -> p r l", r=R), AX_X,
                                        ALU.add).then_inc(low_ready, 1)
                    elif kind == "lowT":
                        dve.wait_ge(written, i + 1)
                        v.tensor_copy(low_t[:, j, :], bank[0:R, 0:P]).then_inc(lowt_ready, 1)
                    elif kind == "W2T" and j % 2 == 1:
                        dve.wait_ge(written, i + 1)
                        v.tensor_copy(w2t[:, j // KC, j % KC, :], bank[:]).then_inc(w2_dve, 1)
                    elif kind == "x2T":
                        if j == 0:
                            adapter = adapters(mybir.EngineType.DVE)
                        dve.wait_ge(x2m_hi_done, j + 1)
                        if j < 2:
                            dve.wait_ge(x2m_lo_zero, j + 1)
                        for k in range(KC):
                            c = masked(j % 2, k)
                            hi, lo = (x[:, c:c + BT * (P + S)].rearrange("p (b c) -> p b c", c=P + S)[:, :, 0:S]
                                      for x in (x2m_hi, x2m_lo))
                            src = bank[:, k * P:(k + 1) * P].rearrange("p (b c) -> p b c", c=S)
                            t = v.tensor_tensor(lo, src, f32(hi), ALU.subtract)
                        t.then_inc(x2m_ready, 1)
                        if j == 0:
                            for h in range(SLOTS):
                                split_w(h)


def pages_of(nc, table, b, first, count, engine):
    return nc.values_load_multi_w_load_instructions(table[0:1, bass.ds(b * NPP + first, count)], engines=[engine],
                                                    min_val=0, max_val=PAGES - 1,
                                                    skip_runtime_bounds_check_because=IN_RANGE)[1]


def load_new_keys(eng, q_d, k_d, b, q, tile, sem):
    eng.dma_start(q[:], q_d[bass.ds(b, 1)].rearrange("a h d x -> d (a h) x")).then_inc(sem, 16)
    eng.dma_start(tile[:, NPP].rearrange("p h t -> p (h t)"), k_d[bass.ds(b, 1)].rearrange("a d x -> (a d) x")).then_inc(sem, 16)


def load_key_page(eng, kt_d, tile, j, page, sem):
    eng.dma_start(tile[:, j].rearrange("p h t -> p (h t)"),
                  kt_d[bass.ds(page, 1)].rearrange("a d x -> (a d) x")).then_inc(sem, 16)


def load_value_page(eng, inp, tile, j, page, sem):
    v_pages = inp["L3_cond_v_cache"].rearrange("g s h d -> g s (h d)")
    r = slice(j % PPT * PS, (j % PPT + 1) * PS)
    eng.dma_start(tile[r, j // PPT, :], v_pages[bass.ds(page, 1)].rearrange("a s c -> (a s) c")).then_inc(sem, 16)


def stage_project(nc, inp, ident, xT_hi, xT_lo, tabs, wn0, w_in0, table, q0, kT0, vc0, kq_in0, v_in0, q_d, k_d, v_d, kt_d):
    with ExitStack() as ctx:
        m = Bench(nc, ctx, "prj")
        wn = [wn0.rearrange("p e k h -> p (e k) h"), m.sb("wn1", [P, WE // P, H])]
        wt_hi = [m.sb(f"wt_hi{i}", [P, KC, WE], F32R) for i in range(2)]
        wt_lo = [m.sb(f"wt_lo{i}", [P, KC, WE], F32R) for i in range(2)]
        kn = [m.sb(f"kn{i}", [P, HK * D]) for i in range(2)]
        kst = [m.sb(f"kst{i}", [P, PPT, HK, PS]) for i in range(2)]
        sq = [m.sb(f"sq{i}", [P, QK]) for i in range(2)]
        ta = [m.sb(f"ta{i}", [P, QK]) for i in range(2)]
        tb = [m.sb(f"tb{i}", [P, QK]) for i in range(2)]
        qn = [m.sb(f"qn{i}", [P, QK]) for i in range(2)]
        ss = [m.sb(f"ss{i}", [P, REP + 1]) for i in range(2)]
        rs = [m.sb(f"rs{i}", [P, REP + 1]) for i in range(2)]
        rstd = [m.sb(f"rstd{i}", [P, REP + 1]) for i in range(2)]
        power = m.sb("power", [P, REP + 1])
        floor = m.sb("floor", [P, REP + 1])
        qst = [m.sb(f"qst{i}", [P, BT, ST]) for i in range(2)]
        vst = [m.sb(f"vst{i}", [P, D]) for i in range(4)]
        ps = [m.psum(f"ps{i}", [P, 2 * BANK]) for i in range(2)]
        pt = m.psum("pt", [P, 2 * BANK])
        pw = m.psum("pw", [P, 2, BANK])
        first_banks = [pw[:, 0], pw[:, 1]] + [x[:, i * BANK:(i + 1) * BANK] for x in (pt, ps[1]) for i in range(2)]

        w_in = [w_in0, m.sem("w_in1")]
        kn_in = [m.sem(f"kn_in{i}") for i in range(2)]
        job_t = m.sem("job_t")
        job_act = m.sem("job_act")
        job_dve = m.sem("job_dve")
        mm_done = m.sem("mm_done")
        q_squared = m.sem("q_squared")
        squared = m.sem("squared")
        k_roped = m.sem("k_roped")
        v_staged = m.sem("v_staged")
        roped = m.sem("roped")
        reduced = m.sem("reduced")
        normed = m.sem("normed")
        pool_step = m.sem("pool_step")
        turned = m.sem("turned")
        q_staged = m.sem("q_staged")
        stage_free = m.sem("stage_free")
        kst_free = m.sem("kst_free")
        ids_in = m.sem("ids_in")
        stored = m.sem("stored")
        k_stored = m.sem("k_stored")

        cq, sn_q, ck, sn_k = (tabs[:, i] for i in range(4))
        k_rows = inp["L3_cond_k_cache"].rearrange("a s h d -> (a s) (h d)")

        WJ = KC + 2
        UNROLL = 2 * TT

        def job_of(c, g):
            return WJ + c * (WJ + 2) + g

        def cache_step(t, last_head):
            return t < 2 if last_head else t >= WJ

        def loop(eng, body):
            last = HK // 2 - 1
            with eng.Fori(0, last) as it:
                for j in range(UNROLL):
                    body(it, j, False)
            for j in range(UNROLL):
                body(last, j, True)

        with nc.Block() as block:

            @block.sync
            def _(sp):
                def load_w(c, slot):
                    load_head(sp, inp, c, wn[slot], w_in[slot])

                def load_k(t, slot):
                    src = k_rows.rearrange("(t p) c -> t p c", p=P)[bass.ds(t, 1)]
                    sp.dma_start(kn[slot][:], src.rearrange("a p c -> (a p) c")).then_inc(kn_in[slot], 16)

                sp.sem_inc(stage_free, 2)
                sp.sem_inc(kst_free, 2)
                load_w(1, 1)
                load_k(0, 0)
                load_k(1, 1)
                sp.dma_start(table[:], inp["itok_Bx16_0_63"].rearrange("(a b) j -> a (b j)", a=1)).then_inc(ids_in, 16)
                sp.wait_ge(ids_in, 16)

                def body(it, j, tail):
                    n, c, t, slot = it * UNROLL + j, it * 2 + j // TT, j % TT, j // TT
                    if t == 0 and not tail:
                        sp.wait_ge(job_t, job_of(c, 0))
                        load_w(c + 2, slot)
                    last_head = tail and slot == 1
                    if cache_step(t, last_head):
                        u = t % 2
                        k = c * 2 + u
                        sp.wait_ge(job_act, job_of(c, t) + 1)
                        sp.wait_ge(job_dve, job_of(c, t) + 1)
                        dst = kt_d[bass.ds(k * PPT, PPT)].rearrange("g d x -> d g x")
                        sp.dma_start(dst, kst[u][:].rearrange("p g h t -> p g (h t)")).then_inc(k_stored, 16)
                        if not last_head:
                            load_k(k + 2, u)
                    sp.wait_ge(q_staged, n + 3)
                    tile = slice(t * BT, (t + 1) * BT)
                    sp.dma_start(q_d[tile, bass.ds(c, 1)].rearrange("b a d x -> d (b a) x"),
                                 qst[j % 2][:, :, 0:QS]).then_inc(stored, 16)
                    sp.dma_start(k_d[tile, :, bass.ds(c * S, S)].rearrange("b d x -> d b x"),
                                 qst[j % 2][:, :, QS:ST]).then_inc(stored, 16)
                    sp.wait_ge(v_staged, n + 1)
                    sp.dma_start(v_d[t, :, bass.ds(c * D, D)], vst[j % 4][:]).then_inc(stored, 16)
                    if last_head:
                        for i in VALUES_IN[t]:
                            load_value_page(sp, inp, vc0, i, pages0[i], v_in0)
                        for i in KEYS_IN[t]:
                            load_key_page(sp, kt_d, kT0, i, pages0[i], kq_in0)
                    sp.wait_ge(stored, (n + 1) * 48)
                    sp.sem_inc(stage_free, 1)
                    if last_head and t == 1:
                        load_new_keys(sp, q_d, k_d, 0, q0, kT0, kq_in0)
                    if cache_step(t, last_head):
                        sp.wait_ge(k_stored, (k + 1) * 16)
                        sp.sem_inc(kst_free, 1)

                VALUES_IN = [range(0, 2), range(2, 4), (4,), (5,), (6,), (7,), (8,), (9,)]
                KEYS_IN = [(), (), range(0, 4), range(4, 8), range(8, 12), range(12, 16), (), ()]
                pages0 = pages_of(nc, table, 0, 0, NPP, mybir.EngineType.SP)
                loop(sp, body)

            @block.tensor
            def _(pe):
                def weight_job(g, slot, bank):
                    for i in range(4):
                        k, o = (g, i) if g < KC else ((g - KC) * 2 + i // 2, REP + i % 2)
                        t = pe.transpose(bank[:, i * P:(i + 1) * P], wn[slot][:, o, k * P:(k + 1) * P], ident[:])
                    t.then_inc(job_t, 1)

                def cache_job(slot):
                    for h in range(HK):
                        o = pw[:, h // 4, (h % 4) * P:(h % 4 + 1) * P]
                        t = pe.transpose(o, kn[slot][:, h * D:(h + 1) * D], ident[:])
                    t.then_inc(job_t, 1)

                def multiply(j):
                    t, slot = j % TT, j // TT % 2
                    tok = slice(t * P, (t + 1) * P)
                    for out, cols in ((ps[j % 2][:, 0:QW], slice(0, QW)), (ps[j % 2][:, QW:WE], slice(QW, WE))):
                        for k in range(KC):
                            last = three_pass(pe, out, xT_hi[:, k, tok], xT_lo[:, k, tok], wt_hi[slot][:, k, cols],
                                              wt_lo[slot][:, k, cols], k == 0, k == KC - 1)
                    last.then_inc(mm_done, 1)

                pe.wait_ge(w_in[0], 48)
                for g in range(WJ):
                    weight_job(g, 0, first_banks[g])
                pe.wait_ge(job_dve, WJ)
                multiply(0)
                multiply(1)

                def body(it, j, tail):
                    n, c, t, slot = it * UNROLL + j, it * 2 + j // TT, j % TT, j // TT
                    last_head = tail and slot == 1
                    if cache_step(t, last_head) or not last_head:
                        pe.wait_ge(job_dve, job_of(c, t))
                        pe.wait_ge(job_act, job_of(c, t))
                        if t == 0 and not last_head:
                            pe.wait_ge(w_in[1 - slot], (it + 1 + slot) * 48)
                        if not cache_step(t, last_head):
                            weight_job(t, 1 - slot, pw[:, t % 2])
                        else:
                            pe.wait_ge(kn_in[t % 2], (c + 1) * 16)
                            cache_job(t % 2)
                    if not (tail and j >= UNROLL - 2):
                        pe.wait_ge(roped, n + 1)
                        pe.wait_ge(v_staged, n + 1)
                        multiply(j + 2)
                    pe.wait_ge(normed, n + 1)
                    pe.wait_ge(q_staged, n + 2)
                    for h in range(REP + 1):
                        o = pt[:, h * P:(h + 1) * P]
                        last = pe.transpose(o, qn[j % 2][:, h * P:(h + 1) * P], ident[:])
                    last.then_inc(turned, 1)

                loop(pe, body)

            def split_of(g, slot, bank):
                if g < KC:
                    return wt_hi[slot][:, g, 0:QW], wt_lo[slot][:, g, 0:QW], bank
                k = slice((g - KC) * 2, (g - KC) * 2 + 2)
                return wt_hi[slot][:, k, QW:WE], wt_lo[slot][:, k, QW:WE], bank.rearrange("p (k c) -> p k c", k=2)

            def keys_of(half, slot):
                return (kst[slot][:, :, half * 4:half * 4 + 4, :].rearrange("p g h t -> p h g t"),
                        pw[:, half, :].rearrange("p (h g t) -> p h g t", h=4, g=PPT))

            @block.scalar
            def _(act):
                act.sem_inc(q_staged, 2)
                for g in range(WJ):
                    hi, _, bank = split_of(g, 0, first_banks[g])
                    act.wait_ge(job_t, g + 1)
                    act.activation(hi, bank, ACT.Copy).then_inc(job_act, 1)

                def squares(j, n):
                    act.wait_ge(mm_done, n + 1)
                    if not isinstance(n, int) or n >= 2:
                        act.wait_ge(reduced, n - 1)
                    act.activation(sq[j % 2][:, 0:QW], ps[j % 2][:, 0:QW], ACT.Square).then_inc(q_squared, 1)
                    act.wait_ge(k_roped, n + 1)
                    act.activation(sq[j % 2][:, QW:QK], ps[j % 2][:, QW:QK], ACT.Square).then_inc(squared, 1)
                    if not isinstance(n, int) or n >= 4:
                        act.wait_ge(stage_free, n - 1)
                    act.activation(vst[j % 4][:], ps[j % 2][:, QK:WE], ACT.Copy).then_inc(v_staged, 1)

                squares(0, 0)
                squares(1, 1)

                def body(it, j, tail):
                    n, c, t, slot = it * UNROLL + j, it * 2 + j // TT, j % TT, j // TT
                    last_head = tail and slot == 1
                    if cache_step(t, last_head) or not last_head:
                        act.wait_ge(job_t, job_of(c, t) + 1)
                        if not cache_step(t, last_head):
                            hi, _, bank = split_of(t, 1 - slot, pw[:, t % 2])
                            act.activation(hi, bank, ACT.Copy).then_inc(job_act, 1)
                        else:
                            act.wait_ge(kst_free, c * 2 + t % 2 + 1)
                            dst, bank = keys_of(0, t % 2)
                            act.activation(dst, bank, ACT.Copy).then_inc(job_act, 1)
                    if not (tail and j >= UNROLL - 2):
                        squares(j + 2, n + 2)
                    act.wait_ge(turned, n + 1)
                    act.wait_ge(stage_free, n + 1)
                    q_src = pt[:, 0:QW].rearrange("p (h b t) -> p b h t", h=REP, b=BT)
                    k_src = pt[:, QW:QK].rearrange("p (b t) -> p b t", b=BT)
                    act.activation(qst[j % 2][:, :, 0:QS].rearrange("p b (h t) -> p b h t", h=REP), q_src, ACT.Copy)
                    act.activation(qst[j % 2][:, :, QS:ST], k_src, ACT.Copy).then_inc(q_staged, 1)

                loop(act, body)

            @block.vector
            def _(dve):
                v = nc.vector
                for g in range(WJ):
                    hi, lo, bank = split_of(g, 0, first_banks[g])
                    dve.wait_ge(job_act, g + 1)
                    v.tensor_tensor(lo, bank, f32(hi), ALU.subtract).then_inc(job_dve, 1)

                def rope(j, n):
                    t, s = j % TT, j % 2
                    dve.wait_ge(mm_done, n + 1)
                    if not isinstance(n, int) or n >= 2:
                        dve.wait_ge(normed, n - 1)
                    q = ps[s][:, 0:QW].rearrange("p (h d) -> p h d", h=REP)
                    a = ta[s][:, 0:QW].rearrange("p (h d) -> p h d", h=REP)
                    b = tb[s][:, 0:QW].rearrange("p (h d) -> p h d", h=REP)
                    lo, hi = slice(0, HALF), slice(HALF, D)
                    k = ps[s][:, QW:QK]
                    v.tensor_tensor(ta[s][:, QW:QK], k, ck[:, t, :], ALU.mult)
                    v.tensor_tensor(tb[s][:, QW:QW + HALF], k[:, hi], sn_k[:, t, lo], ALU.mult)
                    v.tensor_tensor(tb[s][:, QW + HALF:QK], k[:, lo], sn_k[:, t, hi], ALU.mult).then_inc(k_roped, 1)
                    dve.wait_ge(q_squared, n + 1)
                    v.tensor_tensor(a, q, cq[:, t:t + 1, :].broadcast_to([P, REP, D]), ALU.mult)
                    v.tensor_tensor(b[:, :, lo], q[:, :, hi], sn_q[:, t:t + 1, lo].broadcast_to([P, REP, HALF]), ALU.mult)
                    v.tensor_tensor(b[:, :, hi], q[:, :, lo], sn_q[:, t:t + 1, hi].broadcast_to([P, REP, HALF]), ALU.mult).then_inc(roped, 1)
                    dve.wait_ge(squared, n + 1)
                    v.tensor_reduce(ss[s][:], sq[s][:].rearrange("p (h d) -> p h d", h=REP + 1), AX_X, ALU.add).then_inc(reduced, 1)

                rope(0, 0)
                rope(1, 1)

                def body(it, j, tail):
                    n, c, t, slot = it * UNROLL + j, it * 2 + j // TT, j % TT, j // TT
                    last_head = tail and slot == 1
                    if cache_step(t, last_head) or not last_head:
                        if not cache_step(t, last_head):
                            hi, lo, bank = split_of(t, 1 - slot, pw[:, t % 2])
                            dve.wait_ge(job_act, job_of(c, t) + 1)
                            v.tensor_tensor(lo, bank, f32(hi), ALU.subtract).then_inc(job_dve, 1)
                        else:
                            dve.wait_ge(job_t, job_of(c, t) + 1)
                            dve.wait_ge(kst_free, c * 2 + t % 2 + 1)
                            dst, bank = keys_of(1, t % 2)
                            v.tensor_copy(dst, bank).then_inc(job_dve, 1)
                    if not (tail and j >= UNROLL - 2):
                        rope(j + 2, n + 2)

                loop(dve, body)

            @block.gpsimd
            def _(pool):
                g = nc.gpsimd
                g.memset(power[:], -0.5)
                g.memset(floor[:], D * EPS).then_inc(pool_step, 1)
                pool.wait_ge(pool_step, 1)

                def body(it, j, tail):
                    n, s = it * UNROLL + j, j % 2
                    pool.wait_ge(roped, n + 1)
                    g.tensor_tensor(ta[s][:], ta[s][:], tb[s][:], ALU.add).then_inc(pool_step, 1)
                    pool.wait_ge(reduced, n + 1)
                    pool.wait_ge(q_staged, n + 1)
                    g.tensor_tensor(rs[s][:], ss[s][:], floor[:], ALU.add).then_inc(pool_step, 1)
                    pool.wait_ge(pool_step, n * 3 + 3)
                    g.tensor_tensor(rstd[s][:], rs[s][:], power[:], ALU.pow).then_inc(pool_step, 1)
                    pool.wait_ge(pool_step, n * 3 + 4)
                    r = rstd[s][:].rearrange("p (h a) -> p h a", a=1).broadcast_to([P, REP + 1, D])
                    rows = lambda x: x[s][:].rearrange("p (h d) -> p h d", h=REP + 1)
                    g.tensor_tensor(rows(qn), rows(ta), r, ALU.mult).then_inc(normed, 1)

                loop(pool, body)


SL = 8


def load_wo(eng, inp, s, tile, sem):
    w = HQ * D // SL
    eng.dma_start(tile[:], inp["L3_cond_Wo"][:, s * w:(s + 1) * w].rearrange("(o p) e -> p o e", p=P)).then_inc(sem, 16)


def stage_attend(nc, inp, ident, table, len_i, wo, wo_in, q0, kT0, vc0, kq_in0, v_in0, q_d, k_d, v_d, kt_d, o_d):
    GROUP = 4
    UNROLL = 2 * HK
    AHEAD = 4
    SPLITS = 4
    EARLY = 7
    with ExitStack() as ctx:
        m = Bench(nc, ctx, "att")
        PA = (PG + 1) // 2
        KA, KB = PA * PS, (PG - PA) * PS
        PAD = 2 * KA
        kT = [kT0, m.sb("kT1", [P, PG, HK, PS])]
        k_hi = [m.sb(f"k_hi{i}", [P, PG, PS], F32R) for i in range(SPLITS)]
        k_lo = [m.sb(f"k_lo{i}", [P, PG, PS], F32R) for i in range(SPLITS)]
        q_hi = [m.sb(f"q_hi{i}", [P, QS], F32R) for i in range(SPLITS)]
        q_lo = [m.sb(f"q_lo{i}", [P, QS], F32R) for i in range(SPLITS)]
        vc = [vc0, m.sb("vc1", [P, NCH, HK * D])]
        q = [q0, m.sb("q1", [P, HK, QS])]
        vn = [m.sb(f"vn{i}", [S, HK * D]) for i in range(2)]
        lens = m.sb("lens", [P, B])
        key_no = m.sb("key_no", [P, PAD])
        mask = [m.sb(f"mask{i}", [P, PAD]) for i in range(2)]
        neg = [m.sb(f"neg{i}", [P, PAD]) for i in range(2)]
        nmax = [m.sb(f"nmax{i}", [P, 1]) for i in range(2)]
        prob = [m.sb(f"prob{i}", [P, KEYS]) for i in range(2)]
        total = [m.sb(f"total{i}", [P, 1]) for i in range(2)]
        inv = [m.sb(f"inv{i}", [P, 1]) for i in range(2)]
        pT = [m.sb(f"pT{i}", [P, NCH + 1, P]) for i in range(2)]
        ost = [m.sb(f"ost{i}", [P, HK, P]) for i in range(2)]
        ps = [m.psum(f"ps{i}", [P, 2, BANK]) for i in range(2)]
        pa = m.psum("pa", [P, BANK])
        pb = m.psum("pb", [P, BANK])
        po = [m.psum(f"po{i}", [P, BANK]) for i in range(2)]

        NA = 2
        lens_ready = m.sem("lens_ready")
        kq_in = [kq_in0, m.sem("kq_in1")]
        v_in = [v_in0, m.sem("v_in1")]
        k_hi_done = m.sem("k_hi_done")
        q_hi_done = m.sem("q_hi_done")
        k_split = m.sem("k_split")
        q_split = m.sem("q_split")
        v_pool_in = [m.sem(f"v_pool_in{i}") for i in range(2)]
        numbered = m.sem("numbered")
        padded = m.sem("padded")
        masked = m.sem("masked")
        may_reduce = m.sem("may_reduce")
        scored = m.sem("scored")
        maxed = m.sem("maxed")
        exped = m.sem("exped")
        inverted = m.sem("inverted")
        normed = m.sem("normed")
        turned_a = m.sem("turned_a")
        turned_b = m.sem("turned_b")
        out_a = m.sem("out_a")
        out_b = m.sem("out_b")
        valued = m.sem("valued")
        o_staged = m.sem("o_staged")
        o_stored = [m.sem(f"o_stored{i}") for i in range(2)]

        def load_keys(eng, b, slot, pages):
            load_new_keys(eng, q_d, k_d, b, q[slot], kT[slot], kq_in[slot])
            for j, page in enumerate(pages):
                load_key_page(eng, kt_d, kT[slot], j, page, kq_in[slot])

        def load_new_values(eng, b, slot):
            eng.dma_start(vn[slot][:], v_d[bass.ds(b, 1)].rearrange("a s c -> (a s) c")).then_inc(v_in[slot], 16)

        def load_values(eng, b, slot, pages):
            load_new_values(eng, b, slot)
            for j in range(NPP - POOL_PAGES):
                load_value_page(eng, inp, vc[slot], j, pages[j], v_in[slot])

        with nc.Block() as block:

            @block.sync
            def _(sp):
                for slot in range(2):
                    sp.sem_inc(o_stored[slot], 16)

                load_new_values(sp, 0, 0)
                pages = pages_of(nc, table, 1, 0, NPP, mybir.EngineType.SP)
                load_keys(sp, 1, 1, pages)
                load_values(sp, 1, 1, pages)
                for i in range(2):
                    load_wo(sp, inp, i, wo[i], wo_in[i])

                def body(it, tail):
                    for slot in range(2):
                        b = it * 2 + slot
                        if not tail:
                            pages = pages_of(nc, table, b + 2, 0, NPP, mybir.EngineType.SP)
                            sp.wait_ge(q_split, (b + 1) * HK)
                            sp.wait_ge(k_split, (b + 1) * HK)
                            load_keys(sp, b + 2, slot, pages)
                            sp.wait_ge(valued, (b + 1) * HK)
                            load_values(sp, b + 2, slot, pages)
                        sp.wait_ge(o_staged, (b + 1) * (HK // GROUP) + 2)
                        sp.dma_start(o_d[bass.ds(b, 1)].rearrange("a d x -> (a d) x"),
                                     ost[slot][:].rearrange("p h x -> p (h x)")).then_inc(o_stored[slot], 16)

                with sp.Fori(0, B // 2 - 1) as it:
                    body(it, False)
                body(B // 2 - 1, True)
                for slot in range(2):
                    sp.wait_ge(o_stored[slot], (B // 2 + 1) * 16)
                    sp.wait_ge(wo_in[slot], 16)

            @block.gpsimd
            def _(pool):
                g = nc.gpsimd
                g.iota(key_no[:, 0:L], pattern=[[1, L]], base=0, channel_multiplier=0,
                       allow_small_or_imprecise_dtypes=True).then_inc(numbered, 1)
                g.memset(key_no[:, L:KEYS], -1.0).then_inc(numbered, 1)
                g.memset(key_no[:, KEYS:PAD], MASKED).then_inc(numbered, 1)
                pages0 = pages_of(nc, table, 0, NPP - POOL_PAGES, POOL_PAGES, mybir.EngineType.Pool)

                def load_first(pages):
                    for i in pages:
                        load_value_page(pool, inp, vc[0], NPP - POOL_PAGES + i, pages0[i], v_pool_in[0])


                def split(j, n):
                    pool.wait_ge(k_hi_done, n + 1)
                    g.tensor_tensor(k_lo[j % SPLITS][:], kT[j // HK % 2][:, :, j % HK, :], f32(k_hi[j % SPLITS][:]),
                                    ALU.subtract).then_inc(k_split, 1)

                def body(it, j, first, tail):
                    split(j, it * UNROLL + j)
                    i = (j % HK + 1) % HK
                    b = j // HK + (i < 1)
                    if i < POOL_PAGES and not (first and b < 1) and not (tail and b >= 2):
                        page, = pages_of(nc, table, it * 2 + b, NPP - POOL_PAGES + i, 1, mybir.EngineType.Pool)
                        if not (first and b < 2):
                            pool.wait_ge(valued, (it * 2 + b - 1) * HK)
                        load_value_page(pool, inp, vc[b % 2], NPP - POOL_PAGES + i, page, v_pool_in[b % 2])

                for j in range(UNROLL):
                    body(0, j, True, False)
                    if j in (1, 2):
                        load_first(range((j - 1) * POOL_PAGES // 2, j * POOL_PAGES // 2))
                with pool.Fori(1, B // 2 - 1) as it:
                    for j in range(UNROLL):
                        body(it, j, False, False)
                for j in range(UNROLL):
                    body(B // 2 - 1, j, False, True)

            @block.tensor
            def _(pe):
                def scores(j, n):
                    i, x = j % 2, j % SPLITS
                    pe.wait_ge(q_split, n + 1)
                    pe.wait_ge(k_split, n + 1)
                    three_pass(pe, ps[i][:, 0, 0:KA], q_hi[x][:], q_lo[x][:], k_hi[x][:, 0:PA, :], k_lo[x][:, 0:PA, :], True, True)
                    three_pass(pe, ps[i][:, 1, 0:KB], q_hi[x][:], q_lo[x][:], k_hi[x][:, PA:PG, :], k_lo[x][:, PA:PG, :],
                               True, True).then_inc(scored, 1)

                def turn(j):
                    p = prob[j % 2]
                    for c in range(NA, NCH):
                        pe.transpose(pb[:, (c - NA) * P:(c - NA + 1) * P], p[:, c * P:(c + 1) * P], ident[:])
                    pe.transpose(pb[0:S, (NCH - NA) * P:(NCH - NA + 1) * P], p[:, L:KEYS], ident[:]).then_inc(turned_b, 1)
                    for c in range(NA):
                        t = pe.transpose(pa[:, c * P:(c + 1) * P], p[:, c * P:(c + 1) * P], ident[:])
                    t.then_inc(turned_a, 1)

                def values(j, n):
                    s, h = j // HK % 2, j % HK
                    cols = slice(h * D, (h + 1) * D)
                    o = po[j // GROUP % 2][:, j % GROUP * P:(j % GROUP + 1) * P]
                    pe.wait_ge(out_b, n + 1)
                    for c in range(NA, NCH):
                        pe.matmul(o, vc[s][:, c, cols], pT[j % 2][:, c, :], start=(c == NA), stop=False)
                    pe.matmul(o, vn[s][:, cols], pT[j % 2][0:S, NCH, :], start=False, stop=False)
                    pe.wait_ge(out_a, n + 1)
                    for c in range(NA):
                        t = pe.matmul(o, vc[s][:, c, cols], pT[j % 2][:, c, :], start=False, stop=(c == NA - 1))
                    t.then_inc(valued, 1)

                pe.wait_ge(padded, 2)
                scores(0, 0)
                scores(1, 1)
                for i in range(2):
                    pe.wait_ge(maxed, i + 1)
                    scores(i + 2, i + 2)
                    pe.wait_ge(normed, i + 1)
                    if i:
                        pe.wait_ge(out_a, i)
                        pe.wait_ge(out_b, i)
                    turn(i)

                def body(it, j, tail):
                    n = it * UNROLL + j
                    b = it * 2 + j // HK
                    if j % GROUP == 0:
                        pe.wait_ge(o_staged, it * (UNROLL // GROUP) + j // GROUP + 1)
                    if j % HK == 0:
                        pe.wait_ge(v_in[j // HK], (it + 1) * (PG - POOL_PAGES) * 16)
                        pe.wait_ge(v_pool_in[j // HK], (it + 1) * POOL_PAGES * 16)
                    values(j, n)
                    if not (tail and j + AHEAD >= UNROLL):
                        pe.wait_ge(maxed, n + 3)
                        scores(j + AHEAD, n + AHEAD)
                    if not (tail and j + 2 >= UNROLL):
                        pe.wait_ge(normed, n + 3)
                        pe.wait_ge(out_a, n + 2)
                        pe.wait_ge(out_b, n + 2)
                        turn(j + 2)

                with pe.Fori(0, B // 2 - 1) as it:
                    for j in range(UNROLL):
                        body(it, j, False)
                for j in range(UNROLL):
                    body(B // 2 - 1, j, True)

            @block.vector
            def _(dve):
                v = nc.vector
                for i in range(2):
                    v.memset(ps[i][:, 1, KB:KA], 0.0).then_inc(padded, 1)
                v.tensor_copy(lens[:], len_i[:]).then_inc(lens_ready, 1)

                def smallest(j):
                    halves = [a.rearrange("p (a k) -> p a k", a=2) for a in (neg[j % 2][:], mask[j // HK % 2][:])]
                    v.tensor_tensor_reduce(halves[0], halves[1], ps[j % 2][:, :, 0:KA], 1.0, 3.0e38,
                                           ALU.add, ALU.min, nmax[j % 2][:]).then_inc(maxed, 1)

                def make_mask(b, slot):
                    v.tensor_scalar(mask[slot][:], key_no[:], lens[:, bass.ds(b, 1)], MASKED, ALU.is_ge, ALU.mult).then_inc(masked, 1)

                def split_q(j, n, it):
                    if not isinstance(n, int) or n >= SPLITS:
                        dve.wait_ge(scored, n - SPLITS + 1)
                    if j % HK == 0:
                        dve.wait_ge(kq_in[j // HK % 2], (it + j // UNROLL + 1) * 16 * (PG + 1))
                    src = q[j // HK % 2][:, j % HK, :]
                    v.tensor_copy(q_hi[j % SPLITS][:], src).then_inc(q_hi_done, 1)
                    dve.wait_ge(q_hi_done, n + 1)
                    v.tensor_tensor(q_lo[j % SPLITS][:], src, f32(q_hi[j % SPLITS][:]), ALU.subtract).then_inc(q_split, 1)

                def minimum(j, n, b):
                    dve.wait_ge(scored, n + 1)
                    if j % HK == 0:
                        dve.wait_ge(masked, b + 1)
                    dve.sem_inc(may_reduce, 1)
                    smallest(j)

                def normalize(j, n):
                    dve.wait_ge(exped, n + 1)
                    v.reciprocal(inv[j % 2][:], total[j % 2][:]).then_inc(inverted, 1)
                    dve.wait_ge(inverted, n + 1)
                    v.tensor_scalar(prob[j % 2][:], prob[j % 2][:], inv[j % 2][:, 0:1], None, ALU.mult).then_inc(normed, 1)

                def keep(j, n):
                    dve.wait_ge(turned_a, n + 1)
                    v.tensor_copy(pT[j % 2][:, 0:NA, :], pa[:, 0:NA * P].rearrange("p (c q) -> p c q", c=NA)).then_inc(out_a, 1)

                split_q(0, 0, 0)
                split_q(1, 1, 0)
                dve.wait_ge(padded, 2)
                dve.wait_ge(numbered, 3)
                dve.wait_ge(lens_ready, 1)
                make_mask(0, 0)
                minimum(0, 0, 0)
                split_q(2, 2, 0)
                split_q(3, 3, 0)
                minimum(1, 1, 0)
                make_mask(1, 1)
                normalize(0, 0)
                keep(0, 0)
                minimum(2, 2, 0)
                normalize(1, 1)
                for i in range(SPLITS, EARLY):
                    split_q(i, i, 0)

                def body(it, j, tail):
                    n = it * UNROLL + j
                    if not (tail and j + 3 >= UNROLL):
                        minimum(j + 3, n + 3, it * 2 + (j + 3) // HK)
                    if not (tail and j + 1 >= UNROLL):
                        keep(j + 1, n + 1)
                    if not (tail and j + 2 >= UNROLL):
                        normalize(j + 2, n + 2)
                    if not (tail and j + EARLY >= UNROLL):
                        split_q(j + EARLY, n + EARLY, it)
                    if not tail and j % HK == HK - 4:
                        dve.wait_ge(maxed, n + 4)
                        make_mask(it * 2 + 2 + j // HK, j // HK)

                with dve.Fori(0, B // 2 - 1) as it:
                    for j in range(UNROLL):
                        body(it, j, False)
                for j in range(UNROLL):
                    body(B // 2 - 1, j, True)

            @block.scalar
            def _(act):
                act.sem_inc(o_staged, 2)

                def exps(j, n):
                    if not isinstance(n, int) or n >= 2:
                        act.wait_ge(turned_a, n - 1)
                    act.wait_ge(maxed, n + 1)
                    act.activation(prob[j % 2][:], neg[j % 2][:, 0:KEYS], ACT.Exp, bias=nmax[j % 2][:, 0:1], scale=-1.0,
                                   accum_out=total[j % 2][:]).then_inc(exped, 1)

                def keep(j, n):
                    act.wait_ge(turned_b, n + 1)
                    act.activation(pT[j % 2][:, NA:NCH, :], pb[:, 0:(NCH - NA) * P].rearrange("p (c q) -> p c q", q=P), ACT.Copy)
                    act.activation(pT[j % 2][0:S, NCH, :], pb[0:S, (NCH - NA) * P:(NCH - NA + 1) * P], ACT.Copy).then_inc(out_b, 1)

                def split_k(j, n, it):
                    if not isinstance(n, int) or n >= SPLITS:
                        act.wait_ge(scored, n - SPLITS + 1)
                    if j % HK == 0:
                        act.wait_ge(kq_in[j // HK % 2], (it + j // UNROLL + 1) * 16 * (PG + 1))
                    act.activation(k_hi[j % SPLITS][:], kT[j // HK % 2][:, :, j % HK, :], ACT.Copy).then_inc(k_hi_done, 1)

                split_k(0, 0, 0)
                split_k(1, 1, 0)
                exps(0, 0)
                split_k(2, 2, 0)
                split_k(3, 3, 0)
                exps(1, 1)
                keep(0, 0)
                exps(2, 2)
                for i in range(SPLITS, EARLY):
                    split_k(i, i, 0)

                def body(it, j, tail):
                    n = it * UNROLL + j
                    if not (tail and j + 1 >= UNROLL):
                        keep(j + 1, n + 1)
                    if not (tail and j + 3 >= UNROLL):
                        exps(j + 3, n + 3)
                    if not (tail and j + EARLY >= UNROLL):
                        split_k(j + EARLY, n + EARLY, it)
                    if j % GROUP == GROUP - 1:
                        g = j // GROUP
                        act.wait_ge(valued, n + 1)
                        if g % 2 == 0:
                            act.wait_ge(o_stored[j // HK], (it + 1) * 16)
                        act.activation(ost[j // HK][:, g % 2 * GROUP:(g % 2 + 1) * GROUP, :],
                                       po[g % 2][:].rearrange("p (h q) -> p h q", h=GROUP), ACT.Copy).then_inc(o_staged, 1)

                with act.Fori(0, B // 2 - 1) as it:
                    for j in range(UNROLL):
                        body(it, j, False)
                for j in range(UNROLL):
                    body(B // 2 - 1, j, True)


def stage_output(nc, inp, ident, wn, w_in, room, o_d, x3_d, out_d):
    CH = HQ * D // P
    Q = 4
    CQ = CH // Q
    UNROLL = 2 * Q
    CS = CH // SL
    with ExitStack() as ctx:
        m = Bench(nc, ctx, "out")
        wt_hi = m.sb("wt_hi", [P, CH, H], F32R)
        wt_lo = m.sb("wt_lo", [P, CH, H], F32R)
        o_n = [m.sb(f"o_n{i}", [P, BT, CQ * S]) for i in range(2)]
        o_hi = [m.sb(f"o_hi{i}", [P, CQ, P], F32R) for i in range(2)]
        o_lo = [m.sb(f"o_lo{i}", [P, CQ, P], F32R) for i in range(2)]
        x3, y = ([room[:, (2 * a + i) * H:(2 * a + i + 1) * H] for i in range(2)] for a in range(2))
        pw = [m.psum(f"pw{i}", [P, BANK]) for i in range(4)]
        py = [m.psum(f"py{i}", [P, BANK]) for i in range(2)]

        w_turned = m.sem("w_turned")
        w_hi = m.sem("w_hi")
        w_lo = m.sem("w_lo")
        o_in = [m.sem(f"o_in{i}") for i in range(2)]
        x3_in = [m.sem(f"x3_in{i}") for i in range(2)]
        o_hi_done = m.sem("o_hi_done")
        o_lo_done = m.sem("o_lo_done")
        unit_done = m.sem("unit_done")
        summed = m.sem("summed")
        stored = [m.sem(f"stored{i}") for i in range(2)]

        with nc.Block() as block:

            @block.sync
            def _(sp):
                def load_o(it, i):
                    t, q, s = it * 2 + i // Q, i % Q, i % 2
                    src = o_d[bass.ds(t * BT, BT), :, q * CQ * S:(q + 1) * CQ * S].rearrange("b d x -> d b x")
                    sp.dma_start(o_n[s][:], src).then_inc(o_in[s], 16)
                    if q == 0:
                        x = x3_d[bass.ds(t, 1)].rearrange("a p h -> (a p) h")
                        sp.dma_start(x3[i // Q % 2], x).then_inc(x3_in[i // Q % 2], 16)

                load_o(0, 0)
                for s in range(2, SL):
                    sp.wait_ge(w_turned, (s - 1) * CS)
                    load_wo(sp, inp, s, wn[s % 2], w_in[s % 2])
                    if s == 3:
                        load_o(0, 1)

                def store(t, s):
                    sp.wait_ge(summed, t + 1)
                    sp.dma_start(out_d[bass.ds(t, 1)].rearrange("a p h -> (a p) h"), y[s]).then_inc(stored[s], 16)

                def body(it, i, first, tail):
                    u = it * UNROLL + i
                    if not (tail and i + 2 >= UNROLL):
                        sp.wait_ge(o_lo_done, u + 1)
                        if (i + 2) % Q == 0 and not (first and i + 2 == Q):
                            sp.wait_ge(summed, it * 2 + (i + 2) // Q - 1)
                        load_o(it, i + 2)
                    if i % Q == 1 and not (first and i == 1):
                        store(it * 2 + i // Q - 1, (i // Q + 1) % 2)

                for i in range(UNROLL):
                    body(0, i, True, False)
                with sp.Fori(1, TT // 2 - 1) as it:
                    for i in range(UNROLL):
                        body(it, i, False, False)
                for i in range(UNROLL):
                    body(TT // 2 - 1, i, False, True)
                store(TT - 1, (TT - 1) % 2)
                for s in range(2):
                    sp.wait_ge(stored[s], 16 * (TT // 2))

            @block.tensor
            def _(pe):
                def turn(q):
                    for c in range(q * CQ, (q + 1) * CQ):
                        s = c // CS
                        if c % CS == 0:
                            pe.wait_ge(w_in[s % 2], 16 * (s // 2 + 1))
                        if c >= 4:
                            pe.wait_ge(w_lo, c - 3)
                        for o in range(KC):
                            t = pe.transpose(pw[c % 4][:, o * P:(o + 1) * P], wn[s % 2][:, o, c % CS * P:(c % CS + 1) * P],
                                             ident[:])
                        t.then_inc(w_turned, 1)

                def body(it, i, tail):
                    u, q = it * UNROLL + i, i % Q
                    pe.wait_ge(o_lo_done, u + 1)
                    if isinstance(it, int) and i < Q:
                        pe.wait_ge(w_lo, (q + 1) * CQ)
                    if q == 0 and not (isinstance(it, int) and it == 0):
                        pe.wait_ge(summed, it * 2 + i // Q - 1)
                    for c in range(CQ):
                        w = q * CQ + c
                        last = three_pass(pe, py[i // Q][:], o_hi[i % 2][:, c, :], o_lo[i % 2][:, c, :], wt_hi[:, w, :],
                                          wt_lo[:, w, :], w == 0, w == CH - 1)
                    last.then_inc(unit_done, 1)

                turn(0)
                for i in range(UNROLL):
                    if i + 1 < Q:
                        turn(i + 1)
                    body(0, i, False)
                with pe.Fori(1, TT // 2) as it:
                    for i in range(UNROLL):
                        body(it, i, False)

            @block.scalar
            def _(act):
                def split_w(q):
                    for c in range(q * CQ, (q + 1) * CQ):
                        act.wait_ge(w_turned, c + 1)
                        act.activation(wt_hi[:, c, :], pw[c % 4][:], ACT.Copy).then_inc(w_hi, 1)

                def body(it, i):
                    u = it * UNROLL + i
                    act.wait_ge(o_in[i % 2], (it * (UNROLL // 2) + i // 2 + 1) * 16)
                    if not isinstance(u, int) or u >= 2:
                        act.wait_ge(unit_done, u - 1)
                    src = o_n[i % 2][:].rearrange("p b (c t) -> p c b t", c=CQ)
                    dst = o_hi[i % 2][:].rearrange("p c (b t) -> p c b t", b=BT)
                    act.activation(dst, src, ACT.Copy).then_inc(o_hi_done, 1)

                for i in range(UNROLL):
                    if i < Q:
                        split_w(i)
                    body(0, i)
                with act.Fori(1, TT // 2) as it:
                    for i in range(UNROLL):
                        body(it, i)

            @block.vector
            def _(dve):
                v = nc.vector
                def split_w(q):
                    for c in range(q * CQ, (q + 1) * CQ):
                        dve.wait_ge(w_hi, c + 1)
                        v.tensor_tensor(wt_lo[:, c, :], pw[c % 4][:], f32(wt_hi[:, c, :]), ALU.subtract).then_inc(w_lo, 1)

                def add(t, s, round_of, first):
                    dve.wait_ge(unit_done, t * Q + Q)
                    dve.wait_ge(x3_in[s], (round_of + 1) * 16)
                    if not first:
                        dve.wait_ge(stored[s], round_of * 16)
                    v.tensor_tensor(y[s], x3[s], py[s][:], ALU.add).then_inc(summed, 1)

                def body(it, i, peeled):
                    u = it * UNROLL + i
                    dve.wait_ge(o_hi_done, u + 1)
                    src = o_n[i % 2][:].rearrange("p b (c t) -> p c b t", c=CQ)
                    dst = o_lo[i % 2][:].rearrange("p c (b t) -> p c b t", b=BT)
                    hi = f32(o_hi[i % 2][:]).rearrange("p c (b t) -> p c b t", b=BT)
                    v.tensor_tensor(dst, src, hi, ALU.subtract).then_inc(o_lo_done, 1)
                    if i == 1 and not peeled:
                        add(it * 2 - 1, 1, it - 1, isinstance(it, int))
                    if i == Q + 1:
                        add(it * 2, 0, it, peeled)

                for i in range(UNROLL):
                    if i < Q:
                        split_w(i)
                    body(0, i, True)
                for i in range(UNROLL):
                    body(1, i, False)
                with dve.Fori(2, TT // 2) as it:
                    for i in range(UNROLL):
                        body(it, i, False)
                add(TT - 1, 1, TT // 2 - 1, False)


def program(nc, inp, out):
    x3_d = nc.dram_tensor("x3_scratch", [TT, P, H], F32).ap()
    q_d = nc.dram_tensor("q_scratch", [B, HK, D, QS], F32).ap()
    k_d = nc.dram_tensor("k_scratch", [B, D, HK * S], F32).ap()
    v_d = nc.dram_tensor("v_scratch", [TT, P, HK * D], F32).ap()
    kt_d = nc.dram_tensor("kt_scratch", [PAGES, D, HK * PS], F32).ap()
    o_d = nc.dram_tensor("o_scratch", [B, D, HK * P], F32).ap()
    with ExitStack() as ctx:
        m = Bench(nc, ctx, "all")
        ident = m.sb("ident", [P, P])
        room_a = m.sb("room_a", [P, PG * HK * PS])
        room_b = m.sb("room_b", [P, NCH * HK * D])
        x = room_a[:, 0:TT * H].rearrange("p (t h) -> p t h", t=TT)
        w2n = room_b[:].rearrange("p (e k h) -> p e k h", e=2, k=KC)
        kT0 = room_a[:].rearrange("p (j h t) -> p j h t", j=PG, h=HK)
        vc0 = room_b[:].rearrange("p (c x) -> p c x", c=NCH)
        q0 = m.sb("q0", [P, HK, QS])
        kq_in0, v_in0 = m.sem("kq_in0"), m.sem("v_in0")
        table = m.sb("table", [1, B * NPP], I32)
        len_i = m.sb("len_i", [P, B], I32)
        with ExitStack() as early:
            e = Bench(nc, early, "early")
            flat_hi = e.sb("xT_hi", [P, KC * TOK + BT * S], F32R)
            xT_hi = flat_hi[:, 0:KC * TOK].rearrange("p (k t) -> p k t", k=KC)
            xT_lo = e.sb("xT_lo", [P, KC, TOK], F32R)
            tabs = e.sb("tabs", [P, 4, TT, D])
            w_in = e.sem("w_in")
            stage_layers(nc, inp, ident, xT_hi, xT_lo, flat_hi, tabs, len_i, x, w2n, w_in, x3_d)
            stage_project(nc, inp, ident, xT_hi, xT_lo, tabs, w2n, w_in, table, q0, kT0, vc0, kq_in0, v_in0, q_d, k_d, v_d, kt_d)
        wo = [m.sb(f"wo{i}", [P, KC, HQ * D // SL]) for i in range(2)]
        wo_in = [m.sem(f"wo_in{i}") for i in range(2)]
        v_rows = v_d.rearrange("t (b s) c -> (t b) s c", s=S)
        stage_attend(nc, inp, ident, table, len_i, wo, wo_in, q0, kT0, vc0, kq_in0, v_in0, q_d, k_d, v_rows, kt_d, o_d)
        stage_output(nc, inp, ident, wo, wo_in, room_a, o_d, x3_d, out.rearrange("(t b) s h -> t (b s) h", b=BT))


INPUTS = ["x", "itok_B_0_15", "itok_B_0_2", "itok_B_3_7", "itok_Bx16_0_63", "itok_B_207_1644", "L0_cond_weights",
          "L1_cond_W", "L1_cond_lora_A", "L1_cond_lora_B_w", "L2_cond_weight", "L3_cond_Wq", "L3_cond_Wk", "L3_cond_Wv",
          "L3_cond_Wo", "L3_cond_q_norm_w", "L3_cond_k_norm_w", "L3_cond_k_cache", "L3_cond_v_cache"]


def inverse_frequencies():
    return (np.float32(1.0) / np.power(np.float32(THETA), np.arange(0, D, 2, dtype=np.float32) / np.float32(D))).astype(np.float32)


def kernel(**inputs):
    import concourse.bacc as bacc
    from concourse.bass_utils import run_bass_kernel_spmd as run

    nc = bacc.Bacc("TRN2", target_bir_lowering=False, num_devices=1)
    arrays, args = {}, {}
    for name in INPUTS + ["rope_inv_freq"]:
        a = inverse_frequencies() if name == "rope_inv_freq" else np.ascontiguousarray(inputs[name])
        arrays[f"in_{name}"] = a
        args[name] = nc.dram_tensor(f"in_{name}", a.shape, mybir.dt.from_np(a.dtype), kind="ExternalInput").ap()
    out = nc.dram_tensor("out", [B, S, H], F32, kind="ExternalOutput").ap()
    program(nc, args, out)
    return run(nc, [arrays], core_ids=[0]).results[0]["out"]
```
